# Optimizing a Trainium2 kernel written in Bass

```python
import numpy as np
import jax
import jax.numpy as jnp

def _softmax(x, axis=-1):
    return jax.nn.softmax(x, axis=axis)

def _gelu(x):
    return jax.nn.gelu(x, approximate=True)

def _silu(x):
    return jax.nn.silu(x)

def _sigmoid(x):
    return jax.nn.sigmoid(x)

def _layernorm(x, axis=-1, eps=1e-05):
    m = jnp.mean(x, axis=axis, keepdims=True)
    v = jnp.var(x, axis=axis, keepdims=True)
    return (x - m) / jnp.sqrt(v + eps)

def _scatter_add(tgt, idx, src, axis=0):
    return tgt.at[idx].add(src)

def _segment_sum(src, seg, n):
    return jax.ops.segment_sum(src, seg, n)
kernel_name = 'mk_hybrid_d2_jaxref_r8_2b69cc'

def setup_inputs(seed: int=0):
    np.random.seed(seed)
    _w = jnp.asarray

    def _L0_attn_a_setup():
        import jax, jax.numpy as jnp
        import numpy as np
        B, T, D_MODEL = (4, 256, 256)
        NUM_HEADS, HEAD_SIZE = (16, 128)
        MODEL_SIZE = 256
        key = jax.random.key(seed)
        ks = jax.random.split(key, 9)
        s = 0.02 / np.sqrt(D_MODEL)
        so = 0.02 / np.sqrt(NUM_HEADS * HEAD_SIZE)
        return {'query': jax.random.normal(ks[0], (B, T, D_MODEL), jnp.float32), 'w_q': jax.random.normal(ks[1], (D_MODEL, NUM_HEADS * HEAD_SIZE), jnp.float32) * s, 'b_q': jnp.zeros((NUM_HEADS * HEAD_SIZE,), jnp.float32), 'w_k': jax.random.normal(ks[2], (D_MODEL, NUM_HEADS * HEAD_SIZE), jnp.float32) * s, 'b_k': jnp.zeros((NUM_HEADS * HEAD_SIZE,), jnp.float32), 'w_v': jax.random.normal(ks[3], (D_MODEL, NUM_HEADS * HEAD_SIZE), jnp.float32) * s, 'b_v': jnp.zeros((NUM_HEADS * HEAD_SIZE,), jnp.float32), 'w_o': jax.random.normal(ks[4], (NUM_HEADS * HEAD_SIZE, MODEL_SIZE), jnp.float32) * so, 'b_o': jnp.zeros((MODEL_SIZE,), jnp.float32)}
    _L0_attn_a_in = _L0_attn_a_setup()

    def _L0_attn_b_setup():
        import jax, jax.numpy as jnp
        import numpy as np
        EMBED_DIM = 256
        NUM_HEADS = 16
        NUM_KV_HEADS = 8
        N_REP = NUM_HEADS // NUM_KV_HEADS
        HEAD_DIM = EMBED_DIM // NUM_HEADS // 2
        DEPTH = 0
        LAMBDA_INIT = 0.8 - 0.6 * float(np.exp(-0.3 * DEPTH))
        EPS = 1e-06
        key = jax.random.key(seed)
        ks = jax.random.split(key, 12)
        B, T, E = (1, 256, EMBED_DIM)
        kv_out = E // N_REP
        s = 0.02
        return {'x': jax.random.normal(ks[0], (B, T, E), jnp.float32), 'Wq': jax.random.normal(ks[1], (E, E), jnp.float32) * s, 'bq': jnp.zeros((E,), jnp.float32), 'Wk': jax.random.normal(ks[2], (E, kv_out), jnp.float32) * s, 'bk': jnp.zeros((kv_out,), jnp.float32), 'Wv': jax.random.normal(ks[3], (E, kv_out), jnp.float32) * s, 'bv': jnp.zeros((kv_out,), jnp.float32), 'Wo': jax.random.normal(ks[4], (E, E), jnp.float32) * s, 'bo': jnp.zeros((E,), jnp.float32), 'lq1': jax.random.normal(ks[5], (HEAD_DIM,), jnp.float32) * 0.1, 'lk1': jax.random.normal(ks[6], (HEAD_DIM,), jnp.float32) * 0.1, 'lq2': jax.random.normal(ks[7], (HEAD_DIM,), jnp.float32) * 0.1, 'lk2': jax.random.normal(ks[8], (HEAD_DIM,), jnp.float32) * 0.1, 'g_subln': jnp.ones((2 * HEAD_DIM,), jnp.float32)}
    _L0_attn_b_in = _L0_attn_b_setup()

    def _L0_ffn_setup():
        import jax, jax.numpy as jnp
        import numpy as np
        LN_EPS = 1e-05
        Q_EPS = 1e-05

        def ternary_quantize(w):
            scale = jnp.mean(jnp.abs(w))
            return jnp.clip(jnp.round(w / (scale + Q_EPS)), -1.0, 1.0)

        def layernorm(x, gamma, beta):
            mu = jnp.mean(x, axis=-1, keepdims=True)
            var = jnp.mean(jnp.square(x - mu), axis=-1, keepdims=True)
            return (x - mu) * jax.lax.rsqrt(var + LN_EPS) * gamma + beta
        key = jax.random.key(seed)
        k_x, k_w = jax.random.split(key)
        B, S, D_IN, D_OUT = (4, 256, 256, 256)
        x = jax.random.normal(k_x, (B, S, D_IN), dtype=jnp.float32)
        std = np.sqrt(2.0 / D_OUT).astype(np.float32)
        weight = jax.random.normal(k_w, (D_OUT, D_IN), dtype=jnp.float32) * std
        bias = jnp.zeros((D_OUT,), dtype=jnp.float32)
        ln_gamma = jnp.ones((D_IN,), dtype=jnp.float32)
        ln_beta = jnp.zeros((D_IN,), dtype=jnp.float32)
        return {'x': x, 'weight': weight, 'bias': bias, 'ln_gamma': ln_gamma, 'ln_beta': ln_beta}
    _L0_ffn_in = _L0_ffn_setup()

    def _L1_attn_a_setup():
        import jax, jax.numpy as jnp
        import numpy as np
        H, NS = (16, 8)
        key = jax.random.key(seed)
        ks = jax.random.split(key, 8)
        B, S, Dm = (1, 256, 256)
        hd = Dm // H
        return {'hidden_states': jax.random.normal(ks[0], (B, S, Dm), jnp.float32), 'Wq': jax.random.normal(ks[1], (Dm, Dm), jnp.float32) * 0.02, 'Wk': jax.random.normal(ks[2], (Dm, Dm), jnp.float32) * 0.02, 'Wv': jax.random.normal(ks[3], (Dm, Dm), jnp.float32) * 0.02, 'Wo': jax.random.normal(ks[4], (Dm, Dm), jnp.float32) * 0.02, 'splat_positions': jax.random.normal(ks[5], (H, NS, hd), jnp.float32) * 0.02, 'splat_directions': jax.random.normal(ks[6], (H, NS, hd), jnp.float32) * 0.02, 'splat_log_scales': jnp.full((H, NS), np.float32(np.log(0.8)), jnp.float32), 'splat_log_amplitudes': jnp.full((H, NS), np.float32(-np.log(NS)), jnp.float32), 'directional_strength': jnp.float32(0.4), 'position_sensitivity': jnp.float32(0.3), 'gsa_strength': jnp.float32(-4.0)}
    _L1_attn_a_in = _L1_attn_a_setup()

    def _L1_attn_b_setup():
        import math
        import jax, jax.numpy as jnp
        import numpy as np
        D_MODEL = 256
        NUM_HEADS = 16
        D_HEAD = D_MODEL // NUM_HEADS
        THETA = 10000.0

        def _rope_tables(seq_len, d_head):
            idx = jnp.arange(0, d_head, 2, dtype=jnp.float32)
            inv_freq = THETA ** (-idx / d_head)
            angles = jnp.arange(seq_len, dtype=jnp.float32)[:, None] * inv_freq[None, :]
            return (jnp.cos(angles), jnp.sin(angles))

        def _apply_rope(x, cos, sin):
            B, H, S, d = x.shape
            xp = x.reshape(B, H, S, d // 2, 2)
            xe, xo = (xp[..., 0], xp[..., 1])
            rot = jnp.stack([xe * cos - xo * sin, xe * sin + xo * cos], axis=-1)
            return rot.reshape(B, H, S, d)
        key = jax.random.key(seed)
        k_x, k_q, k_k, k_v, k_o = jax.random.split(key, 5)
        std = math.sqrt(2.0 / (D_MODEL + D_MODEL))
        x = jax.random.normal(k_x, (4, 256, D_MODEL), dtype=jnp.float32)
        Wq = jax.random.normal(k_q, (D_MODEL, D_MODEL), dtype=jnp.float32) * std
        Wk = jax.random.normal(k_k, (D_MODEL, D_MODEL), dtype=jnp.float32) * std
        Wv = jax.random.normal(k_v, (D_MODEL, D_MODEL), dtype=jnp.float32) * std
        Wo = jax.random.normal(k_o, (D_MODEL, D_MODEL), dtype=jnp.float32) * std
        return {'x': x, 'Wq': Wq, 'Wk': Wk, 'Wv': Wv, 'Wo': Wo}
    _L1_attn_b_in = _L1_attn_b_setup()

    def _L1_ffn_setup():
        import jax, jax.numpy as jnp
        import numpy as np
        B, S, H, I, E, F, K, R, TOPK = (1, 128, 256, 176, 64, 8, 8, 8, 6)
        ISH = 2 * I

        def _fused_linear(x, W, qa, qb, scale, w):
            out = x @ W.T
            a = jnp.einsum('th,krh->tkr', x, qa)
            b = jnp.einsum('tkr,khr->tkh', a, qb)
            mix = jnp.einsum('tkh,tk->th', b, w)
            return out + scale[None, :] * mix

        def _moe_forward(hidden_states, gate_weight, inv_mapping, mask_up_W, gate_W, gate_qa, gate_qb, gate_scale, up_W, up_qa, up_qb, up_scale, down_W, down_qa, down_qb, down_scale, sh_gate_W, sh_up_W, sh_down_W):
            b, s, h = hidden_states.shape
            x = hidden_states.reshape(-1, h)
            T = x.shape[0]
            scores = jax.nn.softmax(x @ gate_weight.T, axis=-1)
            topk_w, topk_idx = jax.lax.top_k(scores, TOPK)
            w_dense = jnp.zeros((T, E), x.dtype).at[jnp.arange(T)[:, None], topk_idx].add(topk_w)
            flat = w_dense[:, inv_mapping]
            scalar = flat.sum(-1)
            soft = jax.nn.softmax(jnp.where(flat == 0, -1000000000.0, flat), axis=-1)

            def expert(muW, gW, gqa, gqb, gs, uW, uqa, uqb, us, dW, dqa, dqb, ds, w):
                xe = x + w @ muW.T
                gate = jax.nn.silu(_fused_linear(xe, gW, gqa, gqb, gs, w))
                up = _fused_linear(xe, uW, uqa, uqb, us, w)
                return _fused_linear(gate * up, dW, dqa, dqb, ds, w)
            outs = jax.vmap(expert, in_axes=(0,) * 13 + (1,))(mask_up_W, gate_W, gate_qa, gate_qb, gate_scale, up_W, up_qa, up_qb, up_scale, down_W, down_qa, down_qb, down_scale, soft)
            y = jnp.einsum('fth,tf->th', outs, scalar).reshape(b, s, h)
            sh = jax.nn.silu(hidden_states @ sh_gate_W.T) * (hidden_states @ sh_up_W.T) @ sh_down_W.T
            return y + sh
        key = jax.random.key(seed)
        ks = jax.random.split(key, 20)
        g = lambda k, shape, s=0.02: jax.random.normal(k, shape, jnp.float32) * s
        return {'hidden_states': jax.random.normal(ks[0], (B, S, H), jnp.float32), 'gate_weight': g(ks[1], (E, H)), 'inv_mapping': jnp.arange(E, dtype=jnp.int32).reshape(F, K), 'mask_up_W': g(ks[2], (F, H, K)), 'gate_W': g(ks[3], (F, I, H)), 'gate_qa': g(ks[4], (F, K, R, H)), 'gate_qb': g(ks[5], (F, K, I, R)), 'gate_scale': jnp.full((F, I), 0.1, jnp.float32), 'up_W': g(ks[6], (F, I, H)), 'up_qa': g(ks[7], (F, K, R, H)), 'up_qb': g(ks[8], (F, K, I, R)), 'up_scale': jnp.full((F, I), 0.1, jnp.float32), 'down_W': g(ks[9], (F, H, I)), 'down_qa': g(ks[10], (F, K, R, I)), 'down_qb': g(ks[11], (F, K, H, R)), 'down_scale': jnp.full((F, H), 0.1, jnp.float32), 'sh_gate_W': g(ks[12], (ISH, H)), 'sh_up_W': g(ks[13], (ISH, H)), 'sh_down_W': g(ks[14], (H, ISH))}
    _L1_ffn_in = _L1_ffn_setup()
    _d = {'L0_attn_a_query': _L0_attn_a_in['query'], 'L0_attn_a_w_q': _L0_attn_a_in['w_q'], 'L0_attn_a_b_q': _L0_attn_a_in['b_q'], 'L0_attn_a_w_k': _L0_attn_a_in['w_k'], 'L0_attn_a_b_k': _L0_attn_a_in['b_k'], 'L0_attn_a_w_v': _L0_attn_a_in['w_v'], 'L0_attn_a_b_v': _L0_attn_a_in['b_v'], 'L0_attn_a_w_o': _L0_attn_a_in['w_o'], 'L0_attn_a_b_o': _L0_attn_a_in['b_o'], 'L0_attn_b_Wq': _L0_attn_b_in['Wq'], 'L0_attn_b_bq': _L0_attn_b_in['bq'], 'L0_attn_b_Wk': _L0_attn_b_in['Wk'], 'L0_attn_b_bk': _L0_attn_b_in['bk'], 'L0_attn_b_Wv': _L0_attn_b_in['Wv'], 'L0_attn_b_bv': _L0_attn_b_in['bv'], 'L0_attn_b_Wo': _L0_attn_b_in['Wo'], 'L0_attn_b_bo': _L0_attn_b_in['bo'], 'L0_attn_b_lq1': _L0_attn_b_in['lq1'], 'L0_attn_b_lk1': _L0_attn_b_in['lk1'], 'L0_attn_b_lq2': _L0_attn_b_in['lq2'], 'L0_attn_b_lk2': _L0_attn_b_in['lk2'], 'L0_attn_b_g_subln': _L0_attn_b_in['g_subln'], 'L0_ffn_weight': _L0_ffn_in['weight'], 'L0_ffn_bias': _L0_ffn_in['bias'], 'L0_ffn_ln_gamma': _L0_ffn_in['ln_gamma'], 'L0_ffn_ln_beta': _L0_ffn_in['ln_beta'], 'L1_attn_a_Wq': _L1_attn_a_in['Wq'], 'L1_attn_a_Wk': _L1_attn_a_in['Wk'], 'L1_attn_a_Wv': _L1_attn_a_in['Wv'], 'L1_attn_a_Wo': _L1_attn_a_in['Wo'], 'L1_attn_a_splat_positions': _L1_attn_a_in['splat_positions'], 'L1_attn_a_splat_directions': _L1_attn_a_in['splat_directions'], 'L1_attn_a_splat_log_scales': _L1_attn_a_in['splat_log_scales'], 'L1_attn_a_splat_log_amplitudes': _L1_attn_a_in['splat_log_amplitudes'], 'L1_attn_a_directional_strength': _L1_attn_a_in['directional_strength'], 'L1_attn_a_position_sensitivity': _L1_attn_a_in['position_sensitivity'], 'L1_attn_a_gsa_strength': _L1_attn_a_in['gsa_strength'], 'L1_attn_b_Wq': _L1_attn_b_in['Wq'], 'L1_attn_b_Wk': _L1_attn_b_in['Wk'], 'L1_attn_b_Wv': _L1_attn_b_in['Wv'], 'L1_attn_b_Wo': _L1_attn_b_in['Wo'], 'L1_ffn_gate_weight': _L1_ffn_in['gate_weight'], 'L1_ffn_inv_mapping': _L1_ffn_in['inv_mapping'], 'L1_ffn_mask_up_W': _L1_ffn_in['mask_up_W'], 'L1_ffn_gate_W': _L1_ffn_in['gate_W'], 'L1_ffn_gate_qa': _L1_ffn_in['gate_qa'], 'L1_ffn_gate_qb': _L1_ffn_in['gate_qb'], 'L1_ffn_gate_scale': _L1_ffn_in['gate_scale'], 'L1_ffn_up_W': _L1_ffn_in['up_W'], 'L1_ffn_up_qa': _L1_ffn_in['up_qa'], 'L1_ffn_up_qb': _L1_ffn_in['up_qb'], 'L1_ffn_up_scale': _L1_ffn_in['up_scale'], 'L1_ffn_down_W': _L1_ffn_in['down_W'], 'L1_ffn_down_qa': _L1_ffn_in['down_qa'], 'L1_ffn_down_qb': _L1_ffn_in['down_qb'], 'L1_ffn_down_scale': _L1_ffn_in['down_scale'], 'L1_ffn_sh_gate_W': _L1_ffn_in['sh_gate_W'], 'L1_ffn_sh_up_W': _L1_ffn_in['sh_up_W'], 'L1_ffn_sh_down_W': _L1_ffn_in['sh_down_W']}
    _x0 = _d['L0_attn_a_query']
    _d['L0_attn_a_query'] = jax.random.normal(jax.random.fold_in(jax.random.key(seed), 1), (4, 512, 256), dtype=_x0.dtype)
    del _x0
    return _d

def reference(L0_attn_a_query, L0_attn_a_w_q, L0_attn_a_b_q, L0_attn_a_w_k, L0_attn_a_b_k, L0_attn_a_w_v, L0_attn_a_b_v, L0_attn_a_w_o, L0_attn_a_b_o, L0_attn_b_Wq, L0_attn_b_bq, L0_attn_b_Wk, L0_attn_b_bk, L0_attn_b_Wv, L0_attn_b_bv, L0_attn_b_Wo, L0_attn_b_bo, L0_attn_b_lq1, L0_attn_b_lk1, L0_attn_b_lq2, L0_attn_b_lk2, L0_attn_b_g_subln, L0_ffn_weight, L0_ffn_bias, L0_ffn_ln_gamma, L0_ffn_ln_beta, L1_attn_a_Wq, L1_attn_a_Wk, L1_attn_a_Wv, L1_attn_a_Wo, L1_attn_a_splat_positions, L1_attn_a_splat_directions, L1_attn_a_splat_log_scales, L1_attn_a_splat_log_amplitudes, L1_attn_a_directional_strength, L1_attn_a_position_sensitivity, L1_attn_a_gsa_strength, L1_attn_b_Wq, L1_attn_b_Wk, L1_attn_b_Wv, L1_attn_b_Wo, L1_ffn_gate_weight, L1_ffn_inv_mapping, L1_ffn_mask_up_W, L1_ffn_gate_W, L1_ffn_gate_qa, L1_ffn_gate_qb, L1_ffn_gate_scale, L1_ffn_up_W, L1_ffn_up_qa, L1_ffn_up_qb, L1_ffn_up_scale, L1_ffn_down_W, L1_ffn_down_qa, L1_ffn_down_qb, L1_ffn_down_scale, L1_ffn_sh_gate_W, L1_ffn_sh_up_W, L1_ffn_sh_down_W):

    def _L0_attn_a_ref(query, w_q, b_q, w_k, b_k, w_v, b_v, w_o, b_o):
        import jax, jax.numpy as jnp
        import numpy as np
        B, T, D_MODEL = (4, 256, 256)
        NUM_HEADS, HEAD_SIZE = (16, 128)
        MODEL_SIZE = 256
        B_, T_, _ = query.shape
        q = (query @ w_q + b_q).reshape(B_, T_, NUM_HEADS, HEAD_SIZE)
        k = (query @ w_k + b_k).reshape(B_, T_, NUM_HEADS, HEAD_SIZE)
        v = (query @ w_v + b_v).reshape(B_, T_, NUM_HEADS, HEAD_SIZE)
        logits = jnp.einsum('bthd,bThd->bhtT', q, k) * jax.lax.rsqrt(jnp.float32(HEAD_SIZE))
        i = jnp.arange(T_, dtype=jnp.int32)[:, None]
        j = jnp.arange(T_, dtype=jnp.int32)
        mask = (i >= j).astype(logits.dtype)
        logits = logits - 10000000000.0 * (1.0 - mask)
        weights = jax.nn.softmax(logits, axis=-1)
        attn = jnp.einsum('bhtT,bThd->bthd', weights, v).reshape(B_, T_, NUM_HEADS * HEAD_SIZE)
        out = attn @ w_o + b_o
        return out

    def _L0_attn_b_ref(x, Wq, bq, Wk, bk, Wv, bv, Wo, bo, lq1, lk1, lq2, lk2, g_subln):
        import jax, jax.numpy as jnp
        import numpy as np
        EMBED_DIM = 256
        NUM_HEADS = 16
        NUM_KV_HEADS = 8
        N_REP = NUM_HEADS // NUM_KV_HEADS
        HEAD_DIM = EMBED_DIM // NUM_HEADS // 2
        DEPTH = 0
        LAMBDA_INIT = 0.8 - 0.6 * float(np.exp(-0.3 * DEPTH))
        EPS = 1e-06
        B, T, E = x.shape
        H, Hkv, hd = (NUM_HEADS, NUM_KV_HEADS, HEAD_DIM)
        q = (x @ Wq + bq).reshape(B, T, 2 * H, hd).transpose(0, 2, 1, 3)
        k = (x @ Wk + bk).reshape(B, T, 2 * Hkv, hd).transpose(0, 2, 1, 3)
        v = (x @ Wv + bv).reshape(B, T, Hkv, 2 * hd).transpose(0, 2, 1, 3)
        k = jnp.repeat(k, N_REP, axis=1)
        v = jnp.repeat(v, N_REP, axis=1)
        q = q * hd ** (-0.5)
        scores = jnp.einsum('bhtd,bhsd->bhts', q, k)
        causal = jnp.triu(jnp.full((T, T), -jnp.inf, jnp.float32), k=1)
        scores = jnp.nan_to_num(scores + causal)
        probs = jax.nn.softmax(scores.astype(jnp.float32), axis=-1).astype(scores.dtype)
        lam1 = jnp.exp(jnp.sum(lq1 * lk1))
        lam2 = jnp.exp(jnp.sum(lq2 * lk2))
        lam = lam1 - lam2 + LAMBDA_INIT
        probs = probs.reshape(B, H, 2, T, T)
        aw = probs[:, :, 0] - lam * probs[:, :, 1]
        attn = jnp.einsum('bhts,bhsd->bhtd', aw, v)
        rms = jax.lax.rsqrt(jnp.mean(attn * attn, axis=-1, keepdims=True) + EPS)
        attn = attn * rms * g_subln
        attn = attn * (1.0 - LAMBDA_INIT)
        attn = attn.transpose(0, 2, 1, 3).reshape(B, T, E)
        return attn @ Wo + bo

    def _L0_ffn_ref(x, weight, bias, ln_gamma, ln_beta):
        import jax, jax.numpy as jnp
        import numpy as np
        LN_EPS = 1e-05
        Q_EPS = 1e-05

        def ternary_quantize(w):
            scale = jnp.mean(jnp.abs(w))
            return jnp.clip(jnp.round(w / (scale + Q_EPS)), -1.0, 1.0)

        def layernorm(x, gamma, beta):
            mu = jnp.mean(x, axis=-1, keepdims=True)
            var = jnp.mean(jnp.square(x - mu), axis=-1, keepdims=True)
            return (x - mu) * jax.lax.rsqrt(var + LN_EPS) * gamma + beta
        xn = layernorm(x, ln_gamma, ln_beta)
        w_q = ternary_quantize(weight)
        return jnp.einsum('bsi,oi->bso', xn, w_q) + bias

    def _L1_attn_a_ref(hidden_states, Wq, Wk, Wv, Wo, splat_positions, splat_directions, splat_log_scales, splat_log_amplitudes, directional_strength, position_sensitivity, gsa_strength):
        import jax, jax.numpy as jnp
        import numpy as np
        H, NS = (16, 8)
        B, S, Dm = hidden_states.shape
        Hn, Ns, hd = splat_positions.shape

        def heads(x):
            return x.reshape(B, S, Hn, hd).transpose(0, 2, 1, 3)
        q = heads(hidden_states @ Wq.T)
        k = heads(hidden_states @ Wk.T)
        v = heads(hidden_states @ Wv.T)
        scores = jnp.einsum('bhid,bhjd->bhij', q, k) / jnp.sqrt(jnp.float32(hd))
        mask = jnp.tril(jnp.ones((S, S), bool))
        neg = jnp.finfo(scores.dtype).min

        def out_proj(attn):
            o = jnp.einsum('bhij,bhjd->bhid', attn, v)
            return o.transpose(0, 2, 1, 3).reshape(B, S, Dm) @ Wo.T
        std_out = out_proj(jax.nn.softmax(jnp.where(mask, scores, neg), axis=-1))
        scales = jnp.exp(splat_log_scales)
        amps = jnp.exp(splat_log_amplitudes)
        dirn = splat_directions / (jnp.linalg.norm(splat_directions, axis=-1, keepdims=True) + 1e-08)

        def splat_feats(x):
            diff = x[:, :, :, None, :] - splat_positions[None, :, None, :, :]
            gauss = jnp.exp(-0.5 * jnp.sum(diff * diff, -1) / (scales ** 2)[None, :, None, :])
            dirp = jnp.tanh(jnp.einsum('bhsnd,hnd->bhsn', diff, dirn))
            return (gauss, dirp)
        qg, qd = splat_feats(q)
        kg, kd = splat_feats(k)
        amp_b = amps[None, :, None, :]
        splat_attn = jnp.einsum('bhin,bhjn->bhij', amp_b * qg, kg) + directional_strength * jnp.einsum('bhin,bhjn->bhij', amp_b * qg * qd, kg * kd)
        gsa_scores = scores + position_sensitivity * splat_attn
        gsa_out = out_proj(jax.nn.softmax(jnp.where(mask, gsa_scores, neg), axis=-1))
        blend = jnp.minimum(jnp.float32(0.03), jax.nn.sigmoid(gsa_strength) * 0.15)
        return (1.0 - blend) * std_out + blend * gsa_out

    def _L1_attn_b_ref(x, Wq, Wk, Wv, Wo):
        import math
        import jax, jax.numpy as jnp
        import numpy as np
        D_MODEL = 256
        NUM_HEADS = 16
        D_HEAD = D_MODEL // NUM_HEADS
        THETA = 10000.0

        def _rope_tables(seq_len, d_head):
            idx = jnp.arange(0, d_head, 2, dtype=jnp.float32)
            inv_freq = THETA ** (-idx / d_head)
            angles = jnp.arange(seq_len, dtype=jnp.float32)[:, None] * inv_freq[None, :]
            return (jnp.cos(angles), jnp.sin(angles))

        def _apply_rope(x, cos, sin):
            B, H, S, d = x.shape
            xp = x.reshape(B, H, S, d // 2, 2)
            xe, xo = (xp[..., 0], xp[..., 1])
            rot = jnp.stack([xe * cos - xo * sin, xe * sin + xo * cos], axis=-1)
            return rot.reshape(B, H, S, d)
        B, S, D = x.shape
        H, dh = (NUM_HEADS, D_HEAD)

        def proj(W):
            y = jnp.einsum('bsi,oi->bso', x, W)
            return y.reshape(B, S, H, dh).transpose(0, 2, 1, 3)
        q, k, v = (proj(Wq), proj(Wk), proj(Wv))
        cos, sin = _rope_tables(S, dh)
        q = _apply_rope(q, cos, sin)
        k = _apply_rope(k, cos, sin)
        scores = jnp.einsum('bhqd,bhkd->bhqk', q.astype(jnp.float32), k.astype(jnp.float32)) / math.sqrt(dh)
        causal = jnp.tril(jnp.ones((S, S), dtype=bool))
        scores = jnp.where(causal, scores, jnp.finfo(jnp.float32).min)
        probs = jax.nn.softmax(scores, axis=-1).astype(v.dtype)
        attn = jnp.einsum('bhqk,bhkd->bhqd', probs, v)
        attn = attn.transpose(0, 2, 1, 3).reshape(B, S, D)
        return jnp.einsum('bsi,oi->bso', attn, Wo)

    def _L1_ffn_ref(hidden_states, gate_weight, inv_mapping, mask_up_W, gate_W, gate_qa, gate_qb, gate_scale, up_W, up_qa, up_qb, up_scale, down_W, down_qa, down_qb, down_scale, sh_gate_W, sh_up_W, sh_down_W):
        import jax, jax.numpy as jnp
        import numpy as np
        B, S, H, I, E, F, K, R, TOPK = (1, 128, 256, 176, 64, 8, 8, 8, 6)
        ISH = 2 * I

        def _fused_linear(x, W, qa, qb, scale, w):
            out = x @ W.T
            a = jnp.einsum('th,krh->tkr', x, qa)
            b = jnp.einsum('tkr,khr->tkh', a, qb)
            mix = jnp.einsum('tkh,tk->th', b, w)
            return out + scale[None, :] * mix

        def _moe_forward(hidden_states, gate_weight, inv_mapping, mask_up_W, gate_W, gate_qa, gate_qb, gate_scale, up_W, up_qa, up_qb, up_scale, down_W, down_qa, down_qb, down_scale, sh_gate_W, sh_up_W, sh_down_W):
            b, s, h = hidden_states.shape
            x = hidden_states.reshape(-1, h)
            T = x.shape[0]
            scores = jax.nn.softmax(x @ gate_weight.T, axis=-1)
            topk_w, topk_idx = jax.lax.top_k(scores, TOPK)
            w_dense = jnp.zeros((T, E), x.dtype).at[jnp.arange(T)[:, None], topk_idx].add(topk_w)
            flat = w_dense[:, inv_mapping]
            scalar = flat.sum(-1)
            soft = jax.nn.softmax(jnp.where(flat == 0, -1000000000.0, flat), axis=-1)

            def expert(muW, gW, gqa, gqb, gs, uW, uqa, uqb, us, dW, dqa, dqb, ds, w):
                xe = x + w @ muW.T
                gate = jax.nn.silu(_fused_linear(xe, gW, gqa, gqb, gs, w))
                up = _fused_linear(xe, uW, uqa, uqb, us, w)
                return _fused_linear(gate * up, dW, dqa, dqb, ds, w)
            outs = jax.vmap(expert, in_axes=(0,) * 13 + (1,))(mask_up_W, gate_W, gate_qa, gate_qb, gate_scale, up_W, up_qa, up_qb, up_scale, down_W, down_qa, down_qb, down_scale, soft)
            y = jnp.einsum('fth,tf->th', outs, scalar).reshape(b, s, h)
            sh = jax.nn.silu(hidden_states @ sh_gate_W.T) * (hidden_states @ sh_up_W.T) @ sh_down_W.T
            return y + sh
        return _moe_forward(hidden_states, gate_weight, inv_mapping, mask_up_W, gate_W, gate_qa, gate_qb, gate_scale, up_W, up_qa, up_qb, up_scale, down_W, down_qa, down_qb, down_scale, sh_gate_W, sh_up_W, sh_down_W)
    x = L0_attn_a_query
    x = x + _L0_attn_a_ref(_layernorm(x, axis=-1), L0_attn_a_w_q, L0_attn_a_b_q, L0_attn_a_w_k, L0_attn_a_b_k, L0_attn_a_w_v, L0_attn_a_b_v, L0_attn_a_w_o, L0_attn_a_b_o)
    x = x + _L0_ffn_ref(_layernorm(x, axis=-1), L0_ffn_weight, L0_ffn_bias, L0_ffn_ln_gamma, L0_ffn_ln_beta)
    x = x + _L0_attn_b_ref(_layernorm(x, axis=-1), L0_attn_b_Wq, L0_attn_b_bq, L0_attn_b_Wk, L0_attn_b_bk, L0_attn_b_Wv, L0_attn_b_bv, L0_attn_b_Wo, L0_attn_b_bo, L0_attn_b_lq1, L0_attn_b_lk1, L0_attn_b_lq2, L0_attn_b_lk2, L0_attn_b_g_subln)
    x = x + _L0_ffn_ref(_layernorm(x, axis=-1), L0_ffn_weight, L0_ffn_bias, L0_ffn_ln_gamma, L0_ffn_ln_beta)
    x = x + _L1_attn_a_ref(_layernorm(x, axis=-1), L1_attn_a_Wq, L1_attn_a_Wk, L1_attn_a_Wv, L1_attn_a_Wo, L1_attn_a_splat_positions, L1_attn_a_splat_directions, L1_attn_a_splat_log_scales, L1_attn_a_splat_log_amplitudes, L1_attn_a_directional_strength, L1_attn_a_position_sensitivity, L1_attn_a_gsa_strength)
    x = x + _L1_ffn_ref(_layernorm(x, axis=-1), L1_ffn_gate_weight, L1_ffn_inv_mapping, L1_ffn_mask_up_W, L1_ffn_gate_W, L1_ffn_gate_qa, L1_ffn_gate_qb, L1_ffn_gate_scale, L1_ffn_up_W, L1_ffn_up_qa, L1_ffn_up_qb, L1_ffn_up_scale, L1_ffn_down_W, L1_ffn_down_qa, L1_ffn_down_qb, L1_ffn_down_scale, L1_ffn_sh_gate_W, L1_ffn_sh_up_W, L1_ffn_sh_down_W)
    x = x + _L1_attn_b_ref(_layernorm(x, axis=-1), L1_attn_b_Wq, L1_attn_b_Wk, L1_attn_b_Wv, L1_attn_b_Wo)
    x = x + _L1_ffn_ref(_layernorm(x, axis=-1), L1_ffn_gate_weight, L1_ffn_inv_mapping, L1_ffn_mask_up_W, L1_ffn_gate_W, L1_ffn_gate_qa, L1_ffn_gate_qb, L1_ffn_gate_scale, L1_ffn_up_W, L1_ffn_up_qa, L1_ffn_up_qb, L1_ffn_up_scale, L1_ffn_down_W, L1_ffn_down_qa, L1_ffn_down_qb, L1_ffn_down_scale, L1_ffn_sh_gate_W, L1_ffn_sh_up_W, L1_ffn_sh_down_W)
    return x

_drawn_inputs = setup_inputs


def setup_inputs(seed=0):
    import zlib

    import numpy as np

    out = dict(_drawn_inputs(seed))
    spreads = {'L0_attn_a_b_q': (0.0, 2.0),
     'L0_attn_a_b_k': (0.0, 2.0),
     'L0_attn_a_b_v': (0.0, 0.8),
     'L0_attn_a_b_o': (0.0, 0.1),
     'L0_attn_b_bq': (0.0, 0.8),
     'L0_attn_b_bk': (0.0, 2.0),
     'L0_attn_b_bv': (0.0, 0.521),
     'L0_attn_b_bo': (0.0, 0.8),
     'L0_attn_b_g_subln': (1.0, 0.6),
     'L0_ffn_bias': (0.0, 0.696),
     'L0_ffn_ln_gamma': (1.0, 0.2),
     'L0_ffn_ln_beta': (0.0, 0.1),
     'L1_attn_a_splat_log_scales': (-0.2231435477733612, 0.6),
     'L1_attn_a_splat_log_amplitudes': (-2.079441547393799, 0.6),
     'L1_ffn_gate_scale': (0.10000000149011612, 0.6),
     'L1_ffn_up_scale': (0.10000000149011612, 0.6),
     'L1_ffn_down_scale': (0.10000000149011612, 0.6)}
    factors = {'L0_attn_a_w_q': 64.0,
     'L0_attn_a_w_k': 64.0,
     'L0_attn_a_w_v': 8.0,
     'L0_attn_a_w_o': 8.0,
     'L0_attn_b_Wq': 8.0,
     'L0_attn_b_Wk': 8.0,
     'L0_attn_b_Wv': 6.541,
     'L0_attn_b_Wo': 3.092,
     'L0_attn_b_lq1': 8.0,
     'L0_attn_b_lk1': 8.0,
     'L0_attn_b_lq2': 8.0,
     'L0_attn_b_lk2': 8.0,
     'L1_attn_a_Wq': 8.0,
     'L1_attn_a_Wk': 8.0,
     'L1_attn_a_Wv': 8.0,
     'L1_attn_a_Wo': 8.0,
     'L1_attn_a_splat_positions': 8.0,
     'L1_attn_a_splat_directions': 8.0,
     'L1_attn_b_Wq': 8.0,
     'L1_attn_b_Wk': 8.0,
     'L1_attn_b_Wv': 5.108,
     'L1_attn_b_Wo': 4.778,
     'L1_ffn_gate_weight': 8.0,
     'L1_ffn_mask_up_W': 8.0,
     'L1_ffn_gate_W': 8.0,
     'L1_ffn_gate_qa': 8.0,
     'L1_ffn_gate_qb': 8.0,
     'L1_ffn_up_W': 8.0,
     'L1_ffn_up_qa': 8.0,
     'L1_ffn_up_qb': 8.0,
     'L1_ffn_down_W': 8.0,
     'L1_ffn_down_qa': 8.0,
     'L1_ffn_down_qb': 8.0,
     'L1_ffn_sh_gate_W': 8.0,
     'L1_ffn_sh_up_W': 8.0,
     'L1_ffn_sh_down_W': 8.0}
    for name, (base, spread) in spreads.items():
        noise = np.random.default_rng([zlib.crc32(name.encode()), seed]).standard_normal(out[name].shape)
        drawn = base * np.exp(spread * noise) if base else spread * noise
        out[name] = jnp.asarray(drawn.astype(out[name].dtype))
    for name, factor in factors.items():
        out[name] = (out[name] * factor).astype(out[name].dtype)
    return out
```

```python
from contextlib import ExitStack

import numpy as np

import concourse.bass as bass
from concourse import mybir

F32 = mybir.dt.float32
BF16 = mybir.dt.bfloat16
I32 = mybir.dt.int32
ACT = mybir.ActivationFunctionType
ALU = mybir.AluOpType
AX = mybir.AxisListType

B, T, D = 4, 512, 256
P = 128
NT = T // P
KD = D // P
TURN = NT * D
LN_EPS = 1e-5
MASKED = -1e30

H0, DH0 = 16, 128
QKV0 = 3 * DH0
PACK0 = KD * QKV0 + 2 + DH0

LAMBDA_INIT = 0.8 - 0.6
SCALE_DIFF = float(8.0 ** -0.5)
RMS_EPS = 1e-6

H1, DH1 = 16, 16
STRIP = 32
HG = P // STRIP
NG = H1 // HG


class Counter:

    def __init__(self, ctx, nc, name):
        self.sem = ctx.enter_context(nc.semaphore(name))
        self.base = 0
        self.per = 0

    def begin(self, per, credit=0):
        self.per = per
        self.base += credit

    def at(self, turn, n):
        return turn * self.per + (self.base + n)

    def end(self, turns):
        self.base += self.per * turns


class Chain:

    PER = 64

    def __init__(self, c, name):
        self.counter = c.counter(name, 0)
        self.n = 0
        self.now = 0

    def link(self, eng, ins):
        ins.then_inc(self.counter.sem, 1)
        self.n += 1
        eng.wait_ge(self.counter.sem, self.counter.at(self.now, self.n))

    def begin_loop(self, eng):
        self.counter.base += self.n
        self.counter.per = self.PER

    def turn(self, turn):
        self.now, self.n = turn, 0

    def top_up(self, eng):
        assert 0 < self.n < self.PER
        eng.sem_inc(self.counter.sem, self.PER - self.n)

    def end(self, turns):
        self.counter.end(turns)


class Chip:

    def __init__(self, ctx, nc):
        self.nc = nc
        self.ctx = ctx
        self.signals = {}
        self.uses = {}
        sb = self.sb
        self.x = sb("x_resid", [P, B * TURN])
        self.xn = sb("x_normed", [P, NT, D])
        self.xnT = sb("x_normed_T", [P, KD, T])
        self.ident = sb("ident", [P, P])
        self.ident_bf = sb("ident_bf", [P, P], BF16)
        self.causal = sb("causal", [P, P], BF16)
        self.ones = sb("ones", [1, P])
        self.minus_half = sb("minus_half", [P, NT * H1])
        self.half = sb("half", [P, P])
        self.stats = sb("stats", [P, NT, 6])
        self.mean_var = sb("mean_var", [P, NT, 2])
        self.var_eps = sb("var_eps", [P, NT])
        self.rstd = sb("rstd", [P, NT])
        self.wait_mark = sb("wait_mark", [P, 1])
        self.bank = ctx.enter_context(nc.psum_tensor("bank", [P, 8, 512], F32))

    def sb(self, name, shape, dt=F32, ctx=None):
        self.uses[name] = self.uses.get(name, 0) + 1
        if self.uses[name] > 1:
            name = f"{name}_{self.uses[name]}"
        return (ctx or self.ctx).enter_context(self.nc.sbuf_tensor(name, shape, dt))

    def counter(self, name, per, credit=0):
        if name not in self.signals:
            self.signals[name] = Counter(self.ctx, self.nc, name)
        self.signals[name].begin(per, credit)
        return self.signals[name]

    def x_cols(self, b, start, n):
        return self.x[:, bass.ds(b * TURN + start, n)]


def build_constants(c, x_dram):
    nc = c.nc
    x_loaded = c.counter("x_loaded", 16)
    filled = c.counter("const_filled", 3)
    made = c.counter("const_made", 3)
    with nc.Block() as block:
        @block.sync
        def _(sp):
            sp.dma_start(c.x[:, :].rearrange("p (b t d) -> p b t d", b=B, t=NT),
                         x_dram.rearrange("b (t p) d -> p b t d", p=P)).then_inc(x_loaded.sem, 16)
            sp.wait_ge(x_loaded.sem, x_loaded.at(0, 16))

        @block.vector
        def _(dve):
            nc.vector.memset(c.ones[:, :], 1.0)
            nc.vector.memset(c.minus_half[:, :], -0.5)
            nc.vector.memset(c.half[:, :], 0.5)

        @block.gpsimd
        def _(pool):
            nc.gpsimd.memset(c.ident[:, :], 0.0).then_inc(filled.sem, 1)
            nc.gpsimd.memset(c.ident_bf[:, :], 0.0).then_inc(filled.sem, 1)
            nc.gpsimd.memset(c.causal[:, :], 0.0).then_inc(filled.sem, 1)
            pool.wait_ge(filled.sem, filled.at(0, 3))
            for eye in (c.ident, c.ident_bf):
                nc.gpsimd.affine_select(out=eye[:, :], in_=eye[:, :], compare_op=ALU.not_equal, fill=1.0,
                                        base=0, pattern=[[-1, P]], channel_multiplier=1).then_inc(made.sem, 1)
            nc.gpsimd.affine_select(out=c.causal[:, :], in_=c.causal[:, :], compare_op=ALU.is_ge, fill=MASKED,
                                    base=0, pattern=[[-1, P]], channel_multiplier=1).then_inc(made.sem, 1)
            pool.wait_ge(made.sem, made.at(0, 3))
    for s in (x_loaded, filled, made):
        s.end(1)


class Norm:

    def __init__(self, c, rounds=1):
        self.c = c
        self.stats_done = c.counter("stats_done", NT * rounds)
        self.moments_done = c.counter("moments_done", NT * rounds)
        self.var_ready = c.counter("var_ready", rounds)
        self.rstd_ready = c.counter("rstd_ready", rounds)
        self.xn_ready = c.counter("xn_ready", NT * rounds)
        self.xT_filled = c.counter("xT_filled", KD)
        self.xT_ready = c.counter("xT_ready", KD)

    def vector(self, dve, turn, source, out, round=0):
        c, nc, r = self.c, self.c.nc, round
        for t in range(NT):
            nc.vector.bn_stats(c.stats[:, t, :], source(t)).then_inc(self.stats_done.sem, 1)
        dve.wait_ge(self.stats_done.sem, self.stats_done.at(turn, NT * (r + 1)))
        nc.vector.memset(c.wait_mark[:, :], 0.0)
        for t in range(NT):
            nc.vector.bn_aggr(c.mean_var[:, t, :], c.stats[:, t, :]).then_inc(self.moments_done.sem, 1)
        dve.wait_ge(self.moments_done.sem, self.moments_done.at(turn, NT * (r + 1)))
        nc.vector.tensor_scalar_add(c.var_eps[:, :], c.mean_var[:, :, 1], LN_EPS).then_inc(self.var_ready.sem, 1)
        dve.wait_ge(self.rstd_ready.sem, self.rstd_ready.at(turn, r + 1))
        for t in range(NT):
            nc.vector.tensor_scalar(out(t), source(t), c.mean_var[:, t, 0:1], c.rstd[:, t:t + 1],
                                    ALU.subtract, ALU.mult).then_inc(self.xn_ready.sem, 1)

    def pool(self, pool, turn, round=0):
        c = self.c
        pool.wait_ge(self.var_ready.sem, self.var_ready.at(turn, round + 1))
        c.nc.gpsimd.tensor_tensor(c.rstd[:, :], c.var_eps[:, :], c.minus_half[:, 0:NT],
                                  ALU.pow).then_inc(self.rstd_ready.sem, 1)

    def tensor(self, pe, banks):
        c = self.c
        for k in range(KD):
            for t in range(NT):
                last = c.nc.tensor.transpose(c.bank[:, banks[k], t * P:(t + 1) * P],
                                             c.xn[:, t, k * P:(k + 1) * P], c.ident[:, :])
            last.then_inc(self.xT_filled.sem, 1)

    def scalar(self, act, turn, banks):
        c = self.c
        for k in range(KD):
            act.wait_ge(self.xT_filled.sem, self.xT_filled.at(turn, k + 1))
            c.nc.scalar.copy(c.xnT[:, k, :], c.bank[:, banks[k], :]).then_inc(self.xT_ready.sem, 1)

    def end(self):
        for s in (self.stats_done, self.moments_done, self.var_ready, self.rstd_ready,
                  self.xn_ready, self.xT_filled, self.xT_ready):
            s.end(B)


def build_ffn(c, w_dram, bias_dram, affine_dram):
    nc = c.nc
    norm = Norm(c, rounds=2)
    loaded = [c.counter(f"ffn_loaded{i}", 16) for i in range(3)]
    abs_done = c.counter("ffn_abs_done", 1)
    mean_filled = c.counter("ffn_mean_filled", 1)
    limit_ready = c.counter("ffn_limit_ready", 2)
    low_ready = c.counter("ffn_low_ready", 1)
    w_ready = c.counter("ffn_w_ready", 1)
    ones_ready = c.counter("ffn_ones_ready", 1)
    scaled = c.counter("ffn_scaled", 1)
    affine_done = c.counter("ffn_affine_done", 1)
    y_filled = c.counter("ffn_y_filled", 2)
    with ExitStack() as ctx:
        w = c.sb("ffn_w", [P, KD, D], ctx=ctx)
        low = c.sb("ffn_low", [P, KD, D], ctx=ctx)
        bias = c.sb("ffn_bias", [1, 2 * D], ctx=ctx)
        affine = c.sb("ffn_affine", [P, 2, D], ctx=ctx)
        all_ones = c.sb("ffn_all_ones", [P, P], ctx=ctx)
        abs_sum = c.sb("ffn_abs_sum", [P, 1], ctx=ctx)
        limit = c.sb("ffn_limit", [P, 2], ctx=ctx)
        block = ctx.enter_context(nc.Block())

        @block.sync
        def _(sp):
            sp.dma_start(w[:, :, :], w_dram).then_inc(loaded[0].sem, 16)
            sp.dma_start(bias[:, :], bias_dram).then_inc(loaded[1].sem, 16)
            sp.dma_start(affine[:, :, :], affine_dram).then_inc(loaded[2].sem, 16)

        @block.vector
        def _(dve):
            nc.vector.memset(all_ones[:, :], 1.0).then_inc(ones_ready.sem, 1)
            dve.wait_ge(loaded[0].sem, loaded[0].at(0, 16))
            nc.vector.tensor_reduce(abs_sum[:, :], w[:, :, :], axis=AX.XY, op=ALU.add,
                                    apply_absolute_value=True).then_inc(abs_done.sem, 1)
            dve.wait_ge(mean_filled.sem, mean_filled.at(0, 1))
            nc.vector.tensor_scalar(limit[:, 0:1], c.bank[:, 0, 0:1], 0.5 / (D * D), 0.5e-5,
                                    ALU.mult, ALU.add).then_inc(limit_ready.sem, 1)
            dve.wait_ge(limit_ready.sem, limit_ready.at(0, 1))
            nc.vector.tensor_scalar_mul(limit[:, 1:2], limit[:, 0:1], -1.0).then_inc(limit_ready.sem, 1)
            dve.wait_ge(limit_ready.sem, limit_ready.at(0, 2))
            nc.vector.tensor_scalar(low[:, :, :], w[:, :, :], limit[:, 1:2], None,
                                    ALU.is_lt).then_inc(low_ready.sem, 1)
            dve.wait_ge(low_ready.sem, low_ready.at(0, 1))
            nc.vector.scalar_tensor_tensor(w[:, :, :], w[:, :, :], limit[:, 0:1], low[:, :, :],
                                           ALU.is_gt, ALU.subtract).then_inc(w_ready.sem, 1)
            dve.wait_ge(loaded[2].sem, loaded[2].at(0, 16))
            with dve.Fori(0, B) as b:
                norm.vector(dve, b, lambda t: c.x_cols(b, t * D, D), lambda t: c.xn[:, t, :])
                dve.wait_ge(norm.xn_ready.sem, norm.xn_ready.at(b, NT))
                norm.vector(dve, b, lambda t: c.xn[:, t, :], lambda t: c.xn[:, t, :], round=1)
                dve.wait_ge(norm.xn_ready.sem, norm.xn_ready.at(b, 2 * NT))
                nc.vector.tensor_tensor(c.xn[:, :, :], c.xn[:, :, :],
                                        affine[:, 0:1, :].broadcast_to([P, NT, D]), ALU.mult).then_inc(scaled.sem, 1)
                dve.wait_ge(scaled.sem, scaled.at(b, 1))
                nc.vector.tensor_tensor(c.xn[:, :, :], c.xn[:, :, :],
                                        affine[:, 1:2, :].broadcast_to([P, NT, D]), ALU.add).then_inc(affine_done.sem, 1)
                for half in range(2):
                    dve.wait_ge(y_filled.sem, y_filled.at(b, half + 1))
                    xs = c.x_cols(b, half * 512, 512)
                    nc.vector.tensor_tensor(xs, xs, c.bank[:, 2 + half, :], ALU.add)

        @block.gpsimd
        def _(pool):
            with pool.Fori(0, B) as b:
                norm.pool(pool, b)
                norm.pool(pool, b, round=1)

        @block.tensor
        def _(pe):
            pe.wait_ge(ones_ready.sem, ones_ready.at(0, 1))
            pe.wait_ge(abs_done.sem, abs_done.at(0, 1))
            nc.tensor.matmul(c.bank[:, 0, 0:1], all_ones[:, :], abs_sum[:, :],
                             start=True, stop=True).then_inc(mean_filled.sem, 1)
            pe.wait_ge(w_ready.sem, w_ready.at(0, 1))
            pe.wait_ge(loaded[1].sem, loaded[1].at(0, 16))
            with pe.Fori(0, B) as b:
                pe.wait_ge(affine_done.sem, affine_done.at(b, 1))
                norm.tensor(pe, (0, 1))
                pe.wait_ge(norm.xT_ready.sem, norm.xT_ready.at(b, KD))
                for half in range(2):
                    nc.tensor.matmul(c.bank[:, 2 + half, :], c.ones[:, :], bias[:, :], start=True, stop=True)
                    for t in (2 * half, 2 * half + 1):
                        for k in range(KD):
                            last = nc.tensor.matmul(c.bank[:, 2 + half, (t % 2) * D:(t % 2 + 1) * D],
                                                    c.xnT[:, k, t * P:(t + 1) * P], w[:, k, :],
                                                    start=False, stop=(k == KD - 1),
                                                    skip_group_check=True)
                    last.then_inc(y_filled.sem, 1)

        @block.scalar
        def _(act):
            with act.Fori(0, B) as b:
                norm.scalar(act, b, (0, 1))
    norm.end()
    for s in (*loaded, abs_done, mean_filled, limit_ready, low_ready, w_ready, ones_ready):
        s.end(1)
    for s in (scaled, affine_done, y_filled):
        s.end(B)


def build_big_attention(c, w_dram, wo_dram, bo_dram):
    nc = c.nc
    scale = float(1.0 / np.sqrt(np.float32(DH0)))
    pairs = H0 // 2
    norm = Norm(c)
    w_loaded = [c.counter(f"big_w_loaded{p}", 16) for p in range(2)]
    wo_loaded = [c.counter(f"big_wo_loaded{p}", 16) for p in range(2)]
    bo_loaded = c.counter("big_bo_loaded", 16)
    bq_ready = c.counter("big_bq_ready", 1)
    proj_filled = c.counter("big_proj_filled", 3)
    qk_ready = c.counter("big_qk_ready", 2, credit=4)
    v_ready = c.counter("big_v_ready", 1, credit=2)
    s_filled = c.counter("big_s_filled", NT)
    max_ready = c.counter("big_max_ready", NT)
    exp_done = c.counter("big_exp_done", NT)
    rinv_ready = c.counter("big_rinv_ready", NT)
    p_ready = c.counter("big_p_ready", NT)
    t_filled = c.counter("big_t_filled", NT)
    pt_ready = c.counter("big_pt_ready", NT)
    ot_filled = c.counter("big_ot_filled", 1)
    ot_ready = c.counter("big_ot_ready", 1)
    head_added = c.counter("big_head_added", 1, credit=2)
    QV, K, S0, TB, OTB, Y0 = 0, 1, 2, 4, 5, 6
    with ExitStack() as ctx:
        w = c.sb("big_w", [P, 2, PACK0], ctx=ctx)
        wo = c.sb("big_wo", [P, 2, D], ctx=ctx)
        bo = c.sb("big_bo", [1, 2 * D], ctx=ctx)
        bq_scaled = c.sb("big_bq_scaled", [P, 2], ctx=ctx)
        qT = c.sb("big_qT", [P, 2, T], ctx=ctx)
        kT = c.sb("big_kT", [P, 2, T], ctx=ctx)
        v = c.sb("big_v", [P, 2, NT, DH0], ctx=ctx)
        probs = c.sb("big_probs", [P, NT, T], ctx=ctx)
        pT = c.sb("big_pT", [P, 2, NT, T], ctx=ctx)
        oT = c.sb("big_oT", [P, 2, T], ctx=ctx)
        neg_max = c.sb("big_neg_max", [P, 2, NT], ctx=ctx)
        total = c.sb("big_total", [P, 2, NT], ctx=ctx)
        rinv = c.sb("big_rinv", [P, 2, NT], ctx=ctx)
        block = ctx.enter_context(nc.Block())

        def each_turn(eng, start, unit, end):
            with eng.Fori(0, B) as b:
                start(b)
                for slot in (0, 1):
                    unit(b * pairs, slot, first=(slot == 0), last=False)
                with eng.Fori(1, pairs - 1) as pair:
                    for slot in (0, 1):
                        unit(b * pairs + pair, slot, first=False, last=False)
                for slot in (0, 1):
                    unit(b * pairs + (pairs - 1), slot, first=False, last=(slot == 1))
                end(b)

        def following(g, slot):
            return (g, 1) if slot == 0 else (g + 1, 0)

        @block.sync
        def _(sp):
            sp.dma_start(bo[:, :], bo_dram).then_inc(bo_loaded.sem, 16)
            with sp.Fori(0, B) as b:
                with sp.Fori(0, pairs) as pair:
                    for slot in (0, 1):
                        u = (b * pairs + pair) * 2 + slot
                        head = sp.snap(pair * 2 + slot)
                        sp.wait_ge(v_ready.sem, v_ready.at(u, -1))
                        sp.wait_ge(qk_ready.sem, qk_ready.at(u, -2))
                        sp.dma_start(w[:, slot, :], w_dram[bass.ds(head, 1)]
                                     .rearrange("a p n -> p (a n)")).then_inc(w_loaded[slot].sem, 16)
                        sp.wait_ge(head_added.sem, head_added.at(u, -1))
                        sp.dma_start(wo[:, slot, :], wo_dram[bass.ds(head, 1)]
                                     .rearrange("a p n -> p (a n)")).then_inc(wo_loaded[slot].sem, 16)

        @block.tensor
        def _(pe):
            def project(slot, part):
                def cols(k):
                    return w[:, slot, k * QKV0 + part * DH0:k * QKV0 + (part + 1) * DH0]
                if part < 2:
                    for k in range(KD):
                        last = nc.tensor.matmul(c.bank[:, (QV, K)[part], :], cols(k), c.xnT[:, k, :],
                                                start=(k == 0), stop=(k == KD - 1))
                else:
                    for t in range(NT):
                        for k in range(KD):
                            last = nc.tensor.matmul(c.bank[:, QV, t * P:(t + 1) * P],
                                                    c.xnT[:, k, t * P:(t + 1) * P], cols(k),
                                                    start=(k == 0), stop=(k == KD - 1))
                last.then_inc(proj_filled.sem, 1)

            def scores(slot, i):
                bank, width = S0 + i % 2, (i + 1) * P
                nc.tensor.matmul(c.bank[:, bank, 0:width], qT[:, slot, i * P:width], kT[:, slot, 0:width],
                                 start=True, stop=False)
                nc.tensor.matmul(c.bank[:, bank, i * P:width], c.ident_bf[:, :], c.causal[:, :],
                                 start=False, stop=True).then_inc(s_filled.sem, 1)

            def transposes(u, i):
                pe.wait_ge(p_ready.sem, p_ready.at(u, i + 1))
                if i:
                    pe.wait_ge(pt_ready.sem, pt_ready.at(u, i))
                for j in range(i + 1):
                    last = nc.tensor.transpose(c.bank[:, TB, j * P:(j + 1) * P],
                                               probs[:, i, j * P:(j + 1) * P], c.ident[:, :])
                last.then_inc(t_filled.sem, 1)

            def add_head(u, g, slot, final):
                pe.wait_ge(ot_ready.sem, ot_ready.at(u, 1))
                pe.wait_ge(wo_loaded[slot].sem, wo_loaded[slot].at(g, 16))
                for t in range(NT):
                    last = nc.tensor.matmul(c.bank[:, Y0 + t // 2, (t % 2) * D:(t % 2 + 1) * D],
                                            oT[:, slot, t * P:(t + 1) * P], wo[:, slot, :],
                                            start=False, stop=final, skip_group_check=True)
                last.then_inc(head_added.sem, 1)

            def start(b):
                pe.wait_ge(norm.xn_ready.sem, norm.xn_ready.at(b, NT))
                norm.tensor(pe, (TB, OTB))
                for bank in (Y0, Y0 + 1):
                    nc.tensor.matmul(c.bank[:, bank, :], c.ones[:, :], bo[:, :], start=True, stop=True)
                pe.wait_ge(norm.xT_ready.sem, norm.xT_ready.at(b, KD))
                pe.wait_ge(w_loaded[0].sem, w_loaded[0].at(b * pairs, 16))
                project(0, 0)
                project(0, 1)
                pe.wait_ge(qk_ready.sem, qk_ready.at(b * H0, 1))
                project(0, 2)

            def unit(g, slot, first, last):
                u = g * 2 + slot
                g_next, slot_next = following(g, slot)
                pe.wait_ge(qk_ready.sem, qk_ready.at(u, 2))
                scores(slot, 0)
                scores(slot, 1)
                pe.wait_ge(v_ready.sem, v_ready.at(u, 1))
                if not last:
                    pe.wait_ge(w_loaded[slot_next].sem, w_loaded[slot_next].at(g_next, 16))
                    project(slot_next, 0)
                transposes(u, 0)
                pe.wait_ge(exp_done.sem, exp_done.at(u, 1))
                scores(slot, 2)
                if not last:
                    project(slot_next, 1)
                transposes(u, 1)
                pe.wait_ge(exp_done.sem, exp_done.at(u, 2))
                scores(slot, 3)
                transposes(u, 2)
                if not first:
                    add_head(u + -1, g + (-1 if slot == 0 else 0), 1 - slot, False)
                if not last:
                    pe.wait_ge(qk_ready.sem, qk_ready.at(u, 3))
                    project(slot_next, 2)
                transposes(u, 3)
                pe.wait_ge(pt_ready.sem, pt_ready.at(u, NT))
                for j in range(NT):
                    mm = nc.tensor.matmul(c.bank[:, OTB, j * P:T], v[:, slot, j, :], pT[:, slot, j, j * P:T],
                                          start=(j == 0), stop=(j == NT - 1))
                mm.then_inc(ot_filled.sem, 1)

            def end(b):
                add_head(b * H0 + (H0 - 1), b * pairs + (pairs - 1), 1, True)

            pe.wait_ge(bo_loaded.sem, bo_loaded.at(0, 16))
            each_turn(pe, start, unit, end)

        @block.scalar
        def _(act):
            def copy_q(u, slot):
                act.wait_ge(bq_ready.sem, bq_ready.at(u, 1))
                act.wait_ge(proj_filled.sem, proj_filled.at(u, 1))
                nc.scalar.activation(qT[:, slot, :], c.bank[:, QV, :], ACT.Identity,
                                     bias=bq_scaled[:, slot:slot + 1], scale=scale).then_inc(qk_ready.sem, 1)

            def copy_k(u, slot):
                act.wait_ge(proj_filled.sem, proj_filled.at(u, 2))
                at = KD * QKV0 + 1
                nc.scalar.activation(kT[:, slot, :], c.bank[:, K, :], ACT.Identity,
                                     bias=w[:, slot, at:at + 1]).then_inc(qk_ready.sem, 1)

            def exponential(u, slot, i):
                act.wait_ge(max_ready.sem, max_ready.at(u, i + 1))
                width = (i + 1) * P
                nc.scalar.activation(probs[:, i, 0:width], c.bank[:, S0 + i % 2, 0:width], ACT.Exp,
                                     bias=neg_max[:, slot, i:i + 1],
                                     accum_out=total[:, slot, i:i + 1]).then_inc(exp_done.sem, 1)

            def start(b):
                norm.scalar(act, b, (TB, OTB))
                copy_q(b * H0, 0)
                copy_k(b * H0, 0)

            def unit(g, slot, first, last):
                u = g * 2 + slot
                exponential(u, slot, 0)
                exponential(u, slot, 1)
                if not last:
                    copy_q(u + 1, 1 - slot)
                exponential(u, slot, 2)
                if not last:
                    copy_k(u + 1, 1 - slot)
                exponential(u, slot, 3)
                act.wait_ge(ot_filled.sem, ot_filled.at(u, 1))
                nc.scalar.copy(oT[:, slot, :], c.bank[:, OTB, :]).then_inc(ot_ready.sem, 1)

            act.sem_inc(qk_ready.sem, 4)
            each_turn(act, start, unit, lambda b: None)

        @block.vector
        def _(dve):
            def scale_bias(g, slot, u):
                dve.wait_ge(w_loaded[slot].sem, w_loaded[slot].at(g, 16))
                nc.vector.tensor_scalar_mul(bq_scaled[:, slot:slot + 1], w[:, slot, KD * QKV0:KD * QKV0 + 1],
                                            scale).then_inc(bq_ready.sem, 1)

            def copy_v(u, slot):
                dve.wait_ge(proj_filled.sem, proj_filled.at(u, 3))
                bias = w[:, slot, KD * QKV0 + 2:PACK0].rearrange("p (a n) -> p a n", a=1)
                nc.vector.tensor_tensor(v[:, slot, :, :], c.bank[:, QV, :].rearrange("p (t n) -> p t n", t=NT),
                                        bias.broadcast_to([P, NT, DH0]), ALU.add).then_inc(v_ready.sem, 1)

            def maximum(u, slot, i):
                dve.wait_ge(s_filled.sem, s_filled.at(u, i + 1))
                nc.vector.tensor_reduce(neg_max[:, slot, i:i + 1], c.bank[:, S0 + i % 2, 0:(i + 1) * P],
                                        axis=AX.X, op=ALU.max, negate=True).then_inc(max_ready.sem, 1)

            def normalise(u, slot, i):
                dve.wait_ge(exp_done.sem, exp_done.at(u, i + 1))
                nc.vector.reciprocal(rinv[:, slot, i:i + 1], total[:, slot, i:i + 1]).then_inc(rinv_ready.sem, 1)
                dve.wait_ge(rinv_ready.sem, rinv_ready.at(u, i + 1))
                row = probs[:, i, 0:(i + 1) * P]
                nc.vector.tensor_scalar(row, row, rinv[:, slot, i:i + 1], None, ALU.mult).then_inc(p_ready.sem, 1)

            def copy_pT(u, slot, i):
                dve.wait_ge(t_filled.sem, t_filled.at(u, i + 1))
                nc.vector.tensor_copy(pT[:, slot, 0:i + 1, i * P:(i + 1) * P],
                                      c.bank[:, TB, 0:(i + 1) * P].rearrange("p (j q) -> p j q", q=P))\
                  .then_inc(pt_ready.sem, 1)

            def start(b):
                norm.vector(dve, b, lambda t: c.x_cols(b, t * D, D), lambda t: c.xn[:, t, :])
                scale_bias(b * pairs, 0, b * H0)
                copy_v(b * H0, 0)

            def unit(g, slot, first, last):
                u = g * 2 + slot
                maximum(u, slot, 0)
                maximum(u, slot, 1)
                if not last:
                    scale_bias(*following(g, slot), u + 1)
                normalise(u, slot, 0)
                copy_pT(u, slot, 0)
                maximum(u, slot, 2)
                normalise(u, slot, 1)
                copy_pT(u, slot, 1)
                maximum(u, slot, 3)
                normalise(u, slot, 2)
                copy_pT(u, slot, 2)
                normalise(u, slot, 3)
                if not last:
                    copy_v(u + 1, 1 - slot)
                copy_pT(u, slot, 3)

            def end(b):
                dve.wait_ge(head_added.sem, head_added.at(b * H0, H0))
                for half in range(2):
                    xs = c.x_cols(b, half * 512, 512)
                    nc.vector.tensor_tensor(xs, xs, c.bank[:, Y0 + half, :], ALU.add)

            dve.sem_inc(v_ready.sem, 2)
            each_turn(dve, start, unit, end)

        @block.gpsimd
        def _(pool):
            pool.sem_inc(head_added.sem, 2)
            with pool.Fori(0, B) as b:
                norm.pool(pool, b)
    norm.end()
    bo_loaded.end(1)
    for s in (*w_loaded, *wo_loaded):
        s.end(B * pairs)
    for s in (bq_ready, proj_filled, qk_ready, v_ready, s_filled, max_ready, exp_done, rinv_ready,
              p_ready, t_filled, pt_ready, ot_filled, ot_ready, head_added):
        s.end(B * H0)


def build_small_attention(c, kind, ins):
    nc = c.nc
    two = kind != "rope"
    QH = ins[f"{kind}_wq"].shape[-1]
    KH = ins[f"{kind}_wk"].shape[-1]
    VH = ins[f"{kind}_wv"].shape[-1]
    kv_repeat = D // VH
    dk = KH // H1
    cells = H1 * NT
    group_cells = HG * NT
    norm = Norm(c)

    wide = lambda n: [0, 1] if n == D else [0]
    plan = [("q", i) for i in wide(QH)] + [("k", i) for i in wide(KH)] + [("v", i) for i in wide(VH)]
    stacks_of = lambda what: [(f"{what} stack", h) for h in range(H1)]
    if kind == "rope":
        plan += stacks_of("q") + stacks_of("k")
    elif kind == "differential":
        plan += stacks_of("q") + stacks_of("k") + stacks_of("k2")
    else:
        plan += stacks_of("q") + [("qf", 0), ("qf", 1)] + stacks_of("k") + [("kf", 0), ("kf", 1)]
        plan += stacks_of("qf") + stacks_of("kf")
    splits = ("q", "k", "qf", "kf") if kind == "splat" else ("q", "k")

    def owner_of(s):
        what, part = plan[s]
        if what.endswith("stack"):
            return "scalar" if part % 2 == 0 else "vector"
        if what == "v":
            return "vector" if kind == "differential" else "scalar"
        return "scalar" if kind == "splat" and what in ("q", "k") else "vector"

    owner = [owner_of(s) for s in range(len(plan))]

    def bank_of(s):
        return 4 + s % 4

    def drains_up_to(s, eng):
        return sum(1 for o in owner[:s + 1] if o == eng)

    rows_filled = c.counter("rows_filled", len(plan))
    drained = {e: c.counter(f"rows_drained_{e}", drains_up_to(len(plan), e)) for e in ("scalar", "vector")}
    loads = {"differential": ("wq", "wk", "wv", "wo", "bq", "bk", "bv", "bo", "lam", "gsub"),
             "splat": ("wq", "wk", "wv", "wo", "pos", "dir", "logs", "blocks", "masks", "scal"),
             "rope": ("wq", "wk", "wv", "wo", "cos", "sin")}[kind]
    loaded = {n: c.counter(f"small_loaded_{i}", 16) for i, n in enumerate(loads)}
    zeroed = c.counter("small_zeroed", 2)
    chain = Chain(c, "small_chain")
    split_ready = c.counter("small_split_ready", len(splits))
    blocks_ready = c.counter("small_blocks_ready", 1)
    sums_ready = c.counter("small_sums_ready", 1)
    setup_exp = c.counter("small_setup_exp", 1)
    args_ready = c.counter("small_args_ready", 2)
    features = c.counter("small_features", 2)
    s_filled = [c.counter(f"small_s{m}_filled", cells) for m in range(2)]
    max_ready = [c.counter(f"small_max{m}_ready", cells) for m in range(2)]
    exp_done = [c.counter(f"small_exp{m}_done", cells) for m in range(2)]
    inv_ready = c.counter("small_inv_ready", cells)
    weight_ready = c.counter("small_weight_ready", cells)
    p_ready = c.counter("small_p_ready", cells)
    t_filled = c.counter("small_t_filled", cells)
    pt_ready = c.counter("small_pt_ready", cells)
    ov_filled = c.counter("small_ov_filled", NG)
    ov_ready = c.counter("small_ov_ready", NG)
    or_filled = c.counter("small_or_filled", NG)
    or_read = c.counter("small_or_read", NG)
    group_done = c.counter("small_group_done", NG if kind == "differential" else 0)
    square_ready = c.counter("small_square_ready", NG)
    rms_ready = c.counter("small_rms_ready", NG)
    ot_filled = c.counter("small_ot_filled", KD)
    ot_ready = c.counter("small_ot_ready", KD)
    y_filled = c.counter("small_y_filled", 2)
    HALVED = ("q stack", "k stack") if kind == "splat" else ()
    OV, OR = 6, 7
    with ExitStack() as ctx:
        sb = lambda name, shape, dt=F32: c.sb(f"{kind}_{name}", shape, dt, ctx=ctx)
        held = {n: sb(n, list(ins[f"{kind}_{n}"].shape)) for n in loads if n not in ("pos", "dir")}
        v_rows = sb("v_rows", [P, NT, VH // DH1, STRIP])
        ops = ("q", "k", "k2") if kind == "differential" else splits
        stack = {n: sb(f"{n}_stack", [P, H1, T], BF16) for n in ops}
        pT = sb("pT", [P, 2, HG, NT, T])
        ROWS = NT * H1 * DH1
        arena = [pT[:, i // HG, i % HG, :, :].rearrange("p a b -> p (a b)") for i in range(2 * HG)]

        def in_arena(i, half, d=DH1):
            flat = arena[i][:, half * ROWS:half * ROWS + NT * H1 * d]
            return flat.rearrange("p (t h d) -> p t h d", t=NT, d=d)

        q_rows, k_rows = in_arena(0, 0), in_arena(0, 1, dk)
        rest = arena[1][:, 0:ROWS]
        PAD = DH1 - dk
        part_of = [arena[1][:, ROWS:2 * ROWS].bitcast(BF16)[:, i * ROWS:(i + 1) * ROWS] for i in range(2)]
        part_of.append(sb("low_part", [P, ROWS], BF16))
        in_parts = lambda half: pT[:, 1, half:half + 2, :, :].rearrange("p j a b -> p (j a b)").bitcast(BF16) \
            .rearrange("p (t h d) -> p t h d", t=NT, d=P)
        parts = {"q": in_parts(0), "k": sb("k_parts", [P, NT, H1, PAD + P], BF16) if PAD else in_parts(2)}
        probs = [sb(f"probs{m}", [P, 3, T]) for m in range(1 + two)]
        neg_max = [sb(f"neg_max{m}", [P, cells]) for m in range(2)]
        total = [sb(f"total{m}", [P, cells]) for m in range(2)]
        inv = sb("inv", [P, cells])
        weight = sb("weight", [P, cells])
        row_inv = sb("row_inv", [P, group_cells])
        ovT = sb("ovT", [P, T])
        attn = c.xn
        attnT = c.xnT
        if kind == "differential":
            square = sb("square", [P, NT, HG, DH1])
            mean_sq = sb("mean_sq", [P, NT, HG])
            rms = sb("rms", [P, NT, HG])
        if two:
            small = sb("small", [P, 8])
        if kind == "splat":
            half_p2, inv_norm, p_dir = (sb(n, [P, P]) for n in ("half_p2", "inv_norm", "p_dir"))
            half_q2 = sb("half_q2", [P, NT * H1])
            qf_rows, kf_rows = in_arena(2, 0), in_arena(2, 1)
            features_at = arena[3][:, 0:ROWS].rearrange("p (i t h n) -> p i t h n", i=2, t=NT, n=8)
            gauss, tilt = features_at[:, 0], features_at[:, 1]
            block_parts = sb("block_parts", [P, 2, H1, 16], BF16)
            block_steps = arena[6][:, 0:5 * D].rearrange("p (i n) -> p i n", i=5)
            square = arena[3][:, ROWS:2 * ROWS].rearrange("p (t d) -> p t d", d=DH1)
            raw_pos, raw_dir, work = arena[4], arena[5], arena[7]
        if kind == "rope":
            turned = [sb(f"turned{i}", [P, 2, H1, DH1]) for i in range(2)]
        block = ctx.enter_context(nc.Block())
        at_row = {"q": q_rows, "k": k_rows}

        def head_of(n):
            return n // group_cells, n // NT % HG, n % NT

        @block.sync
        def _(sp):
            for n in loads:
                target = {"pos": lambda: raw_pos, "dir": lambda: raw_dir}.get(n, lambda: held[n][:])()
                sp.dma_start(target, ins[f"{kind}_{n}"]).then_inc(loaded[n].sem, 16)

        @block.tensor
        def _(pe):
            def wait_drained(b, steps):
                for e in ("scalar", "vector"):
                    mine = [s for s in steps if owner[s] == e]
                    if mine:
                        pe.wait_ge(drained[e].sem, drained[e].at(b, drains_up_to(max(mine), e)))

            def project(s, what, part):
                w = held[f"w{what}"]
                n = w.shape[-1]
                per_bank = 512 // n
                for t in range(part * per_bank, (part + 1) * per_bank):
                    at = (t % per_bank) * n
                    for k in range(KD):
                        last = nc.tensor.matmul(c.bank[:, bank_of(s), at:at + n], c.xnT[:, k, t * P:(t + 1) * P],
                                                w[:, k, :], start=(k == 0), stop=(k == KD - 1))
                return last

            def make_stack(s, what, h):
                at = PAD if what == "k" else 0
                for t in range(NT):
                    last = nc.tensor.matmul(c.bank[:, bank_of(s), t * P:(t + 1) * P], parts[what[0]][:, t, h, at:at + P],
                                            c.ident_bf[:, :], start=True, stop=True)
                return last

            def splat_products(s, side, part):
                for t in (2 * part, 2 * part + 1):
                    for h in range(H1):
                        at = (t % 2) * D + h * 16
                        last = nc.tensor.matmul(c.bank[:, bank_of(s), at:at + 16], stack[side][:, h, t * P:(t + 1) * P],
                                                block_parts[:, "qk".index(side), h, :], start=True, stop=True)
                return last

            def fill(b, s):
                what, part = plan[s]
                source = what.split()[0]
                needs = [s - 4] if s >= 4 else []
                if what.endswith("stack") and part == 0 and source in splits:
                    pe.wait_ge(split_ready.sem, split_ready.at(b, splits.index(source) + 1))
                if what in ("qf", "kf") and part == 0:
                    needs += [plan.index((f"{what[0]} stack", h)) for h in range(H1)]
                wait_drained(b, needs)
                if what in ("q", "k", "v"):
                    return project(s, what, part)
                if what.endswith("stack"):
                    return make_stack(s, source, part)
                return splat_products(s, what[0], part)

            def scores(b, n):
                g, j, i = head_of(n)
                if n >= 2:
                    for m in range(1 + two):
                        pe.wait_ge(exp_done[m].sem, exp_done[m].at(b, n - 1))
                width = (i + 1) * P
                h = g * HG + j
                for m in range(1 + two):
                    bank = 2 * m + n % 2
                    pairs = [("q", "k2" if kind == "differential" and m == 1 else "k")]
                    if kind == "splat" and m == 1:
                        pairs.append(("qf", "kf"))
                    for first, (q, k) in enumerate(pairs):
                        nc.tensor.matmul(c.bank[:, bank, 0:width], stack[q][:, h, i * P:width],
                                         stack[k][:, h, 0:width], start=(first == 0), stop=False)
                    nc.tensor.matmul(c.bank[:, bank, i * P:width], c.ident_bf[:, :], c.causal[:, :],
                                     start=False, stop=True).then_inc(s_filled[m].sem, 1)

            def transposes(b, n):
                ready = p_ready if two else exp_done[0]
                pe.wait_ge(ready.sem, ready.at(b, n + 1))
                if n >= 2:
                    pe.wait_ge(pt_ready.sem, pt_ready.at(b, n - 1))
                for j in range(n % NT + 1):
                    last = nc.tensor.transpose(c.bank[:, 4 + n % 2, j * P:(j + 1) * P],
                                               probs[0][:, n % 3, j * P:(j + 1) * P], c.ident[:, :])
                last.then_inc(t_filled.sem, 1)

            def values(b, g):
                pe.wait_ge(pt_ready.sem, pt_ready.at(b, (g + 1) * group_cells))
                for key_tile in range(NT):
                    for j in range(HG):
                        last = nc.tensor.matmul(c.bank[STRIP * j:STRIP * (j + 1), OV, key_tile * P:T],
                                                v_rows[:, key_tile, (g * HG + j) // kv_repeat, :],
                                                pT[:, g % 2, j, key_tile, key_tile * P:T],
                                                start=(key_tile == 0), stop=(key_tile == NT - 1))
                last.then_inc(ov_filled.sem, 1)

            def values_by_row(b, g):
                pe.wait_ge(ov_ready.sem, ov_ready.at(b, g + 1))
                if g:
                    pe.wait_ge(or_read.sem, or_read.at(b, g))
                for t in range(NT):
                    last = nc.tensor.transpose(c.bank[:, OR, t * P:(t + 1) * P], ovT[:, t * P:(t + 1) * P],
                                               c.ident[:, :])
                last.then_inc(or_filled.sem, 1)

            for n in loads:
                if n in ("wq", "wk", "wv", "wo", "bo"):
                    pe.wait_ge(loaded[n].sem, loaded[n].at(0, 16))
            pe.wait_ge(zeroed.sem, zeroed.at(0, zeroed.per))
            if kind == "splat":
                pe.wait_ge(blocks_ready.sem, blocks_ready.at(0, 1))
            with pe.Fori(0, B) as b:
                pe.wait_ge(norm.xn_ready.sem, norm.xn_ready.at(b, NT))
                norm.tensor(pe, (0, 1))
                pe.wait_ge(norm.xT_ready.sem, norm.xT_ready.at(b, KD))
                for s in range(len(plan)):
                    fill(b, s).then_inc(rows_filled.sem, 1)
                for e in ("scalar", "vector"):
                    pe.wait_ge(drained[e].sem, drained[e].at(b, drained[e].per))
                for n in range(cells + 6):
                    if n < cells:
                        scores(b, n)
                    if 2 <= n < cells + 2:
                        transposes(b, n - 2)
                    if n % group_cells == 2 and n > 2:
                        values(b, n // group_cells - 1)
                    if n % group_cells == 4 and n > 4:
                        values_by_row(b, n // group_cells - 1)
                done = group_done if kind == "differential" else or_read
                pe.wait_ge(done.sem, done.at(b, NG))
                for k in range(KD):
                    for t in range(NT):
                        last = nc.tensor.transpose(c.bank[:, 4 + k, t * P:(t + 1) * P],
                                                   attn[:, t, k * P:(k + 1) * P], c.ident[:, :])
                    last.then_inc(ot_filled.sem, 1)
                pe.wait_ge(ot_ready.sem, ot_ready.at(b, KD))
                for half in range(2):
                    if "bo" in loads:
                        nc.tensor.matmul(c.bank[:, 6 + half, :], c.ones[:, :], held["bo"][:, :], start=True, stop=True)
                    for t in (2 * half, 2 * half + 1):
                        for k in range(KD):
                            last = nc.tensor.matmul(c.bank[:, 6 + half, (t % 2) * D:(t % 2 + 1) * D],
                                                    attnT[:, k, t * P:(t + 1) * P], held["wo"][:, k, :],
                                                    start=("bo" not in loads and k == 0), stop=(k == KD - 1),
                                                    skip_group_check=True)
                    last.then_inc(y_filled.sem, 1)

        def copy_pT(eng, b, n):
            g, j, i = head_of(n)
            eng.wait_ge(t_filled.sem, t_filled.at(b, n + 1))
            out = pT[:, g % 2, j, 0:i + 1, i * P:(i + 1) * P]
            bank = c.bank[:, 4 + n % 2, 0:(i + 1) * P].rearrange("p (k q) -> p k q", q=P)
            if two:
                nc.scalar.copy(out, bank).then_inc(pt_ready.sem, 1)
            else:
                nc.vector.tensor_copy(out, bank).then_inc(pt_ready.sem, 1)

        @block.scalar
        def _(act):
            def drain(b, s):
                what, part = plan[s]
                act.wait_ge(rows_filled.sem, rows_filled.at(b, s + 1))
                bank = c.bank[:, bank_of(s), :]
                if what.endswith("stack"):
                    out = stack[what.split()[0]][:, part, :]
                    if what in HALVED:
                        return nc.scalar.activation(out, bank, ACT.Copy, scale=0.5)
                    return nc.scalar.copy(out, bank)
                rows = {"q": q_rows, "k": k_rows, "v": v_rows}[what]
                return nc.scalar.copy(rows[:, 2 * part:2 * part + 2, :, 0:DH1],
                                      bank.rearrange("p (t h d) -> p t h d", t=2, d=DH1))

            def exponentials(b, n):
                width = (n % NT + 1) * P
                for m in range(1 + two):
                    act.wait_ge(max_ready[m].sem, max_ready[m].at(b, n + 1))
                    nc.scalar.activation(probs[m][:, n % 3, 0:width], c.bank[:, 2 * m + n % 2, 0:width], ACT.Exp,
                                         bias=neg_max[m][:, n:n + 1],
                                         accum_out=total[m][:, n:n + 1]).then_inc(exp_done[m].sem, 1)

            if kind == "differential":
                act.wait_ge(sums_ready.sem, sums_ready.at(0, 1))
                nc.scalar.activation(small[:, 2:4], small[:, 0:2], ACT.Exp).then_inc(setup_exp.sem, 1)
            if kind == "splat":
                act.wait_ge(loaded["logs"].sem, loaded["logs"].at(0, 16))
                act.wait_ge(loaded["scal"].sem, loaded["scal"].at(0, 16))
                logs = held["logs"]
                nc.scalar.activation(logs[:, 0, :], logs[:, 0, :], ACT.Exp, scale=-2.0)
                nc.scalar.activation(logs[:, 1, :], logs[:, 1, :], ACT.Exp)
                nc.scalar.activation(small[:, 0:1], held["scal"][:, 2:3], ACT.Exp, scale=-1.0)
                act.wait_ge(sums_ready.sem, sums_ready.at(0, 1))
                nc.scalar.activation(inv_norm[:, :], inv_norm[:, :], ACT.Sqrt).then_inc(setup_exp.sem, 1)
            with act.Fori(0, B) as b:
                norm.scalar(act, b, (0, 1))
                for s in range(len(plan)):
                    if plan[s] in (("qf", 1), ("kf", 1)):
                        f = 0 if plan[s][0] == "qf" else 1
                        act.wait_ge(args_ready.sem, args_ready.at(b, f + 1))
                        nc.scalar.activation(gauss[:, :, :, :], gauss[:, :, :, :], ACT.Exp)
                        nc.scalar.activation(tilt[:, :, :, :], tilt[:, :, :, :], ACT.Tanh).then_inc(features.sem, 1)
                    if owner[s] == "scalar":
                        drain(b, s).then_inc(drained["scalar"].sem, 1)
                for n in range(cells + 6):
                    if n < cells:
                        exponentials(b, n)
                    if 2 <= n < cells + 2 and two:
                        copy_pT(act, b, n - 2)
                    if n % group_cells == 3 and n > 3:
                        g = n // group_cells - 1
                        act.wait_ge(ov_filled.sem, ov_filled.at(b, g + 1))
                        nc.scalar.copy(ovT[:, :], c.bank[:, OV, :]).then_inc(ov_ready.sem, 1)
                for k in range(KD):
                    act.wait_ge(ot_filled.sem, ot_filled.at(b, k + 1))
                    nc.scalar.copy(attnT[:, k, :], c.bank[:, 4 + k, :]).then_inc(ot_ready.sem, 1)

        @block.vector
        def _(dve):
            link = lambda ins: chain.link(dve, ins)

            def setup_differential():
                for n in ("bq", "bk", "bv", "lam", "gsub"):
                    dve.wait_ge(loaded[n].sem, loaded[n].at(0, 16))
                lam = held["lam"]
                nc.vector.tensor_tensor(lam[:, 0, :], lam[:, 0, :], lam[:, 1, :], ALU.mult)
                link(nc.vector.tensor_tensor(lam[:, 2, :], lam[:, 2, :], lam[:, 3, :], ALU.mult))
                nc.vector.reduce_sum(small[:, 0:1], lam[:, 0, :], axis=AX.X)
                nc.vector.reduce_sum(small[:, 1:2], lam[:, 2, :], axis=AX.X).then_inc(sums_ready.sem, 1)
                nc.vector.tensor_scalar_mul(held["bq"][:, :], held["bq"][:, :], SCALE_DIFF)
                nc.vector.tensor_scalar_mul(held["gsub"][:, :], held["gsub"][:, :], 1.0 - LAMBDA_INIT)
                dve.wait_ge(setup_exp.sem, setup_exp.at(0, 1))
                link(nc.vector.tensor_tensor(small[:, 4:5], small[:, 3:4], small[:, 2:3], ALU.subtract))
                link(nc.vector.tensor_scalar_add(small[:, 5:6], small[:, 4:5], -LAMBDA_INIT))

            def setup_splat():
                for n in ("pos", "dir"):
                    dve.wait_ge(loaded[n].sem, loaded[n].at(0, 16))
                by_splat = work.rearrange("p (s d) -> p s d", d=DH1)
                link(nc.vector.tensor_tensor(work, raw_pos, raw_pos, ALU.mult))
                link(nc.vector.reduce_sum(half_p2[:, :], by_splat, axis=AX.X))
                link(nc.vector.tensor_scalar_mul(half_p2[:, :], half_p2[:, :], 0.5))
                link(nc.vector.tensor_tensor(work, raw_pos, raw_dir, ALU.mult))
                link(nc.vector.reduce_sum(p_dir[:, :], by_splat, axis=AX.X))
                link(nc.vector.tensor_tensor(work, raw_dir, raw_dir, ALU.mult))
                nc.vector.reduce_sum(inv_norm[:, :], by_splat, axis=AX.X).then_inc(sums_ready.sem, 1)
                dve.wait_ge(setup_exp.sem, setup_exp.at(0, 1))
                link(nc.vector.tensor_scalar_add(inv_norm[:, :], inv_norm[:, :], 1e-8))
                for n in ("blocks", "masks"):
                    dve.wait_ge(loaded[n].sem, loaded[n].at(0, 16))
                whole, masks = held["blocks"], held["masks"]
                rounded, left, rounded2, left2, total_of = (block_steps[:, i, :] for i in range(5))
                narrow = block_parts[:, :, :, :].rearrange("p s h n -> p s (h n)")
                link(nc.vector.tensor_copy(narrow[:, 0, :], whole[:, :]))
                link(nc.vector.tensor_copy(rounded, narrow[:, 0, :]))
                link(nc.vector.tensor_tensor(left, whole[:, :], rounded, ALU.subtract))
                link(nc.vector.tensor_copy(narrow[:, 0, :], left))
                link(nc.vector.tensor_copy(rounded2, narrow[:, 0, :]))
                link(nc.vector.tensor_tensor(left2, left, rounded2, ALU.subtract))
                for side in range(2):
                    mask = lambda i: masks[:, 3 * side + i:3 * side + i + 1]
                    link(nc.vector.tensor_scalar(total_of, rounded, mask(0), None, ALU.mult))
                    link(nc.vector.scalar_tensor_tensor(total_of, rounded2, mask(1), total_of, ALU.mult, ALU.add))
                    last = nc.vector.scalar_tensor_tensor(narrow[:, side, :], left2, mask(2), total_of, ALU.mult, ALU.add)
                    link(last)
                nc.vector.memset(c.wait_mark[:, :], 0.0).then_inc(blocks_ready.sem, 1)
                nc.vector.reciprocal(inv_norm[:, :], inv_norm[:, :])
                nc.vector.tensor_scalar(held["logs"][:, 1, :], held["logs"][:, 1, :], held["scal"][:, 1:2], None, ALU.mult)
                link(nc.vector.tensor_scalar_add(small[:, 1:2], small[:, 0:1], 1.0))
                link(nc.vector.reciprocal(small[:, 2:3], small[:, 1:2]))
                link(nc.vector.tensor_scalar(small[:, 3:4], small[:, 2:3], 0.15, 0.03, ALU.mult, ALU.min))
                link(nc.vector.tensor_scalar(small[:, 4:5], small[:, 3:4], -1.0, 1.0, ALU.mult, ALU.add))
                link(nc.vector.reciprocal(small[:, 6:7], small[:, 4:5]))
                link(nc.vector.tensor_tensor(small[:, 5:6], small[:, 6:7], small[:, 3:4], ALU.mult))

            def drain_biased(what, part, bank):
                rows = {"q": q_rows, "k": k_rows, "v": v_rows}[what]
                width, d = {"q": (QH, DH1), "k": (KH, dk), "v": (VH, DH1)}[what]
                n = 512 // width
                out = rows[:, n * part:n * (part + 1), :, 0:d]
                src = bank.rearrange("p (t h d) -> p t h d", t=n, d=d)
                bias = held["b" + what][:, :].rearrange("p (a h d) -> p a h d", a=1, d=d).broadcast_to([P, n, width // d, d])
                if what == "q":
                    for t in range(n):
                        last = nc.vector.scalar_tensor_tensor(out[:, t], src[:, t], SCALE_DIFF, bias[:, t], ALU.mult, ALU.add)
                    return last
                return nc.vector.tensor_tensor(out, src, bias, ALU.add)

            def drain_rotated(b, what, part, bank):
                rows = {"q": q_rows, "k": k_rows}[what]
                cos = held["cos"][:, "qk".index(what), 2 * part:2 * part + 2, :]
                sin = held["sin"][:, "qk".index(what), 2 * part:2 * part + 2, :]
                before = {"q": 0, "k": 2}[what] + part
                if before:
                    dve.wait_ge(drained["vector"].sem, drained["vector"].at(b, before))
                pairs = bank.rearrange("p (t h d e) -> p t h d e", t=2, d=DH1 // 2, e=2)
                wide = lambda a: a.rearrange("p t (a d) -> p t a d", a=1).broadcast_to([P, 2, H1, DH1 // 2])
                even, odd = pairs[:, :, :, :, 0], pairs[:, :, :, :, 1]
                for t in range(2):
                    sub = lambda a: a[:, t]
                    nc.vector.tensor_tensor(turned[0][:, t, :, 0:8], sub(even), sub(wide(cos)), ALU.mult)
                    nc.vector.tensor_tensor(turned[0][:, t, :, 8:16], sub(even), sub(wide(sin)), ALU.mult)
                    nc.vector.tensor_tensor(turned[1][:, t, :, 0:8], sub(odd), sub(wide(sin)), ALU.mult)
                    last = nc.vector.tensor_tensor(turned[1][:, t, :, 8:16], sub(odd), sub(wide(cos)), ALU.mult)
                link(last)
                out = rows[:, 2 * part:2 * part + 2, :, 0:DH1].rearrange("p t h (d e) -> p t h d e", e=2)
                nc.vector.tensor_tensor(out[:, :, :, :, 0], turned[0][:, :, :, 0:8], turned[1][:, :, :, 0:8], ALU.subtract)
                return nc.vector.tensor_tensor(out[:, :, :, :, 1], turned[0][:, :, :, 8:16], turned[1][:, :, :, 8:16], ALU.add)

            def splat_features(b, what, s):
                rows, feature = {"qf": (q_rows, qf_rows), "kf": (k_rows, kf_rows)}[what]
                flat = lambda a: a.rearrange("p t h n -> p (t h) n")
                values = flat(rows)
                link(nc.vector.tensor_tensor(square, values, values, ALU.mult))
                link(nc.vector.reduce_sum(half_q2[:, :], square, axis=AX.X))
                link(nc.vector.tensor_scalar_mul(half_q2[:, :], half_q2[:, :], 0.5))
                dve.wait_ge(rows_filled.sem, rows_filled.at(b, s + 1))
                first = bank_of(s) - 1
                products = c.bank[:, first:first + 2, :].rearrange("p a (u n) -> p (a u) n", n=16)
                nc.vector.tensor_tensor(flat(gauss), products[:, :, 0:8], half_q2[:, :].rearrange("p (u a) -> p u a", a=1)
                                        .broadcast_to([P, NT * H1, 8]), ALU.subtract)
                per_splat = lambda a: a.rearrange("p (a h n) -> p a h n", a=1, n=8).broadcast_to([P, NT, H1, 8])
                nc.vector.tensor_copy(flat(tilt), products[:, :, 8:16]).then_inc(drained["vector"].sem, 2)
                dve.wait_ge(drained["vector"].sem, drained["vector"].at(b, drains_up_to(s, "vector")))
                link(nc.vector.tensor_tensor(gauss[:, :, :, :], gauss[:, :, :, :], per_splat(half_p2[:, :]), ALU.subtract))
                link(nc.vector.tensor_tensor(tilt[:, :, :, :], tilt[:, :, :, :], per_splat(p_dir[:, :]), ALU.subtract))
                nc.vector.tensor_tensor(gauss[:, :, :, :], gauss[:, :, :, :], per_splat(held["logs"][:, 0, :]), ALU.mult)
                nc.vector.tensor_tensor(tilt[:, :, :, :], tilt[:, :, :, :], per_splat(inv_norm[:, :]),
                                        ALU.mult).then_inc(args_ready.sem, 1)
                f = 0 if what == "qf" else 1
                dve.wait_ge(features.sem, features.at(b, f + 1))
                near, toward = feature[:, :, :, 0:8], feature[:, :, :, 8:16]
                if what == "qf":
                    link(nc.vector.tensor_tensor(near, gauss[:, :, :, :], per_splat(held["logs"][:, 1, :]), ALU.mult))
                    link(nc.vector.scalar_tensor_tensor(flat(toward), flat(near), held["scal"][:, 0:1],
                                                        flat(tilt), ALU.mult, ALU.mult))
                else:
                    nc.vector.tensor_copy(near, gauss[:, :, :, :])
                    link(nc.vector.tensor_tensor(toward, gauss[:, :, :, :], tilt[:, :, :, :], ALU.mult))

            def split(b, what, source):
                side = what[0]
                d = dk if side == "k" else DH1
                if splits.index(what):
                    dve.wait_ge(split_ready.sem, split_ready.at(b, splits.index(what)))
                source = source.rearrange("p t h d -> p (t h) d")
                compact = lambda a: a[:, 0:NT * H1 * d].rearrange("p (u d) -> p u d", d=d)
                left, (high, middle, low) = compact(rest), map(compact, part_of)
                link(nc.vector.tensor_copy(high, source))
                link(nc.vector.tensor_tensor(left, source, high, ALU.subtract))
                link(nc.vector.tensor_copy(middle, left))
                link(nc.vector.tensor_tensor(low, left, middle, ALU.subtract))
                at = PAD if side == "k" else 0
                places = parts[side][:, :, :, at:at + P].rearrange("p t h (c d) -> p (t h) c d", d=DH1)
                for i, part in enumerate((high, middle, low)):
                    for place in [n for n in range(8) if (n % 3 if side == "k" else n // 3) == i]:
                        last = nc.vector.tensor_copy(places[:, :, place, 0:d], part)
                last.then_inc(split_ready.sem, 1)

            def drain(b, s):
                what, part = plan[s]
                dve.wait_ge(rows_filled.sem, rows_filled.at(b, s + 1))
                bank = c.bank[:, bank_of(s), :]
                if what.endswith("stack"):
                    out = stack[what.split()[0]][:, part, :]
                    if what in HALVED:
                        return nc.vector.tensor_scalar(out, bank, 0.5, None, ALU.mult)
                    return nc.vector.tensor_copy(out, bank)
                return drain_rotated(b, what, part, bank) if kind == "rope" else drain_biased(what, part, bank)

            def maximum(b, n, m):
                dve.wait_ge(s_filled[m].sem, s_filled[m].at(b, n + 1))
                nc.vector.tensor_reduce(neg_max[m][:, n:n + 1], c.bank[:, 2 * m + n % 2, 0:(n % NT + 1) * P],
                                        axis=AX.X, op=ALU.max, negate=True).then_inc(max_ready[m].sem, 1)

            def invert(b, n):
                dve.wait_ge(exp_done[1].sem, exp_done[1].at(b, n + 1))
                nc.vector.reciprocal(inv[:, n:n + 1], total[1][:, n:n + 1]).then_inc(inv_ready.sem, 1)

            def weigh(b, n):
                dve.wait_ge(inv_ready.sem, inv_ready.at(b, n + 1))
                nc.vector.tensor_scalar(weight[:, n:n + 1], inv[:, n:n + 1], total[0][:, n:n + 1], small[:, 5:6],
                                        ALU.mult, ALU.mult).then_inc(weight_ready.sem, 1)

            def mix(b, n):
                dve.wait_ge(weight_ready.sem, weight_ready.at(b, n + 1))
                p0, p1 = (probs[m][:, n % 3, 0:(n % NT + 1) * P] for m in range(2))
                nc.vector.scalar_tensor_tensor(p0, p1, weight[:, n:n + 1], p0, ALU.mult, ALU.add).then_inc(p_ready.sem, 1)

            def finish_group(b, g):
                cols = slice(g * group_cells, (g + 1) * group_cells)
                link(nc.vector.reciprocal(row_inv[:, :], total[0][:, cols]))
                if kind == "splat":
                    link(nc.vector.tensor_scalar(row_inv[:, :], row_inv[:, :], small[:, 4:5], None, ALU.mult))
                dve.wait_ge(or_filled.sem, or_filled.at(b, g + 1))
                out = attn[:, :, g * HG * DH1:(g + 1) * HG * DH1].rearrange("p t (h d) -> p t h d", d=DH1)
                rows = c.bank[:, OR, :].rearrange("p (t h d) -> p t h d", t=NT, d=STRIP)[:, :, :, 0:DH1]
                scale = row_inv[:, :].rearrange("p (h t a) -> p t h a", t=NT, a=1).broadcast_to([P, NT, HG, DH1])
                nc.vector.tensor_tensor(out, rows, scale, ALU.mult).then_inc(or_read.sem, 1)
                if kind != "differential":
                    return
                dve.wait_ge(or_read.sem, or_read.at(b, g + 1))
                link(nc.vector.tensor_tensor(square[:, :, :, :], out, out, ALU.mult))
                link(nc.vector.tensor_reduce(mean_sq[:, :, :], square[:, :, :, :], axis=AX.X, op=ALU.add))
                nc.vector.tensor_scalar(mean_sq[:, :, :], mean_sq[:, :, :], 1.0 / DH1, RMS_EPS,
                                        ALU.mult, ALU.add).then_inc(square_ready.sem, 1)
                for_each = held["gsub"][:, :].rearrange("p (a d) -> p a d", a=1).broadcast_to([P, HG, DH1])
                for t in range(NT):
                    last = nc.vector.tensor_tensor(out[:, t], out[:, t], for_each, ALU.mult)
                link(last)
                dve.wait_ge(rms_ready.sem, rms_ready.at(b, g + 1))
                nc.vector.tensor_tensor(out, out, rms[:, :, :].rearrange("p t (h a) -> p t h a", a=1)
                                        .broadcast_to([P, NT, HG, DH1]), ALU.mult).then_inc(group_done.sem, 1)

            nc.vector.memset((parts["k"] if PAD else c.wait_mark)[:], 0.0).then_inc(zeroed.sem, 1)
            nc.vector.memset(v_rows[:, :, :, :], 0.0).then_inc(zeroed.sem, 1)
            dve.wait_ge(zeroed.sem, zeroed.at(0, 2))
            if kind == "differential":
                setup_differential()
            elif kind == "splat":
                setup_splat()
            else:
                for n in ("cos", "sin"):
                    dve.wait_ge(loaded[n].sem, loaded[n].at(0, 16))
            chain.begin_loop(dve)
            with dve.Fori(0, B) as b:
                chain.turn(b)
                norm.vector(dve, b, lambda t: c.x_cols(b, t * D, D), lambda t: c.xn[:, t, :])
                for s in range(len(plan)):
                    what, part = plan[s]
                    if what in ("qf", "kf"):
                        if part == 1:
                            splat_features(b, what, s)
                            split(b, what, {"qf": qf_rows, "kf": kf_rows}[what])
                    elif owner[s] == "vector":
                        drain(b, s).then_inc(drained["vector"].sem, 1)
                    if what in ("q", "k") and plan[s + 1][0] != what:
                        dve.wait_ge(drained[owner[s]].sem, drained[owner[s]].at(b, drains_up_to(s, owner[s])))
                        split(b, what, {"q": q_rows, "k": k_rows}[what])
                for n in range(cells + 6):
                    if n < cells:
                        maximum(b, n, 0)
                    if two and 1 <= n < cells + 1:
                        invert(b, n - 1)
                    if two and n < cells:
                        maximum(b, n, 1)
                    if two and 1 <= n < cells + 1:
                        weigh(b, n - 1)
                        mix(b, n - 1)
                    if 2 <= n < cells + 2 and not two:
                        copy_pT(dve, b, n - 2)
                    if n % group_cells == 5 and n > 5:
                        finish_group(b, n // group_cells - 1)
                for half in range(2):
                    dve.wait_ge(y_filled.sem, y_filled.at(b, half + 1))
                    xs = c.x_cols(b, half * 512, 512)
                    last = nc.vector.tensor_tensor(xs, xs, c.bank[:, 6 + half, :], ALU.add)
                link(last)
                chain.top_up(dve)

        @block.gpsimd
        def _(pool):
            with pool.Fori(0, B) as b:
                norm.pool(pool, b)
                if kind == "differential":
                    for g in range(NG):
                        pool.wait_ge(square_ready.sem, square_ready.at(b, g + 1))
                        flat = lambda a: a[:, :, :].rearrange("p t h -> p (t h)")
                        nc.gpsimd.tensor_tensor(flat(rms), flat(mean_sq), c.minus_half[:, 0:group_cells],
                                                ALU.pow).then_inc(rms_ready.sem, 1)
    norm.end()
    chain.end(B)
    for s in (*loaded.values(), zeroed):
        s.end(1)
    split_ready.end(B)
    if kind == "splat":
        blocks_ready.end(1)
    if two:
        sums_ready.end(1)
        setup_exp.end(1)
    if kind == "splat":
        for s in (args_ready, features):
            s.end(B)
    if kind == "differential":
        for s in (square_ready, rms_ready):
            s.end(B)
    for s in (s_filled[1], max_ready[1], exp_done[1], inv_ready, weight_ready, p_ready):
        if two:
            s.end(B)
    for s in (rows_filled, *drained.values(), s_filled[0], max_ready[0], exp_done[0], t_filled, pt_ready,
              ov_filled, ov_ready, or_filled, or_read, group_done, ot_filled, ot_ready, y_filled):
        s.end(B)


E_ALL, F, K, R, TOPK = 64, 8, 8, 8, 6
I = 176
KR = K * R
TAIL = I - P
UP = 2 * I
AT = {}
for _name, _width in (("w1", KD * (UP + 2 * KR)), ("qb", UP), ("qb_scale", UP), ("mu", D), ("down", D + KR),
                      ("qa_tail", KR), ("low", D), ("low_scale", D)):
    AT[_name] = sum(w for _, w in AT.values()), _width
PACK_E = sum(w for _, w in AT.values())


def build_moe(c, ins):
    nc = c.nc
    norm = Norm(c)
    units = 2 * B
    turns = F // 2 + 1
    loaded = {n: c.counter(f"moe_loaded_{i}", 16) for i, n in enumerate(("gate", "map"))}
    w_loaded = [c.counter(f"moe_w_loaded{p}", 16) for p in range(2)]
    chain = Chain(c, "moe_chain")
    index_ready = c.counter("moe_index_ready", 1)
    pick_ready = c.counter("moe_pick_ready", 1)
    logits_filled = c.counter("moe_logits_filled", 1)
    arg_ready = c.counter("moe_arg_ready", 2)
    exp_done = c.counter("moe_exp_done", 2)
    dense_ready = c.counter("moe_dense_ready", 1)
    denseT_filled = c.counter("moe_denseT_filled", 1)
    denseT_ready = c.counter("moe_denseT_ready", 1)
    flat_filled = c.counter("moe_flat_filled", 1)
    soft_ready = c.counter("moe_soft_ready", 1)
    softT_filled = c.counter("moe_softT_filled", 1)
    routed_done = c.counter("moe_routed_done", 1)
    scaled = c.counter("moe_scaled", 2)
    sig = {n: c.counter(f"moe_{n}", per * units, credit=int(n == "y_added")) for n, per in (
        ("xe_filled", 1), ("xe_ready", 1), ("a_filled", 1), ("aw_ready", 1), ("aT_filled", 1), ("aT_ready", 1),
        ("gu_filled", NT), ("silu_done", NT), ("h_ready", NT), ("hT_filled", 1), ("hT_ready", 1),
        ("a2_filled", 1), ("aw2_ready", 1), ("tailT_filled", 1), ("tailT_ready", 1), ("y_filled", 1), ("y_added", 1))}
    XB, AB, TB, GB, HB = 0, 2, 3, 4, 6
    with ExitStack() as ctx:
        sb = lambda name, shape, dt=F32: c.sb(f"moe_{name}", shape, dt, ctx=ctx)
        w = sb("w", [P, 2, PACK_E])
        gate = sb("gate", [P, KD, E_ALL])
        mapping = sb("mapping", [E_ALL, E_ALL], I32)
        entry = sb("entry", [E_ALL, E_ALL])
        negative = sb("negative", [E_ALL, E_ALL])
        index = sb("index", [E_ALL, 1], I32)
        index_f = sb("index_f", [E_ALL, 1])
        pick = sb("pick", [E_ALL, E_ALL])
        xT = sb("xT", [P, KD, B * T])
        soft = sb("soft", [P, B * NT, E_ALL])
        share = sb("share", [P, B * NT, F])
        softT = sb("softT", [E_ALL, B * T])
        score = sb("score", [P, NT, E_ALL + 2])
        rest = sb("rest", [P, NT, E_ALL + 2])
        dense = sb("dense", [P, NT, E_ALL])
        denseT = sb("denseT", [E_ALL, T])
        row = sb("row", [P, NT * F])
        row2 = sb("row2", [P, NT * F])
        top8 = sb("top8", [P, NT, 8])
        xeT = sb("xeT", [P, 2, KD, T])
        aw = sb("aw", [P, NT, 2 * KR])
        awT = sb("awT", [P, 2, T])
        silu = sb("silu", [P, NT, I])
        inner = sb("inner", [P, 2, NT, KR + I])
        hT = sb("hT", [P, 2, T])
        hT_tail = sb("hT_tail", [TAIL, 2, T])
        tailT = sb("tailT", [KR + TAIL, 2, T])
        block = ctx.enter_context(nc.Block())

        def cols(slot, name, rows=P, start=0, n=None):
            at, width = AT[name]
            return w[0:rows, slot, at + start:at + (width if n is None else start + n)]

        def unit_of(u):
            return u // B, u % B

        @block.sync
        def _(sp):
            sp.dma_start(gate[:, :, :], ins["moe_gate"]).then_inc(loaded["gate"].sem, 16)
            sp.dma_start(mapping[:, :], ins["moe_map"]).then_inc(loaded["map"].sem, 16)
            for slot in range(2):
                sp.dma_start(w[:, slot, :], ins["moe_w"][slot]).then_inc(w_loaded[slot].sem, 16)
            with sp.Fori(1, turns) as turn:
                for slot in range(2):
                    expert = sp.snap(turn * 2 + slot)
                    y = sig["y_filled"]
                    sp.wait_ge(y.sem, y.at(turn, -units + (slot + 1) * B))
                    sp.dma_start(w[:, slot, :], ins["moe_w"][bass.ds(expert, 1)].rearrange("a p n -> p (a n)"))\
                      .then_inc(w_loaded[slot].sem, 16)

        @block.gpsimd
        def _(pool):
            nc.gpsimd.iota(index[:, :], pattern=[[0, 1]], base=0, channel_multiplier=1).then_inc(index_ready.sem, 1)
            with pool.Fori(0, B) as b:
                norm.pool(pool, b)

        @block.tensor
        def _(pe):
            def route(b):
                pe.wait_ge(norm.xn_ready.sem, norm.xn_ready.at(b, NT))
                norm.tensor(pe, (0, 1))
                pe.wait_ge(norm.xT_ready.sem, norm.xT_ready.at(b, KD))
                for t in range(NT):
                    for k in range(KD):
                        last = nc.tensor.matmul(c.bank[:, 2, t * E_ALL:(t + 1) * E_ALL], c.xnT[:, k, t * P:(t + 1) * P],
                                                gate[:, k, :], start=(k == 0), stop=(k == KD - 1))
                last.then_inc(logits_filled.sem, 1)
                pe.wait_ge(dense_ready.sem, dense_ready.at(b, 1))
                for t in range(NT):
                    last = nc.tensor.matmul(c.bank[0:E_ALL, 3, t * P:(t + 1) * P], dense[:, t, :], c.ident[:, :],
                                            start=True, stop=True)
                last.then_inc(denseT_filled.sem, 1)
                pe.wait_ge(denseT_ready.sem, denseT_ready.at(b, 1))
                for t in range(NT):
                    last = nc.tensor.matmul(c.bank[:, 2, t * E_ALL:(t + 1) * E_ALL], denseT[:, t * P:(t + 1) * P],
                                            pick[:, :], start=True, stop=True)
                last.then_inc(flat_filled.sem, 1)
                pe.wait_ge(soft_ready.sem, soft_ready.at(b, 1))
                for t in range(NT):
                    last = nc.tensor.matmul(c.bank[0:E_ALL, 3, t * P:(t + 1) * P], dense[:, t, :], c.ident[:, :],
                                            start=True, stop=True)
                last.then_inc(softT_filled.sem, 1)

            def experts(turn, routed):
                def wait(name, u, n=1, per=1):
                    pe.wait_ge(sig[name].sem, sig[name].at(turn, u * per + n))

                def expert_input(u):
                    slot, b = unit_of(u)
                    if b == 0:
                        pe.wait_ge(w_loaded[slot].sem, w_loaded[slot].at(turn, 16))
                    if u == 0 or u >= 3:
                        wait("y_added", max(u - 3, 0), int(u > 0))
                    for k in range(KD):
                        last = nc.tensor.matmul(c.bank[:, XB + k, :], cols(slot, "mu", E_ALL, k * P, P),
                                                softT[:, b * T:(b + 1) * T], start=True, stop=True)
                    last.then_inc(sig["xe_filled"].sem, 1)

                def low_rank_in(u):
                    slot, b = unit_of(u)
                    wait("xe_ready", u)
                    if u >= 2:
                        wait("aw2_ready", u - 2)
                    for t in range(NT):
                        for k in range(KD):
                            last = nc.tensor.matmul(c.bank[:, AB, t * P:(t + 1) * P], xeT[:, u % 2, k, t * P:(t + 1) * P],
                                                    cols(slot, "w1", P, k * (UP + 2 * KR) + UP, 2 * KR),
                                                    start=(k == 0), stop=(k == KD - 1))
                    last.then_inc(sig["a_filled"].sem, 1)

                def transpose_in(u):
                    wait("aw_ready", u)
                    if u >= 2:
                        wait("tailT_ready", u - 2)
                    for t in range(NT):
                        last = nc.tensor.transpose(c.bank[:, TB, t * P:(t + 1) * P], aw[:, t, :], c.ident[:, :])
                    last.then_inc(sig["aT_filled"].sem, 1)

                def gate_up(u, t):
                    slot, b = unit_of(u)
                    if t == 0:
                        if routed:
                            if b == 0:
                                pe.wait_ge(scaled.sem, scaled.at(turn, slot + 1))
                            wait("aT_ready", u)
                        elif b == 0:
                            pe.wait_ge(w_loaded[slot].sem, w_loaded[slot].at(turn, 16))
                    if u * NT + t >= 2:
                        wait("h_ready", u * NT + t - 2)
                    out = c.bank[:, GB + t % 2, 0:UP]
                    for k in range(KD):
                        x = xeT[:, u % 2, k, t * P:(t + 1) * P] if routed else xT[:, k, b * T + t * P:b * T + (t + 1) * P]
                        last = nc.tensor.matmul(out, x, cols(slot, "w1", P, k * (UP + 2 * KR), UP),
                                                start=(k == 0), stop=(not routed and k == KD - 1))
                    if routed:
                        last = nc.tensor.matmul(out, awT[:, u % 2, t * P:(t + 1) * P], cols(slot, "qb"),
                                                start=False, stop=True)
                    last.then_inc(sig["gu_filled"].sem, 1)

                def transpose_h(u):
                    for t in range(NT):
                        wait("h_ready", u, t + 1, NT)
                        h = inner[:, u % 2, t, KR:KR + I]
                        nc.tensor.transpose(c.bank[:, HB, t * P:(t + 1) * P], h[:, TAIL:I], c.ident[:, :])
                        last = nc.tensor.transpose(c.bank[0:TAIL, HB + 1, t * P:(t + 1) * P], h[:, 0:TAIL], c.ident[:, :])
                    last.then_inc(sig["hT_filled"].sem, 1)

                def low_rank_down(u):
                    slot, b = unit_of(u)
                    wait("hT_ready", u)
                    for t in range(NT):
                        out = c.bank[:, AB, t * KR:(t + 1) * KR]
                        nc.tensor.matmul(out, hT[:, u % 2, t * P:(t + 1) * P], cols(slot, "down", P, D, KR),
                                         start=True, stop=False)
                        last = nc.tensor.matmul(out, hT_tail[:, u % 2, t * P:(t + 1) * P], cols(slot, "qa_tail", TAIL),
                                                start=False, stop=True)
                    last.then_inc(sig["a2_filled"].sem, 1)

                def transpose_tail(u):
                    wait("aw2_ready", u)
                    for t in range(NT):
                        last = nc.tensor.transpose(c.bank[0:KR + TAIL, TB, t * P:(t + 1) * P],
                                                   inner[:, u % 2, t, 0:KR + TAIL], c.ident[:, :])
                    last.then_inc(sig["tailT_filled"].sem, 1)

                def output(u):
                    slot, b = unit_of(u)
                    wait("tailT_ready" if routed else "hT_ready", u)
                    if not routed or u >= units - 2:
                        wait("y_added", u, 0)
                    for t in range(NT):
                        out = c.bank[:, XB + t // 2, (t % 2) * D:(t % 2 + 1) * D]
                        nc.tensor.matmul(out, hT[:, u % 2, t * P:(t + 1) * P], cols(slot, "down", P, 0, D),
                                         start=True, stop=False)
                        if routed:
                            last = nc.tensor.matmul(out, tailT[:, u % 2, t * P:(t + 1) * P],
                                                    cols(slot, "low", KR + TAIL), start=False, stop=True)
                        else:
                            last = nc.tensor.matmul(out, hT_tail[:, u % 2, t * P:(t + 1) * P],
                                                    cols(slot, "low", TAIL), start=False, stop=True)
                    last.then_inc(sig["y_filled"].sem, 1)

                if routed:
                    expert_input(0)
                    low_rank_in(0)
                    transpose_in(0)
                for u in range(units + 1):
                    if u < units:
                        gate_up(u, 0)
                        if routed and u + 1 < units:
                            expert_input(u + 1)
                    if routed and u:
                        low_rank_down(u - 1)
                    if u < units:
                        gate_up(u, 1)
                        if routed and u + 1 < units:
                            low_rank_in(u + 1)
                    if routed and u:
                        transpose_tail(u - 1)
                    if u < units:
                        gate_up(u, 2)
                        if routed and u + 1 < units:
                            transpose_in(u + 1)
                        gate_up(u, 3)
                    if u:
                        output(u - 1)
                    if u < units:
                        transpose_h(u)

            pe.wait_ge(loaded["gate"].sem, loaded["gate"].at(0, 16))
            pe.wait_ge(pick_ready.sem, pick_ready.at(0, 1))
            with pe.Fori(0, B) as b:
                route(b)
            pe.wait_ge(routed_done.sem, routed_done.at(B - 1, 1))
            with pe.Fori(0, turns - 1) as turn:
                experts(turn, True)
            experts(turns - 1, False)

        @block.scalar
        def _(act):
            with act.Fori(0, B) as b:
                norm.scalar(act, b, (0, 1))
                act.wait_ge(arg_ready.sem, arg_ready.at(b, 1))
                nc.scalar.activation(score[:, :, 0:E_ALL], score[:, :, 0:E_ALL], ACT.Exp).then_inc(exp_done.sem, 1)
                act.wait_ge(denseT_filled.sem, denseT_filled.at(b, 1))
                nc.scalar.copy(denseT[:, :], c.bank[0:E_ALL, 3, :]).then_inc(denseT_ready.sem, 1)
                act.wait_ge(arg_ready.sem, arg_ready.at(b, 2))
                nc.scalar.activation(dense[:, :, :], dense[:, :, :], ACT.Exp).then_inc(exp_done.sem, 1)

            def experts(turn, routed):
                def wait(name, u, n=1, per=1):
                    act.wait_ge(sig[name].sem, sig[name].at(turn, u * per + n))

                def apply_silu(u, t):
                    wait("gu_filled", u, t + 1, NT)
                    nc.scalar.activation(silu[:, t, :], c.bank[:, GB + t % 2, 0:I], ACT.Silu).then_inc(sig["silu_done"].sem, 1)

                for u in range(-1, units + 1):
                    if 0 <= u < units:
                        apply_silu(u, 0)
                        apply_silu(u, 1)
                    if routed and u >= 1:
                        wait("tailT_filled", u - 1)
                        nc.scalar.copy(tailT[:, (u - 1) % 2, :], c.bank[0:KR + TAIL, TB, :]).then_inc(sig["tailT_ready"].sem, 1)
                    if 0 <= u < units:
                        apply_silu(u, 2)
                    if routed and u + 1 < units:
                        wait("aT_filled", u + 1)
                        nc.scalar.copy(awT[:, (u + 1) % 2, :], c.bank[:, TB, :]).then_inc(sig["aT_ready"].sem, 1)
                    if 0 <= u < units:
                        apply_silu(u, 3)
                        wait("hT_filled", u)
                        nc.scalar.copy(hT[:, u % 2, :], c.bank[:, HB, :])
                        nc.scalar.copy(hT_tail[:, u % 2, :], c.bank[0:TAIL, HB + 1, :]).then_inc(sig["hT_ready"].sem, 1)

            with act.Fori(0, turns - 1) as turn:
                experts(turn, True)
            experts(turns - 1, False)

        @block.vector
        def _(dve):
            link = lambda ins: chain.link(dve, ins)
            wide = lambda a, n: a.rearrange("p (u a) -> p u a", a=1).broadcast_to([a.shape[0], a.shape[1], n])

            def route(b):
                norm.vector(dve, b, lambda t: c.x_cols(b, t * D, D), lambda t: c.xn[:, t, :])
                dve.wait_ge(norm.xT_ready.sem, norm.xT_ready.at(b, KD))
                for k in range(KD):
                    nc.vector.tensor_scalar(xT[:, k, bass.ds(b * T, T)], c.xnT[:, k, :], 1.0, None, ALU.mult)
                logits = c.bank[:, 2, 0:NT * E_ALL].rearrange("p (t e) -> p t e", t=NT)
                scores = score[:, :, 0:E_ALL]
                dve.wait_ge(logits_filled.sem, logits_filled.at(b, 1))
                link(nc.vector.tensor_reduce(row[:, 0:NT], logits, axis=AX.X, op=ALU.max))
                nc.vector.tensor_tensor(scores, logits, wide(row[:, 0:NT], E_ALL), ALU.subtract).then_inc(arg_ready.sem, 1)
                dve.wait_ge(exp_done.sem, exp_done.at(b, 1))
                link(nc.vector.tensor_reduce(row[:, 0:NT], scores, axis=AX.X, op=ALU.add))
                link(nc.vector.reciprocal(row2[:, 0:NT], row[:, 0:NT]))
                link(nc.vector.tensor_tensor(scores, scores, wide(row2[:, 0:NT], E_ALL), ALU.mult))
                nc.vector.memset(c.wait_mark[:, :], 0.0)
                for t in range(NT):
                    last = nc.vector.max(top8[:, t, :], score[:, t, 0:E_ALL])
                link(last)
                nc.vector.memset(top8[:, :, 6:7], -1.0)
                link(nc.vector.memset(top8[:, :, 7:8], -2.0))
                nc.vector.memset(c.wait_mark[:, :], 0.0)
                for t in range(NT):
                    last = nc.vector.match_replace(rest[:, t, :], top8[:, t, :], score[:, t, :], 0.0)
                link(last)
                nc.vector.tensor_tensor(dense[:, :, :], scores, rest[:, :, 0:E_ALL], ALU.subtract).then_inc(dense_ready.sem, 1)
                dve.wait_ge(flat_filled.sem, flat_filled.at(b, 1))
                flat = c.bank[:, 2, 0:NT * E_ALL]
                by_expert = lambda a: a.rearrange("p (u k) -> p u k", k=K)
                all_dense = dense[:, :, :].rearrange("p t e -> p (t e)")
                link(nc.vector.tensor_scalar(all_dense, flat, 0.0, -1e9, ALU.is_equal, ALU.mult))
                link(nc.vector.tensor_tensor(all_dense, all_dense, flat, ALU.add))
                link(nc.vector.tensor_reduce(row[:, :], by_expert(flat), axis=AX.X, op=ALU.add))
                nc.vector.tensor_scalar(share[:, bass.ds(b * NT, NT), :].rearrange("p t f -> p (t f)"), row[:, :], 1.0, None, ALU.mult)
                link(nc.vector.tensor_reduce(row2[:, :], by_expert(all_dense), axis=AX.X, op=ALU.max))
                nc.vector.tensor_tensor(by_expert(all_dense), by_expert(all_dense), wide(row2[:, :], K),
                                        ALU.subtract).then_inc(arg_ready.sem, 1)
                dve.wait_ge(exp_done.sem, exp_done.at(b, 2))
                link(nc.vector.tensor_reduce(row[:, :], by_expert(all_dense), axis=AX.X, op=ALU.add))
                link(nc.vector.reciprocal(row2[:, :], row[:, :]))
                nc.vector.tensor_tensor(by_expert(all_dense), by_expert(all_dense), wide(row2[:, :], K),
                                        ALU.mult).then_inc(soft_ready.sem, 1)
                dve.wait_ge(soft_ready.sem, soft_ready.at(b, 1))
                nc.vector.tensor_scalar(soft[:, bass.ds(b * NT, NT), :].rearrange("p t e -> p (t e)"), all_dense, 1.0, None, ALU.mult)
                dve.wait_ge(softT_filled.sem, softT_filled.at(b, 1))
                nc.vector.tensor_scalar(softT[:, bass.ds(b * T, T)], c.bank[0:E_ALL, 3, :], 1.0, None,
                                        ALU.mult).then_inc(routed_done.sem, 1)
                dve.wait_ge(routed_done.sem, routed_done.at(b, 1))
                chain.top_up(dve)

            def experts(turn, routed):
                def wait(name, u, n=1, per=1):
                    dve.wait_ge(sig[name].sem, sig[name].at(turn, u * per + n))

                def scale_weights(slot):
                    dve.wait_ge(w_loaded[slot].sem, w_loaded[slot].at(turn, 16))
                    nc.vector.tensor_tensor(cols(slot, "qb"), cols(slot, "qb"), cols(slot, "qb_scale"), ALU.mult)
                    nc.vector.tensor_tensor(cols(slot, "low", KR), cols(slot, "low", KR), cols(slot, "low_scale", KR),
                                            ALU.mult).then_inc(scaled.sem, 1)

                def routing(u):
                    slot, b = unit_of(u)
                    at = turn * (2 * K) + slot * K
                    return soft[:, b * NT:(b + 1) * NT, bass.ds(at, K)].rearrange("p t (k a) -> p t k a", a=1)

                def add_input(u):
                    slot, b = unit_of(u)
                    wait("xe_filled", u)
                    for k in range(KD):
                        last = nc.vector.tensor_tensor(xeT[:, u % 2, k, :], c.bank[:, XB + k, :],
                                                       xT[:, k, b * T:(b + 1) * T], ALU.add)
                    last.then_inc(sig["xe_ready"].sem, 1)

                def weigh(u):
                    wait("a_filled", u)
                    nc.vector.tensor_tensor(aw[:, :, :].rearrange("p t (k r) -> p t k r", k=K),
                                            c.bank[:, AB, :].rearrange("p (t k r) -> p t k r", t=NT, k=K),
                                            routing(u).broadcast_to([P, NT, K, 2 * R]), ALU.mult).then_inc(sig["aw_ready"].sem, 1)

                def weigh_down(u):
                    wait("a2_filled", u)
                    nc.vector.tensor_tensor(inner[:, u % 2, :, 0:KR].rearrange("p t (k r) -> p t k r", k=K),
                                            c.bank[:, AB, 0:NT * KR].rearrange("p (t k r) -> p t k r", t=NT, k=K),
                                            routing(u).broadcast_to([P, NT, K, R]), ALU.mult).then_inc(sig["aw2_ready"].sem, 1)

                def multiply(u, t):
                    slot, b = unit_of(u)
                    wait("silu_done", u, t + 1, NT)
                    h, up = inner[:, u % 2, t, KR:KR + I], c.bank[:, GB + t % 2, I:UP]
                    if routed:
                        by = share[:, b * NT + t, bass.ds(turn * 2 + slot, 1)]
                        ins = nc.vector.scalar_tensor_tensor(h, up, by, silu[:, t, :], ALU.mult, ALU.mult)
                    else:
                        ins = nc.vector.tensor_tensor(h, up, silu[:, t, :], ALU.mult)
                    ins.then_inc(sig["h_ready"].sem, 1)

                def add_output(u):
                    slot, b = unit_of(u)
                    wait("y_filled", u)
                    for half in range(2):
                        xs = c.x[:, b * TURN + half * 512:b * TURN + (half + 1) * 512]
                        last = nc.vector.tensor_tensor(xs, xs, c.bank[:, XB + half, :], ALU.add)
                    last.then_inc(sig["y_added"].sem, 1)

                if routed:
                    scale_weights(0)
                    add_input(0)
                    weigh(0)
                for u in range(units + 1):
                    if u < units:
                        multiply(u, 0)
                        if routed and u + 1 < units:
                            add_input(u + 1)
                    if routed and u:
                        weigh_down(u - 1)
                    if u < units:
                        multiply(u, 1)
                        if routed and u + 1 < units:
                            weigh(u + 1)
                        multiply(u, 2)
                        multiply(u, 3)
                        if routed and u == 2:
                            scale_weights(1)
                    if u:
                        add_output(u - 1)

            dve.sem_inc(sig["y_added"].sem, 1)
            nc.vector.memset(score[:, :, E_ALL:E_ALL + 1], -1.0)
            link(nc.vector.memset(score[:, :, E_ALL + 1:E_ALL + 2], -2.0))
            dve.wait_ge(index_ready.sem, index_ready.at(0, 1))
            nc.vector.tensor_copy(index_f[:, :], index[:, :])
            dve.wait_ge(loaded["map"].sem, loaded["map"].at(0, 16))
            link(nc.vector.tensor_copy(entry[:, :], mapping[:, :]))
            link(nc.vector.tensor_scalar(negative[:, :], entry[:, :], 0.0, float(E_ALL), ALU.is_lt, ALU.mult))
            link(nc.vector.tensor_tensor(entry[:, :], entry[:, :], negative[:, :], ALU.add))
            link(nc.vector.tensor_scalar(entry[:, :], entry[:, :], 0.0, float(E_ALL - 1), ALU.max, ALU.min))
            nc.vector.tensor_scalar(pick[:, :], entry[:, :], index_f[:, :], None, ALU.is_equal).then_inc(pick_ready.sem, 1)
            chain.begin_loop(dve)
            with dve.Fori(0, B) as b:
                chain.turn(b)
                route(b)
            with dve.Fori(0, turns - 1) as turn:
                experts(turn, True)
            experts(turns - 1, False)
    norm.end()
    chain.end(B)
    for s in (*loaded.values(), index_ready, pick_ready):
        s.end(1)
    for s in (logits_filled, arg_ready, exp_done, dense_ready, denseT_filled, denseT_ready, flat_filled,
              soft_ready, softT_filled, routed_done):
        s.end(B)
    for s in w_loaded:
        s.end(turns)
    routed_only = ("xe_filled", "xe_ready", "a_filled", "aw_ready", "aT_filled", "aT_ready", "a2_filled",
                   "aw2_ready", "tailT_filled", "tailT_ready")
    scaled.end(turns - 1)
    for n, s in sig.items():
        s.end(turns - (n in routed_only))


def build_store(c, out_dram):
    stored = c.counter("stored", 16)
    with c.nc.Block() as block:
        @block.sync
        def _(sp):
            sp.dma_start(out_dram.rearrange("b (t p) d -> p b t d", p=P),
                         c.x[:, :].rearrange("p (b t d) -> p b t d", b=B, t=NT)).then_inc(stored.sem, 16)
            sp.wait_ge(stored.sem, stored.at(0, 16))


def build_program(nc, ins, out, stages):
    with ExitStack() as ctx:
        c = Chip(ctx, nc)
        build_constants(c, ins["x"])
        for stage in stages:
            if stage == "big":
                build_big_attention(c, ins["big_w"], ins["big_wo"], ins["big_bo"])
            elif stage == "ffn":
                build_ffn(c, ins["ffn_w"], ins["ffn_bias"], ins["ffn_affine"])
            elif stage == "moe":
                build_moe(c, ins)
            else:
                build_small_attention(c, stage, ins)
        build_store(c, out)


STAGES = ("big", "ffn", "differential", "ffn", "splat", "moe", "rope", "moe")



def rows(w):
    return w.reshape(-1, P, w.shape[-1]).transpose(1, 0, 2)


def put(pack, name, v, row=0, col=0):
    at = AT[name][0] + col
    pack[row:row + v.shape[0], at:at + v.shape[1]] = v


def lay_out(a):
    g = {}
    g["x"] = a["L0_attn_a_query"]
    big = [a[f"L0_attn_a_w_{n}"].reshape(D, H0, DH0).transpose(1, 0, 2) for n in "qkv"]
    big = np.concatenate(big, axis=2).reshape(H0, KD, P, QKV0).transpose(0, 2, 1, 3).reshape(H0, P, KD * QKV0)
    bq, bk, bv = (a[f"L0_attn_a_b_{n}"].reshape(H0, DH0) for n in "qkv")
    g["big_w"] = np.concatenate([big, bq[:, :, None], bk[:, :, None],
                                 np.broadcast_to(bv[:, None, :], (H0, P, DH0))], axis=2)
    g["big_wo"] = a["L0_attn_a_w_o"].reshape(H0, DH0, D)
    g["big_bo"] = np.tile(a["L0_attn_a_b_o"][None, :], (1, 2))
    g["ffn_w"] = rows(a["L0_ffn_weight"].T)
    g["ffn_bias"] = np.tile(a["L0_ffn_bias"][None, :], (1, 2))
    g["ffn_affine"] = np.broadcast_to(np.stack([a["L0_ffn_ln_gamma"], a["L0_ffn_ln_beta"]])[None], (P, 2, D))
    spread = lambda v: np.broadcast_to(v, (P, *v.shape))
    d = {n: a[f"L0_attn_b_{n}"] for n in ("Wq", "Wk", "Wv", "Wo", "bq", "bk", "bv", "bo", "lq1", "lk1", "lq2", "lk2", "g_subln")}
    for n in "qkvo":
        g[f"differential_w{n}"] = rows(d[f"W{n}"])
        g[f"splat_w{n}"] = rows(a[f"L1_attn_a_W{n}"].T)
        g[f"rope_w{n}"] = rows(a[f"L1_attn_b_W{n}"].T)
    for n in "qkv":
        g[f"differential_b{n}"] = spread(d[f"b{n}"])
    g["differential_bo"] = np.tile(d["bo"][None, :], (1, 2))
    g["differential_lam"] = spread(np.stack([d["lq1"], d["lk1"], d["lq2"], d["lk2"]]))
    g["differential_gsub"] = spread(d["g_subln"])
    pos, direction = a["L1_attn_a_splat_positions"], a["L1_attn_a_splat_directions"]
    g["splat_pos"] = spread(pos.reshape(-1))
    g["splat_dir"] = spread(direction.reshape(-1))
    g["splat_logs"] = spread(np.stack([a["L1_attn_a_splat_log_scales"].reshape(-1),
                                       a["L1_attn_a_splat_log_amplitudes"].reshape(-1)]))
    g["splat_scal"] = spread(np.stack([a["L1_attn_a_directional_strength"], a["L1_attn_a_position_sensitivity"],
                                       a["L1_attn_a_gsa_strength"]]))
    blocks = np.concatenate([pos.transpose(2, 0, 1), direction.transpose(2, 0, 1)], axis=2)
    g["splat_blocks"] = np.tile(blocks.reshape(DH1, D), (8, 1))
    orders = np.array([[0, 1, 2, 0, 1, 2, 0, 1], [0, 0, 0, 1, 1, 1, 2, 2]])
    masks = 2.0 * (orders[:, :, None] == np.arange(3)).astype(np.float32)
    g["splat_masks"] = np.repeat(masks.transpose(1, 0, 2).reshape(8, 6), DH1, axis=0)
    inv_freq = np.float32(10000.0) ** (-np.arange(0, DH1, 2, dtype=np.float32) / np.float32(DH1))
    angles = (np.arange(T, dtype=np.float32)[:, None] * inv_freq[None, :]).astype(np.float32)
    for n, f in (("cos", np.cos), ("sin", np.sin)):
        table = f(angles).astype(np.float32).reshape(NT, P, DH1 // 2).transpose(1, 0, 2)
        g[f"rope_{n}"] = np.stack([table * np.float32(0.25), table], axis=1)
    m = {n[len("L1_ffn_"):]: v for n, v in a.items() if n.startswith("L1_ffn_")}
    g["moe_gate"] = rows(m["gate_weight"].T)
    g["moe_map"] = np.broadcast_to(m["inv_mapping"].reshape(1, -1), (E_ALL, E_ALL))
    packs = np.zeros((F + 2, P, PACK_E), np.float32)
    for f in range(F):
        qa = np.concatenate([m["gate_qa"][f], m["up_qa"][f]], axis=1).reshape(2 * KR, D)
        w1 = np.concatenate([m["gate_W"][f].T, m["up_W"][f].T, qa.T], axis=1)
        put(packs[f], "w1", rows(w1).reshape(P, -1))
        qb = np.zeros((K, 2, R, 2, I), np.float32)
        qb[:, 0, :, 0, :] = m["gate_qb"][f].transpose(0, 2, 1)
        qb[:, 1, :, 1, :] = m["up_qb"][f].transpose(0, 2, 1)
        put(packs[f], "qb", qb.reshape(P, UP))
        put(packs[f], "qb_scale", np.broadcast_to(np.concatenate([m["gate_scale"][f], m["up_scale"][f]]), (P, UP)))
        put(packs[f], "mu", m["mask_up_W"][f].T, row=f * K)
        down, down_qa = m["down_W"][f].T, m["down_qa"][f].reshape(KR, I).T
        put(packs[f], "down", down[TAIL:])
        put(packs[f], "down", down_qa[TAIL:], col=D)
        put(packs[f], "qa_tail", down_qa[:TAIL])
        put(packs[f], "low", m["down_qb"][f].transpose(0, 2, 1).reshape(KR, D))
        put(packs[f], "low", down[:TAIL], row=KR)
        put(packs[f], "low_scale", np.broadcast_to(m["down_scale"][f], (KR, D)))
    for i in range(2):
        f, part = F + i, slice(i * I, (i + 1) * I)
        w1 = np.concatenate([m["sh_gate_W"][part].T, m["sh_up_W"][part].T, np.zeros((D, 2 * KR), np.float32)], axis=1)
        put(packs[f], "w1", rows(w1).reshape(P, -1))
        put(packs[f], "down", m["sh_down_W"].T[part][TAIL:])
        put(packs[f], "low", m["sh_down_W"].T[part][:TAIL])
    g["moe_w"] = packs
    return {k: np.ascontiguousarray(v) for k, v in g.items()}


def kernel(**inputs):
    import concourse.bacc as bacc
    from concourse.bass_utils import run_bass_kernel_spmd

    arrays = lay_out({k: np.asarray(v) for k, v in inputs.items()})
    nc = bacc.Bacc("TRN2", target_bir_lowering=False, num_devices=1)
    ins = {k: nc.dram_tensor(f"in_{k}", v.shape, mybir.dt.from_np(v.dtype), kind="ExternalInput").ap()
           for k, v in arrays.items()}
    out = nc.dram_tensor("out", (B, T, D), F32, kind="ExternalOutput").ap()
    build_program(nc, ins, out, STAGES)
    result = run_bass_kernel_spmd(nc, [{f"in_{k}": v for k, v in arrays.items()}], core_ids=[0])
    return result.results[0]["out"]
```

```python
from contextlib import ExitStack

import numpy as np

import concourse.bass as bass
from concourse import mybir

F32 = mybir.dt.float32
BF16 = mybir.dt.bfloat16
I32 = mybir.dt.int32
ACT = mybir.ActivationFunctionType
ALU = mybir.AluOpType
AX = mybir.AxisListType

B, T, D = 4, 512, 256
P = 128
NT = T // P
KD = D // P
TURN = NT * D
LN_EPS = 1e-5
MASKED = -1e30

H0, DH0 = 16, 128
QKV0 = 3 * DH0
PACK0 = KD * QKV0 + 2 + DH0

LAMBDA_INIT = 0.8 - 0.6
SCALE_DIFF = float(8.0 ** -0.5)
RMS_EPS = 1e-6

H1, DH1 = 16, 16
STRIP = 32
HG = P // STRIP
NG = H1 // HG


class Counter:

    def __init__(self, ctx, nc, name):
        self.sem = ctx.enter_context(nc.semaphore(name))
        self.base = 0
        self.per = 0

    def begin(self, per, credit=0):
        self.per = per
        self.base += credit

    def at(self, turn, n):
        return turn * self.per + (self.base + n)

    def end(self, turns):
        self.base += self.per * turns


class Chain:

    PER = 64

    def __init__(self, c, name):
        self.counter = c.counter(name, 0)
        self.n = 0
        self.now = 0

    def link(self, eng, ins):
        ins.then_inc(self.counter.sem, 1)
        self.n += 1
        eng.wait_ge(self.counter.sem, self.counter.at(self.now, self.n))

    def begin_loop(self, eng):
        self.counter.base += self.n
        self.counter.per = self.PER

    def finish(self):
        self.counter.base += self.n

    def turn(self, turn):
        self.now, self.n = turn, 0

    def top_up(self, eng):
        assert 0 < self.n < self.PER
        eng.sem_inc(self.counter.sem, self.PER - self.n)

    def end(self, turns):
        self.counter.end(turns)


class Chip:

    def __init__(self, ctx, nc):
        self.nc = nc
        self.ctx = ctx
        self.signals = {}
        self.uses = {}
        sb = self.sb
        self.x = sb("x_resid", [P, (B + 1) * TURN])
        self.xn = sb("x_normed", [P, NT, D])
        self.xnT = sb("x_normed_T", [P, KD, T])
        self.ident = sb("ident", [P, P])
        self.ident_bf = sb("ident_bf", [P, P], BF16)
        self.causal = sb("causal", [P, P], BF16)
        self.ones = sb("ones", [1, P])
        self.minus_half = sb("minus_half", [P, NT])
        self.minus_one = sb("minus_one", [P, 1])
        self.stats = sb("stats", [P, NT, 6])
        self.mean_var = sb("mean_var", [P, NT, 2])
        self.var_eps = sb("var_eps", [P, NT])
        self.rstd = sb("rstd", [P, NT])
        self.wait_mark = sb("wait_mark", [P, 1])
        self.bank = ctx.enter_context(nc.psum_tensor("bank", [P, 8, 512], F32))

    def sb(self, name, shape, dt=F32, ctx=None):
        self.uses[name] = self.uses.get(name, 0) + 1
        if self.uses[name] > 1:
            name = f"{name}_{self.uses[name]}"
        return (ctx or self.ctx).enter_context(self.nc.sbuf_tensor(name, shape, dt))

    def counter(self, name, per, credit=0):
        if name not in self.signals:
            self.signals[name] = Counter(self.ctx, self.nc, name)
        self.signals[name].begin(per, credit)
        return self.signals[name]

    def x_cols(self, b, start, n):
        return self.x[:, bass.ds(b * TURN + start, n)]


def build_constants(c, x_dram):
    nc = c.nc
    x_loaded = c.counter("x_loaded", 16)
    filled = c.counter("const_filled", 3)
    made = c.counter("const_made", 3)
    with nc.Block() as block:
        @block.sync
        def _(sp):
            sp.dma_start(c.x[:, 0:B * TURN].rearrange("p (b t d) -> p b t d", b=B, t=NT),
                         x_dram.rearrange("b (t p) d -> p b t d", p=P)).then_inc(x_loaded.sem, 16)
            sp.wait_ge(x_loaded.sem, x_loaded.at(0, 16))

        @block.vector
        def _(dve):
            nc.vector.memset(c.x[:, B * TURN:(B + 1) * TURN], 0.0)
            nc.vector.memset(c.ones[:, :], 1.0)
            nc.vector.memset(c.minus_half[:, :], -0.5)
            nc.vector.memset(c.minus_one[:, :], -1.0)

        @block.gpsimd
        def _(pool):
            nc.gpsimd.memset(c.ident[:, :], 0.0).then_inc(filled.sem, 1)
            nc.gpsimd.memset(c.ident_bf[:, :], 0.0).then_inc(filled.sem, 1)
            nc.gpsimd.memset(c.causal[:, :], 0.0).then_inc(filled.sem, 1)
            pool.wait_ge(filled.sem, filled.at(0, 3))
            for eye in (c.ident, c.ident_bf):
                nc.gpsimd.affine_select(out=eye[:, :], in_=eye[:, :], compare_op=ALU.not_equal, fill=1.0,
                                        base=0, pattern=[[-1, P]], channel_multiplier=1).then_inc(made.sem, 1)
            nc.gpsimd.affine_select(out=c.causal[:, :], in_=c.causal[:, :], compare_op=ALU.is_ge, fill=MASKED,
                                    base=0, pattern=[[-1, P]], channel_multiplier=1).then_inc(made.sem, 1)
            pool.wait_ge(made.sem, made.at(0, 3))
    for s in (x_loaded, filled, made):
        s.end(1)


class Norm:

    def __init__(self, c):
        self.c = c
        self.stats_done = c.counter("stats_done", NT)
        self.moments_done = c.counter("moments_done", NT)
        self.var_ready = c.counter("var_ready", 1)
        self.rstd_ready = c.counter("rstd_ready", 1)
        self.xn_ready = c.counter("xn_ready", NT)
        self.xT_filled = c.counter("xT_filled", KD)
        self.xT_ready = c.counter("xT_ready", KD)

    def moments(self, dve, turn):
        c, nc = self.c, self.c.nc
        for t in range(NT):
            nc.vector.bn_stats(c.stats[:, t, :], c.x_cols(turn, t * D, D)).then_inc(self.stats_done.sem, 1)
        dve.wait_ge(self.stats_done.sem, self.stats_done.at(turn, NT))
        nc.vector.memset(c.wait_mark[:, :], 0.0)
        for t in range(NT):
            nc.vector.bn_aggr(c.mean_var[:, t, :], c.stats[:, t, :]).then_inc(self.moments_done.sem, 1)
        dve.wait_ge(self.moments_done.sem, self.moments_done.at(turn, NT))
        nc.vector.tensor_scalar_add(c.var_eps[:, :], c.mean_var[:, :, 1], LN_EPS).then_inc(self.var_ready.sem, 1)

    def rows(self, dve, turn):
        c, nc = self.c, self.c.nc
        dve.wait_ge(self.rstd_ready.sem, self.rstd_ready.at(turn, 1))
        for t in range(NT):
            nc.vector.tensor_scalar(c.xn[:, t, :], c.x_cols(turn, t * D, D), c.mean_var[:, t, 0:1], c.rstd[:, t:t + 1],
                                    ALU.subtract, ALU.mult).then_inc(self.xn_ready.sem, 1)

    def pool(self, pool, turn):
        c = self.c
        pool.wait_ge(self.var_ready.sem, self.var_ready.at(turn, 1))
        c.nc.gpsimd.tensor_tensor(c.rstd[:, :], c.var_eps[:, :], c.minus_half[:, 0:NT],
                                  ALU.pow).then_inc(self.rstd_ready.sem, 1)

    def tensor(self, pe, banks):
        c = self.c
        for k in range(KD):
            for t in range(NT):
                last = c.nc.tensor.transpose(c.bank[:, banks[k], t * P:(t + 1) * P],
                                             c.xn[:, t, k * P:(k + 1) * P], c.ident[:, :])
            last.then_inc(self.xT_filled.sem, 1)

    def scalar(self, act, turn, banks):
        c = self.c
        for k in range(KD):
            act.wait_ge(self.xT_filled.sem, self.xT_filled.at(turn, k + 1))
            c.nc.scalar.copy(c.xnT[:, k, :], c.bank[:, banks[k], :]).then_inc(self.xT_ready.sem, 1)

    def end(self):
        for s in (self.stats_done, self.moments_done, self.var_ready, self.rstd_ready, self.xn_ready):
            s.end(B + 1)
        for s in (self.xT_filled, self.xT_ready):
            s.end(B)


class NormAll:

    def __init__(self, c, ctx, rounds=1):
        self.c = c
        tiles = B * NT
        self.xn = c.sb("all_xn", [P, tiles, D], ctx=ctx)
        self.stats = c.sb("all_stats", [P, tiles, 6], ctx=ctx)
        self.mean_var = c.sb("all_mean_var", [P, tiles, 2], ctx=ctx)
        self.var_eps = c.sb("all_var_eps", [P, tiles], ctx=ctx)
        self.rstd = c.sb("all_rstd", [P, tiles], ctx=ctx)
        self.stats_done = c.counter("all_stats_done", tiles * rounds)
        self.moments_done = c.counter("all_moments_done", tiles * rounds)
        self.var_ready = c.counter("all_var_ready", B * rounds)
        self.rstd_ready = c.counter("all_rstd_ready", B * rounds)
        self.xn_ready = c.counter("all_xn_ready", tiles * rounds)

    def source(self, t, round):
        return self.xn[:, t, :] if round else self.c.x[:, t * D:(t + 1) * D]

    def moments(self, dve, b, round=0):
        c, nc = self.c, self.c.nc
        these, done = range(b * NT, (b + 1) * NT), (round * B + b + 1) * NT
        if round:
            dve.wait_ge(self.xn_ready.sem, self.xn_ready.at(0, done - B * NT))
            nc.vector.memset(c.wait_mark[:, :], 0.0)
        for t in these:
            nc.vector.bn_stats(self.stats[:, t, :], self.source(t, round)).then_inc(self.stats_done.sem, 1)
        dve.wait_ge(self.stats_done.sem, self.stats_done.at(0, done))
        nc.vector.memset(c.wait_mark[:, :], 0.0)
        for t in these:
            nc.vector.bn_aggr(self.mean_var[:, t, :], self.stats[:, t, :]).then_inc(self.moments_done.sem, 1)
        dve.wait_ge(self.moments_done.sem, self.moments_done.at(0, done))
        nc.vector.tensor_scalar_add(self.var_eps[:, b * NT:(b + 1) * NT], self.mean_var[:, b * NT:(b + 1) * NT, 1],
                                    LN_EPS).then_inc(self.var_ready.sem, 1)

    def rows(self, dve, b, round=0):
        dve.wait_ge(self.rstd_ready.sem, self.rstd_ready.at(0, round * B + b + 1))
        for t in range(b * NT, (b + 1) * NT):
            self.c.nc.vector.tensor_scalar(self.xn[:, t, :], self.source(t, round), self.mean_var[:, t, 0:1],
                                           self.rstd[:, t:t + 1], ALU.subtract, ALU.mult).then_inc(self.xn_ready.sem, 1)

    def pool(self, pool, rounds=1):
        c = self.c
        for n in range(B * rounds):
            these = slice(n % B * NT, (n % B + 1) * NT)
            pool.wait_ge(self.var_ready.sem, self.var_ready.at(0, n + 1))
            c.nc.gpsimd.tensor_tensor(self.rstd[:, these], self.var_eps[:, these], c.minus_half[:, 0:NT],
                                      ALU.pow).then_inc(self.rstd_ready.sem, 1)

    def end(self):
        for s in (self.stats_done, self.moments_done, self.var_ready, self.rstd_ready, self.xn_ready):
            s.end(1)


def build_ffn(c, w_dram, bias_dram, affine_dram):
    nc = c.nc
    loaded = [c.counter(f"ffn_loaded{i}", 16) for i in range(3)]
    abs_done = c.counter("ffn_abs_done", 1)
    mean_filled = c.counter("ffn_mean_filled", 1)
    limit_ready = c.counter("ffn_limit_ready", 2)
    low_ready = c.counter("ffn_low_ready", 1)
    w_ready = c.counter("ffn_w_ready", 1)
    ones_ready = c.counter("ffn_ones_ready", 1)
    scaled = c.counter("ffn_scaled", B)
    affine_done = c.counter("ffn_affine_done", B)
    xT_filled, xT_ready = c.counter("ffn_xT_filled", B * KD), c.counter("ffn_xT_ready", B * KD)
    y_filled, y_added = c.counter("ffn_y_filled", 2 * B), c.counter("ffn_y_added", 2 * B)
    with ExitStack() as ctx:
        w = c.sb("ffn_w", [P, KD, D], ctx=ctx)
        low = c.sb("ffn_low", [P, KD, D], ctx=ctx)
        bias = c.sb("ffn_bias", [1, 2 * D], ctx=ctx)
        affine = c.sb("ffn_affine", [P, 2, D], ctx=ctx)
        all_ones = c.sb("ffn_all_ones", [P, P], ctx=ctx)
        abs_sum = c.sb("ffn_abs_sum", [P, 1], ctx=ctx)
        limit = c.sb("ffn_limit", [P, 2], ctx=ctx)
        xT = c.sb("ffn_xT", [P, 2, KD, T], ctx=ctx)
        norm = NormAll(c, ctx, rounds=2)
        block = ctx.enter_context(nc.Block())
        banks = lambda b: 4 * (b % 2)

        @block.sync
        def _(sp):
            sp.dma_start(w[:, :, :], w_dram).then_inc(loaded[0].sem, 16)
            sp.dma_start(bias[:, :], bias_dram).then_inc(loaded[1].sem, 16)
            sp.dma_start(affine[:, :, :], affine_dram).then_inc(loaded[2].sem, 16)

        @block.vector
        def _(dve):
            def make_ternary():
                dve.wait_ge(loaded[0].sem, loaded[0].at(0, 16))
                nc.vector.tensor_reduce(abs_sum[:, :], w[:, :, :], axis=AX.XY, op=ALU.add,
                                        apply_absolute_value=True).then_inc(abs_done.sem, 1)
                dve.wait_ge(mean_filled.sem, mean_filled.at(0, 1))
                nc.vector.tensor_scalar(limit[:, 0:1], c.bank[:, 0, 0:1], 0.5 / (D * D), 0.5e-5,
                                        ALU.mult, ALU.add).then_inc(limit_ready.sem, 1)
                dve.wait_ge(limit_ready.sem, limit_ready.at(0, 1))
                nc.vector.tensor_scalar_mul(limit[:, 1:2], limit[:, 0:1], -1.0).then_inc(limit_ready.sem, 1)
                dve.wait_ge(limit_ready.sem, limit_ready.at(0, 2))
                nc.vector.tensor_scalar(low[:, :, :], w[:, :, :], limit[:, 1:2], None,
                                        ALU.is_lt).then_inc(low_ready.sem, 1)
                dve.wait_ge(low_ready.sem, low_ready.at(0, 1))
                nc.vector.scalar_tensor_tensor(w[:, :, :], w[:, :, :], limit[:, 0:1], low[:, :, :],
                                               ALU.is_gt, ALU.subtract).then_inc(w_ready.sem, 1)

            def affine_rows(b):
                rows = norm.xn[:, b * NT:(b + 1) * NT, :]
                dve.wait_ge(norm.xn_ready.sem, norm.xn_ready.at(0, (B + b + 1) * NT))
                nc.vector.tensor_tensor(rows, rows, affine[:, 0:1, :].broadcast_to([P, NT, D]), ALU.mult)\
                  .then_inc(scaled.sem, 1)
                dve.wait_ge(scaled.sem, scaled.at(0, b + 1))
                nc.vector.tensor_tensor(rows, rows, affine[:, 1:2, :].broadcast_to([P, NT, D]), ALU.add)\
                  .then_inc(affine_done.sem, 1)

            def add_output(b):
                for half in range(2):
                    dve.wait_ge(y_filled.sem, y_filled.at(0, 2 * b + half + 1))
                    xs = c.x[:, b * TURN + half * 512:b * TURN + (half + 1) * 512]
                    nc.vector.tensor_tensor(xs, xs, c.bank[:, banks(b) + 2 + half, :], ALU.add).then_inc(y_added.sem, 1)

            nc.vector.memset(all_ones[:, :], 1.0).then_inc(ones_ready.sem, 1)
            for b in range(B):
                norm.moments(dve, b)
            for b in range(B):
                norm.rows(dve, b)
                norm.moments(dve, b, round=1)
            make_ternary()
            dve.wait_ge(loaded[2].sem, loaded[2].at(0, 16))
            for b in range(B):
                norm.rows(dve, b, round=1)
                affine_rows(b)
                if b:
                    add_output(b - 1)
            add_output(B - 1)

        @block.gpsimd
        def _(pool):
            norm.pool(pool, rounds=2)

        @block.tensor
        def _(pe):
            pe.wait_ge(ones_ready.sem, ones_ready.at(0, 1))
            pe.wait_ge(abs_done.sem, abs_done.at(0, 1))
            nc.tensor.matmul(c.bank[:, 0, 0:1], all_ones[:, :], abs_sum[:, :],
                             start=True, stop=True).then_inc(mean_filled.sem, 1)
            pe.wait_ge(w_ready.sem, w_ready.at(0, 1))
            pe.wait_ge(loaded[1].sem, loaded[1].at(0, 16))

            def transpose_x(b):
                pe.wait_ge(affine_done.sem, affine_done.at(0, b + 1))
                for k in range(KD):
                    for t in range(NT):
                        last = nc.tensor.transpose(c.bank[:, banks(b) + k, t * P:(t + 1) * P],
                                                   norm.xn[:, b * NT + t, k * P:(k + 1) * P], c.ident[:, :])
                    last.then_inc(xT_filled.sem, 1)

            def output(b):
                pe.wait_ge(xT_ready.sem, xT_ready.at(0, (b + 1) * KD))
                if b >= 2:
                    pe.wait_ge(y_added.sem, y_added.at(0, 2 * (b - 1)))
                for half in range(2):
                    out = c.bank[:, banks(b) + 2 + half, :]
                    nc.tensor.matmul(out, c.ones[:, :], bias[:, :], start=True, stop=True)
                    for t in (2 * half, 2 * half + 1):
                        for k in range(KD):
                            last = nc.tensor.matmul(out[:, (t % 2) * D:(t % 2 + 1) * D],
                                                    xT[:, b % 2, k, t * P:(t + 1) * P], w[:, k, :],
                                                    start=False, stop=(k == KD - 1), skip_group_check=True)
                    last.then_inc(y_filled.sem, 1)

            for b in range(B + 1):
                if b < B:
                    transpose_x(b)
                if b:
                    output(b - 1)

        @block.scalar
        def _(act):
            for b in range(B):
                if b >= 2:
                    act.wait_ge(y_filled.sem, y_filled.at(0, 2 * (b - 1)))
                for k in range(KD):
                    act.wait_ge(xT_filled.sem, xT_filled.at(0, b * KD + k + 1))
                    nc.scalar.copy(xT[:, b % 2, k, :], c.bank[:, banks(b) + k, :]).then_inc(xT_ready.sem, 1)
    norm.end()
    for s in (*loaded, abs_done, mean_filled, limit_ready, low_ready, w_ready, ones_ready, scaled, affine_done,
              xT_filled, xT_ready, y_filled, y_added):
        s.end(1)


def build_big_attention(c, w_dram, wo_dram, bo_dram):
    nc = c.nc
    scale = float(1.0 / np.sqrt(np.float32(DH0)))
    pairs = H0 // 2
    norm = Norm(c)
    w_loaded = [c.counter(f"big_w_loaded{p}", 16) for p in range(2)]
    wo_loaded = [c.counter(f"big_wo_loaded{p}", 16) for p in range(2)]
    bo_loaded = c.counter("big_bo_loaded", 16)
    bq_ready = c.counter("big_bq_ready", 1)
    proj_filled = c.counter("big_proj_filled", 3)
    qk_ready = c.counter("big_qk_ready", 2, credit=4)
    v_ready = c.counter("big_v_ready", 1, credit=2)
    s_filled = c.counter("big_s_filled", NT)
    max_ready = c.counter("big_max_ready", NT)
    exp_done = c.counter("big_exp_done", NT)
    rinv_ready = c.counter("big_rinv_ready", NT)
    p_ready = c.counter("big_p_ready", NT)
    t_filled = c.counter("big_t_filled", NT)
    pt_ready = c.counter("big_pt_ready", NT)
    ot_filled = c.counter("big_ot_filled", 1)
    ot_ready = c.counter("big_ot_ready", 1)
    head_added = c.counter("big_head_added", 1, credit=2)
    y_added = c.counter("big_y_added", 1, credit=1)
    QV, K, S0, TB, OTB, Y0 = 0, 1, 2, 4, 5, 6
    with ExitStack() as ctx:
        w = c.sb("big_w", [P, 2, PACK0], ctx=ctx)
        wo = c.sb("big_wo", [P, 2, D], ctx=ctx)
        bo = c.sb("big_bo", [1, 2 * D], ctx=ctx)
        bq_scaled = c.sb("big_bq_scaled", [P, 2], ctx=ctx)
        qT = c.sb("big_qT", [P, 2, T], ctx=ctx)
        kT = c.sb("big_kT", [P, 2, T], ctx=ctx)
        v = c.sb("big_v", [P, 2, NT, DH0], ctx=ctx)
        probs = c.sb("big_probs", [P, NT, T], ctx=ctx)
        pT = c.sb("big_pT", [P, 2, NT, T], ctx=ctx)
        oT = c.sb("big_oT", [P, 2, T], ctx=ctx)
        neg_max = c.sb("big_neg_max", [P, 2, NT], ctx=ctx)
        total = c.sb("big_total", [P, 2, NT], ctx=ctx)
        rinv = c.sb("big_rinv", [P, 2, NT], ctx=ctx)
        block = ctx.enter_context(nc.Block())

        def each_turn(eng, start, unit, end):
            with eng.Fori(0, B) as b:
                start(b)
                for slot in (0, 1):
                    unit(b * pairs, slot, first=(slot == 0), last=False)
                with eng.Fori(1, pairs - 1) as pair:
                    for slot in (0, 1):
                        unit(b * pairs + pair, slot, first=False, last=False)
                for slot in (0, 1):
                    unit(b * pairs + (pairs - 1), slot, first=False, last=(slot == 1))
                end(b)

        def following(g, slot):
            return (g, 1) if slot == 0 else (g + 1, 0)

        @block.sync
        def _(sp):
            sp.dma_start(bo[:, :], bo_dram).then_inc(bo_loaded.sem, 16)
            with sp.Fori(0, B) as b:
                with sp.Fori(0, pairs) as pair:
                    for slot in (0, 1):
                        u = (b * pairs + pair) * 2 + slot
                        head = sp.snap(pair * 2 + slot)
                        sp.wait_ge(v_ready.sem, v_ready.at(u, -1))
                        sp.wait_ge(qk_ready.sem, qk_ready.at(u, -2))
                        sp.dma_start(w[:, slot, :], w_dram[bass.ds(head, 1)]
                                     .rearrange("a p n -> p (a n)")).then_inc(w_loaded[slot].sem, 16)

        @block.tensor
        def _(pe):
            def project(slot, part):
                def cols(k):
                    return w[:, slot, k * QKV0 + part * DH0:k * QKV0 + (part + 1) * DH0]
                if part < 2:
                    for k in range(KD):
                        last = nc.tensor.matmul(c.bank[:, (QV, K)[part], :], cols(k), c.xnT[:, k, :],
                                                start=(k == 0), stop=(k == KD - 1))
                else:
                    for t in range(NT):
                        for k in range(KD):
                            last = nc.tensor.matmul(c.bank[:, QV, t * P:(t + 1) * P],
                                                    c.xnT[:, k, t * P:(t + 1) * P], cols(k),
                                                    start=(k == 0), stop=(k == KD - 1))
                last.then_inc(proj_filled.sem, 1)

            def scores(slot, i):
                bank, width = S0 + i % 2, (i + 1) * P
                nc.tensor.matmul(c.bank[:, bank, 0:width], qT[:, slot, i * P:width], kT[:, slot, 0:width],
                                 start=True, stop=False)
                nc.tensor.matmul(c.bank[:, bank, i * P:width], c.ident_bf[:, :], c.causal[:, :],
                                 start=False, stop=True).then_inc(s_filled.sem, 1)

            def transposes(u, i):
                pe.wait_ge(p_ready.sem, p_ready.at(u, i + 1))
                if i:
                    pe.wait_ge(pt_ready.sem, pt_ready.at(u, i))
                for j in range(i + 1):
                    last = nc.tensor.transpose(c.bank[:, TB, j * P:(j + 1) * P],
                                               probs[:, i, j * P:(j + 1) * P], c.ident[:, :])
                last.then_inc(t_filled.sem, 1)

            def values(u, slot):
                pe.wait_ge(pt_ready.sem, pt_ready.at(u, NT))
                for j in range(NT):
                    mm = nc.tensor.matmul(c.bank[:, OTB, j * P:T], v[:, slot, j, :], pT[:, slot, j, j * P:T],
                                          start=(j == 0), stop=(j == NT - 1))
                mm.then_inc(ot_filled.sem, 1)

            def add_head(u, g, slot, final):
                pe.wait_ge(ot_ready.sem, ot_ready.at(u, 1))
                pe.wait_ge(wo_loaded[slot].sem, wo_loaded[slot].at(g, 16))
                for t in range(NT):
                    last = nc.tensor.matmul(c.bank[:, Y0 + t // 2, (t % 2) * D:(t % 2 + 1) * D],
                                            oT[:, slot, t * P:(t + 1) * P], wo[:, slot, :],
                                            start=False, stop=final, skip_group_check=True)
                last.then_inc(head_added.sem, 1)

            def start(b):
                pe.wait_ge(norm.xn_ready.sem, norm.xn_ready.at(b, NT))
                norm.tensor(pe, (TB, OTB))
                pe.wait_ge(y_added.sem, y_added.at(b, 0))
                for bank in (Y0, Y0 + 1):
                    nc.tensor.matmul(c.bank[:, bank, :], c.ones[:, :], bo[:, :], start=True, stop=True)
                pe.wait_ge(norm.xT_ready.sem, norm.xT_ready.at(b, KD))
                pe.wait_ge(w_loaded[0].sem, w_loaded[0].at(b * pairs, 16))
                project(0, 0)
                project(0, 1)
                pe.wait_ge(qk_ready.sem, qk_ready.at(b * H0, 1))
                project(0, 2)

            def unit(g, slot, first, last):
                u = g * 2 + slot
                g_next, slot_next = following(g, slot)
                before = (u + -1, 1 - slot)
                pe.wait_ge(qk_ready.sem, qk_ready.at(u, 2))
                if not first:
                    pe.wait_ge(exp_done.sem, exp_done.at(before[0], NT))
                scores(slot, 0)
                scores(slot, 1)
                if not first:
                    transposes(before[0], NT - 1)
                pe.wait_ge(v_ready.sem, v_ready.at(u, 1))
                if not last:
                    pe.wait_ge(w_loaded[slot_next].sem, w_loaded[slot_next].at(g_next, 16))
                    project(slot_next, 0)
                if not first:
                    values(*before)
                transposes(u, 0)
                pe.wait_ge(exp_done.sem, exp_done.at(u, 1))
                scores(slot, 2)
                if not last:
                    project(slot_next, 1)
                transposes(u, 1)
                pe.wait_ge(exp_done.sem, exp_done.at(u, 2))
                scores(slot, 3)
                if not first:
                    add_head(before[0], g + (-1 if slot == 0 else 0), 1 - slot, False)
                transposes(u, 2)
                if not last:
                    pe.wait_ge(qk_ready.sem, qk_ready.at(u, 3))
                    project(slot_next, 2)

            def end(b):
                u = b * H0 + (H0 - 1)
                transposes(u, NT - 1)
                values(u, 1)
                add_head(u, b * pairs + (pairs - 1), 1, True)

            pe.wait_ge(bo_loaded.sem, bo_loaded.at(0, 16))
            each_turn(pe, start, unit, end)

        @block.scalar
        def _(act):
            def copy_q(u, slot):
                act.wait_ge(bq_ready.sem, bq_ready.at(u, 1))
                act.wait_ge(proj_filled.sem, proj_filled.at(u, 1))
                nc.scalar.activation(qT[:, slot, :], c.bank[:, QV, :], ACT.Identity,
                                     bias=bq_scaled[:, slot:slot + 1], scale=scale).then_inc(qk_ready.sem, 1)

            def copy_k(u, slot):
                act.wait_ge(proj_filled.sem, proj_filled.at(u, 2))
                at = KD * QKV0 + 1
                nc.scalar.activation(kT[:, slot, :], c.bank[:, K, :], ACT.Identity,
                                     bias=w[:, slot, at:at + 1]).then_inc(qk_ready.sem, 1)

            def exponential(u, slot, i):
                act.wait_ge(max_ready.sem, max_ready.at(u, i + 1))
                width = (i + 1) * P
                nc.scalar.activation(probs[:, i, 0:width], c.bank[:, S0 + i % 2, 0:width], ACT.Exp,
                                     bias=neg_max[:, slot, i:i + 1],
                                     accum_out=total[:, slot, i:i + 1]).then_inc(exp_done.sem, 1)

            def start(b):
                norm.scalar(act, b, (TB, OTB))
                copy_q(b * H0, 0)
                copy_k(b * H0, 0)

            def copy_o(u, slot):
                act.wait_ge(ot_filled.sem, ot_filled.at(u, 1))
                nc.scalar.copy(oT[:, slot, :], c.bank[:, OTB, :]).then_inc(ot_ready.sem, 1)

            def unit(g, slot, first, last):
                u = g * 2 + slot
                exponential(u, slot, 0)
                exponential(u, slot, 1)
                if not last:
                    copy_q(u + 1, 1 - slot)
                if not first:
                    copy_o(u + -1, 1 - slot)
                exponential(u, slot, 2)
                if not last:
                    copy_k(u + 1, 1 - slot)
                exponential(u, slot, 3)

            act.sem_inc(qk_ready.sem, 4)
            each_turn(act, start, unit, lambda b: copy_o(b * H0 + (H0 - 1), 1))

        @block.vector
        def _(dve):
            def scale_bias(g, slot, u):
                dve.wait_ge(w_loaded[slot].sem, w_loaded[slot].at(g, 16))
                nc.vector.tensor_scalar_mul(bq_scaled[:, slot:slot + 1], w[:, slot, KD * QKV0:KD * QKV0 + 1],
                                            scale).then_inc(bq_ready.sem, 1)

            def copy_v(u, slot):
                dve.wait_ge(proj_filled.sem, proj_filled.at(u, 3))
                bias = w[:, slot, KD * QKV0 + 2:PACK0].rearrange("p (a n) -> p a n", a=1)
                nc.vector.tensor_tensor(v[:, slot, :, :], c.bank[:, QV, :].rearrange("p (t n) -> p t n", t=NT),
                                        bias.broadcast_to([P, NT, DH0]), ALU.add).then_inc(v_ready.sem, 1)

            def maximum(u, slot, i):
                dve.wait_ge(s_filled.sem, s_filled.at(u, i + 1))
                nc.vector.tensor_reduce(neg_max[:, slot, i:i + 1], c.bank[:, S0 + i % 2, 0:(i + 1) * P],
                                        axis=AX.X, op=ALU.max, negate=True).then_inc(max_ready.sem, 1)

            def normalise(u, slot, i):
                dve.wait_ge(exp_done.sem, exp_done.at(u, i + 1))
                nc.vector.reciprocal(rinv[:, slot, i:i + 1], total[:, slot, i:i + 1]).then_inc(rinv_ready.sem, 1)
                dve.wait_ge(rinv_ready.sem, rinv_ready.at(u, i + 1))
                row = probs[:, i, 0:(i + 1) * P]
                nc.vector.tensor_scalar(row, row, rinv[:, slot, i:i + 1], None, ALU.mult).then_inc(p_ready.sem, 1)

            def copy_pT(u, slot, i):
                dve.wait_ge(t_filled.sem, t_filled.at(u, i + 1))
                nc.vector.tensor_copy(pT[:, slot, 0:i + 1, i * P:(i + 1) * P],
                                      c.bank[:, TB, 0:(i + 1) * P].rearrange("p (j q) -> p j q", q=P))\
                  .then_inc(pt_ready.sem, 1)

            def start(b):
                scale_bias(b * pairs, 0, b * H0)
                copy_v(b * H0, 0)

            def unit(g, slot, first, last):
                u = g * 2 + slot
                maximum(u, slot, 0)
                maximum(u, slot, 1)
                if not first:
                    copy_pT(u + -1, 1 - slot, NT - 1)
                if not last:
                    scale_bias(*following(g, slot), u + 1)
                normalise(u, slot, 0)
                copy_pT(u, slot, 0)
                maximum(u, slot, 2)
                normalise(u, slot, 1)
                copy_pT(u, slot, 1)
                maximum(u, slot, 3)
                normalise(u, slot, 2)
                copy_pT(u, slot, 2)
                normalise(u, slot, 3)
                if not last:
                    copy_v(u + 1, 1 - slot)

            def end(b):
                norm.moments(dve, b + 1)
                norm.rows(dve, b + 1)
                copy_pT(b * H0 + (H0 - 1), 1, NT - 1)
                dve.wait_ge(head_added.sem, head_added.at(b * H0, H0))
                for half in range(2):
                    xs = c.x_cols(b, half * 512, 512)
                    last = nc.vector.tensor_tensor(xs, xs, c.bank[:, Y0 + half, :], ALU.add)
                last.then_inc(y_added.sem, 1)

            dve.sem_inc(y_added.sem, 1)
            dve.sem_inc(v_ready.sem, 2)
            norm.moments(dve, 0)
            norm.rows(dve, 0)
            each_turn(dve, start, unit, end)

        @block.gpsimd
        def _(pool):
            pool.sem_inc(head_added.sem, 2)
            norm.pool(pool, 0)
            with pool.Fori(0, B) as b:
                with pool.Fori(0, pairs) as pair:
                    for slot in (0, 1):
                        head = pool.snap(pair * 2 + slot)
                        pool.wait_ge(head_added.sem, head_added.at((b * pairs + pair) * 2 + slot, -1))
                        pool.dma_start(wo[:, slot, :], wo_dram[bass.ds(head, 1)]
                                       .rearrange("a p n -> p (a n)")).then_inc(wo_loaded[slot].sem, 16)
                norm.pool(pool, b + 1)
    norm.end()
    y_added.end(B)
    bo_loaded.end(1)
    for s in (*w_loaded, *wo_loaded):
        s.end(B * pairs)
    for s in (bq_ready, proj_filled, qk_ready, v_ready, s_filled, max_ready, exp_done, rinv_ready,
              p_ready, t_filled, pt_ready, ot_filled, ot_ready, head_added):
        s.end(B * H0)


def build_small_attention(c, kind, ins):
    nc = c.nc
    two = kind != "rope"
    QH = ins[f"{kind}_wq"].shape[-1]
    KH = ins[f"{kind}_wk"].shape[-1]
    VH = ins[f"{kind}_wv"].shape[-1]
    kv_repeat = D // VH
    dk = KH // H1
    cells = H1 * NT
    group_cells = HG * NT
    norm = Norm(c)

    wide = lambda n: [0, 1] if n == D else [0]
    plan = [("q", i) for i in wide(QH)] + [("k", i) for i in wide(KH)]
    if kind == "splat":
        plan += [("qf", 0), ("qf", 1), ("kf", 0), ("kf", 1)]
    plan += [("v", i) for i in wide(VH)]
    stacks_of = lambda what: [(f"{what} stack", h) for h in range(H1)]
    if kind == "rope":
        plan += stacks_of("q") + stacks_of("k")
    elif kind == "differential":
        plan += stacks_of("q") + stacks_of("k") + stacks_of("k2")
    else:
        plan += stacks_of("q") + stacks_of("k") + stacks_of("qf") + stacks_of("kf")
    splits = ("q", "k", "qf", "kf") if kind == "splat" else ("q", "k")

    def owner_of(s):
        what, part = plan[s]
        if what.endswith("stack"):
            busy = what == "q stack" or kind == "splat" and what != "kf stack"
            first = 0 if not busy else 11 if kind == "splat" else H1
            return "vector" if part % 2 and part >= first else "scalar"
        if what == "v":
            return "vector" if kind == "differential" else "scalar"
        return "scalar" if kind == "splat" and what in ("q", "k") else "vector"

    owner = [owner_of(s) for s in range(len(plan))]

    def bank_of(s):
        return 4 + s % 4

    def drains_up_to(s, eng):
        return sum(1 for o in owner[:s + 1] if o == eng)

    rows_filled = c.counter("rows_filled", len(plan))
    drained = {e: c.counter(f"rows_drained_{e}", drains_up_to(len(plan), e)) for e in ("scalar", "vector")}
    loads = {"differential": ("wq", "wk", "wv", "wo", "bq", "bk", "bv", "bo", "lam", "gsub"),
             "splat": ("wq", "wk", "wv", "wo", "pos", "dir", "logs", "blocks", "wq_out", "wk_out", "scal"),
             "rope": ("wq", "wk", "wv", "wo", "cos", "sin")}[kind]
    loaded = {n: c.counter(f"small_loaded_{i}", 16) for i, n in enumerate(loads)}
    zeroed = c.counter("small_zeroed", 2)
    chain = Chain(c, "small_chain")
    split_ready = c.counter("small_split_ready", len(splits))
    feature_w_filled = c.counter("small_feature_w_filled", 1)
    feature_w_ready = c.counter("small_feature_w_ready", 1)
    sums_ready = c.counter("small_sums_ready", 1)
    setup_exp = c.counter("small_setup_exp", 1)
    args_ready = c.counter("small_args_ready", 1)
    features = c.counter("small_features", 1)
    s_filled = [c.counter(f"small_s{m}_filled", cells) for m in range(2)]
    max_ready = [c.counter(f"small_max{m}_ready", cells) for m in range(2)]
    exp_done = [c.counter(f"small_exp{m}_done", cells) for m in range(2)]
    inv_ready = c.counter("small_inv_ready", 2 * cells)
    kappa_ready = c.counter("small_kappa_ready", 1)
    weight_ready = c.counter("small_weight_ready", cells)
    p_ready = c.counter("small_p_ready", cells)
    t_filled = c.counter("small_t_filled", cells)
    copier = ["scalar" if two or n % NT >= NT - 2 else "vector" for n in range(cells)]
    copied = {e: c.counter(f"small_copied_{e}", copier.count(e)) for e in ("scalar", "vector")}
    ov_filled = c.counter("small_ov_filled", NG)
    ov_ready = c.counter("small_ov_ready", NG)
    or_filled = c.counter("small_or_filled", NG)
    or_read = c.counter("small_or_read", NG)
    group_done = c.counter("small_group_done", NG if kind == "differential" else 0)
    square_ready = c.counter("small_square_ready", NG)
    rms_ready = c.counter("small_rms_ready", NG * NT)
    ot_filled = c.counter("small_ot_filled", KD)
    ot_ready = c.counter("small_ot_ready", KD)
    y_filled = c.counter("small_y_filled", 2)
    y_added = c.counter("small_y_added", 1, credit=1)
    OV = OR = 6
    DEEP, T_BANKS = 2 if two else 4, (4, 5, 7)
    LAG, COPY_LAG = (3, 3) if two else (4, 3)
    MIX_LAG = 2
    NEXT_AT = group_cells + group_cells // 2
    VALUES_AT, STRIPS_AT, ROWS_AT, FINISH_AT, RMS_AT, AFTER = (LAG + 1 + n for n in (0, 3, 4, 4, 9, 10))
    with ExitStack() as ctx:
        sb = lambda name, shape, dt=F32: c.sb(f"{kind}_{name}", shape, dt, ctx=ctx)
        held = {n: sb(n, list(ins[f"{kind}_{n}"].shape)) for n in loads if n not in ("pos", "dir", "wq_out", "wk_out")}
        v_rows = sb("v_rows", [P, NT, VH // DH1, STRIP])
        ops = ("q", "k", "k2") if kind == "differential" else splits
        stack = {n: sb(f"{n}_stack", [P, H1, T], BF16) for n in ops}
        pT = sb("pT", [P, 2, HG, NT, T])
        ROWS = NT * H1 * DH1
        arena = [pT[:, i // HG, i % HG, :, :].rearrange("p a b -> p (a b)") for i in range(2 * HG)]

        def in_arena(i, half, d=DH1):
            flat = arena[i][:, half * ROWS:half * ROWS + NT * H1 * d]
            return flat.rearrange("p (t h d) -> p t h d", t=NT, d=d)

        q_rows, k_rows = in_arena(0, 0), in_arena(0, 1, dk)
        rest = arena[1][:, 0:ROWS]
        PAD = DH1 - dk
        part_of = [arena[1][:, ROWS:2 * ROWS].bitcast(BF16)[:, i * ROWS:(i + 1) * ROWS] for i in range(2)]
        part_of.append(sb("low_part", [P, ROWS], BF16))
        in_parts = lambda half: pT[:, 1, half:half + 2, :, :].rearrange("p j a b -> p (j a b)").bitcast(BF16) \
            .rearrange("p (t h d) -> p t h d", t=NT, d=P)
        parts = {"q": in_parts(0), "k": sb("k_parts", [P, NT, H1, PAD + P], BF16) if PAD else in_parts(2)}
        probs = [sb(f"probs{m}", [P, LAG + 1, T]) for m in range(1 + two)]
        neg_max = [sb(f"neg_max{m}", [P, cells]) for m in range(2)]
        total = [sb(f"total{m}", [P, cells]) for m in range(2)]
        inv = sb("inv", [P, cells])
        scaled_total = sb("scaled_total", [P, cells])
        weight = sb("weight", [P, cells])
        row_inv = sb("row_inv", [P, group_cells])
        ovT = sb("ovT", [P, T])
        attn = sb("attn", [P, NT, D])
        attnT = c.xnT
        if kind == "differential":
            square = sb("square", [P, NT, HG, DH1])
            mean_sq = sb("mean_sq", [P, NT, HG])
            rms = sb("rms", [P, NT, HG])
        if two:
            small = sb("small", [P, 8])
        if kind == "splat":
            half_p2, inv_norm, p_dir = (sb(n, [P, P]) for n in ("half_p2", "inv_norm", "p_dir"))
            half_q2 = sb("half_q2", [P, 2 * NT * H1])
            feature_rows = arena[2].rearrange("p (s t h d) -> p s t h d", s=2, t=NT, d=DH1)
            features_at = arena[3].rearrange("p (i s t h n) -> p i s t h n", i=2, s=2, t=NT, n=8)
            gauss, tilt = features_at[:, 0], features_at[:, 1]
            feature_w = sb("feature_w", [P, 2, KD, D])
            square = arena[7]
            raw_pos, raw_dir, work = arena[4], arena[5], arena[7]
            w_out = {f"w{n}_out": arena[i][:, 0:KD * D].rearrange("p (a b) -> p a b", a=KD) for i, n in enumerate("qk")}
        if kind == "rope":
            turned = [sb(f"turned{i}", [P, 2, H1, DH1]) for i in range(2)]
        block = ctx.enter_context(nc.Block())

        def head_of(n):
            return n // group_cells, n // NT % HG, n % NT

        @block.sync
        def _(sp):
            for n in loads:
                if n in ("pos", "dir"):
                    target = raw_pos if n == "pos" else raw_dir
                else:
                    target = w_out[n] if n in ("wq_out", "wk_out") else held[n][:]
                sp.dma_start(target, ins[f"{kind}_{n}"]).then_inc(loaded[n].sem, 16)

        @block.tensor
        def _(pe):
            def wait_drained(b, steps):
                for e in ("scalar", "vector"):
                    mine = [s for s in steps if owner[s] == e]
                    if mine:
                        pe.wait_ge(drained[e].sem, drained[e].at(b, drains_up_to(max(mine), e)))

            def project(s, what, part):
                w = feature_w[:, "qk".index(what[0])] if what in ("qf", "kf") else held[f"w{what}"]
                n = w.shape[-1]
                per_bank = 512 // n
                for t in range(part * per_bank, (part + 1) * per_bank):
                    at = (t % per_bank) * n
                    for k in range(KD):
                        last = nc.tensor.matmul(c.bank[:, bank_of(s), at:at + n], c.xnT[:, k, t * P:(t + 1) * P],
                                                w[:, k, :], start=(k == 0), stop=(k == KD - 1))
                return last

            def make_stack(s, what, h):
                at = PAD if what == "k" else 0
                for t in range(NT):
                    last = nc.tensor.matmul(c.bank[:, bank_of(s), t * P:(t + 1) * P], parts[what[0]][:, t, h, at:at + P],
                                            c.ident_bf[:, :], start=True, stop=True)
                return last

            def make_feature_weights():
                for n in ("wq_out", "wk_out", "blocks"):
                    pe.wait_ge(loaded[n].sem, loaded[n].at(0, 16))
                for side in range(2):
                    for k in range(KD):
                        for half in range(KD):
                            at = k * D + half * P
                            last = nc.tensor.matmul(c.bank[:, side, at:at + P],
                                                    w_out["wq_out" if side == 0 else "wk_out"][:, half, k * P:(k + 1) * P],
                                                    held["blocks"][:, half, :], start=True, stop=True)
                last.then_inc(feature_w_filled.sem, 1)

            def wait_copied(b, first, last):
                for e in ("scalar", "vector"):
                    if e in copier[first:last + 1]:
                        pe.wait_ge(copied[e].sem, copied[e].at(b, copier[:last + 1].count(e)))

            def fill(b, s):
                what, part = plan[s]
                source = what.split()[0]
                needs = [s - 4] if s >= 4 else []
                if what.endswith("stack") and part == 0 and source in splits:
                    pe.wait_ge(split_ready.sem, split_ready.at(b, splits.index(source) + 1))
                wait_drained(b, needs)
                if what.endswith("stack"):
                    return make_stack(s, source, part)
                return project(s, what, part)

            def scores(b, n):
                g, j, i = head_of(n)
                if n >= DEEP:
                    for m in range(1 + two):
                        pe.wait_ge(exp_done[m].sem, exp_done[m].at(b, n - DEEP + 1))
                width = (i + 1) * P
                h = g * HG + j
                for m in range(1 + two):
                    bank = 2 * m + n % DEEP
                    pairs = [("q", "k2" if kind == "differential" and m == 1 else "k")]
                    if kind == "splat" and m == 1:
                        pairs.append(("qf", "kf"))
                    for first, (q, k) in enumerate(pairs):
                        nc.tensor.matmul(c.bank[:, bank, 0:width], stack[q][:, h, i * P:width],
                                         stack[k][:, h, 0:width], start=(first == 0), stop=False)
                    nc.tensor.matmul(c.bank[:, bank, i * P:width], c.ident_bf[:, :], c.causal[:, :],
                                     start=False, stop=True).then_inc(s_filled[m].sem, 1)

            def transposes(b, n):
                ready = p_ready if two else exp_done[0]
                pe.wait_ge(ready.sem, ready.at(b, n + 1))
                if n >= len(T_BANKS):
                    wait_copied(b, n - len(T_BANKS), n - len(T_BANKS))
                for j in range(n % NT + 1):
                    last = nc.tensor.transpose(c.bank[:, T_BANKS[n % len(T_BANKS)], j * P:(j + 1) * P],
                                               probs[0][:, n % (LAG + 1), j * P:(j + 1) * P], c.ident[:, :])
                last.then_inc(t_filled.sem, 1)

            def values(b, g, key_tile):
                if key_tile == 0:
                    if g:
                        pe.wait_ge(or_read.sem, or_read.at(b, g))
                    wait_copied(b, g * group_cells, (g + 1) * group_cells - 1)
                for j in range(HG):
                    last = nc.tensor.matmul(c.bank[STRIP * j:STRIP * (j + 1), OV, key_tile * P:T],
                                            v_rows[:, key_tile, (g * HG + j) // kv_repeat, :],
                                            pT[:, g % 2, j, key_tile, key_tile * P:T],
                                            start=(key_tile == 0), stop=(key_tile == NT - 1))
                if key_tile == NT - 1:
                    last.then_inc(ov_filled.sem, 1)

            def values_by_row(b, g):
                pe.wait_ge(ov_ready.sem, ov_ready.at(b, g + 1))
                for t in range(NT):
                    last = nc.tensor.transpose(c.bank[:, OR, t * P:(t + 1) * P], ovT[:, t * P:(t + 1) * P],
                                               c.ident[:, :])
                last.then_inc(or_filled.sem, 1)

            for n in loads:
                if n in ("wq", "wk", "wv", "wo", "bo"):
                    pe.wait_ge(loaded[n].sem, loaded[n].at(0, 16))
            pe.wait_ge(zeroed.sem, zeroed.at(0, zeroed.per))
            if kind == "splat":
                make_feature_weights()
                pe.wait_ge(feature_w_ready.sem, feature_w_ready.at(0, 1))
            with pe.Fori(0, B) as b:
                pe.wait_ge(norm.xn_ready.sem, norm.xn_ready.at(b, NT))
                norm.tensor(pe, (0, 1))
                pe.wait_ge(norm.xT_ready.sem, norm.xT_ready.at(b, KD))
                for s in range(len(plan)):
                    if s == 2:
                        pe.wait_ge(y_added.sem, y_added.at(b, 0))
                    fill(b, s).then_inc(rows_filled.sem, 1)
                for e in ("scalar", "vector"):
                    pe.wait_ge(drained[e].sem, drained[e].at(b, drained[e].per))
                for n in range(cells + AFTER):
                    if n < cells:
                        scores(b, n)
                    if LAG <= n < cells + LAG:
                        transposes(b, n - LAG)
                    g, after = n // group_cells - 1, n % group_cells
                    if g >= 0 and VALUES_AT <= after < VALUES_AT + NT:
                        values(b, g, after - VALUES_AT)
                    if g >= 0 and after == ROWS_AT:
                        values_by_row(b, g)
                done = group_done if kind == "differential" else or_read
                pe.wait_ge(done.sem, done.at(b, NG))
                for k in range(KD):
                    for t in range(NT):
                        last = nc.tensor.transpose(c.bank[:, 4 + k, t * P:(t + 1) * P],
                                                   attn[:, t, k * P:(k + 1) * P], c.ident[:, :])
                    last.then_inc(ot_filled.sem, 1)
                pe.wait_ge(ot_ready.sem, ot_ready.at(b, KD))
                for half in range(2):
                    if "bo" in loads:
                        nc.tensor.matmul(c.bank[:, 6 + half, :], c.ones[:, :], held["bo"][:, :], start=True, stop=True)
                    for t in (2 * half, 2 * half + 1):
                        for k in range(KD):
                            last = nc.tensor.matmul(c.bank[:, 6 + half, (t % 2) * D:(t % 2 + 1) * D],
                                                    attnT[:, k, t * P:(t + 1) * P], held["wo"][:, k, :],
                                                    start=("bo" not in loads and k == 0), stop=(k == KD - 1),
                                                    skip_group_check=True)
                    last.then_inc(y_filled.sem, 1)

        def copy_pT(eng, b, n):
            g, j, i = head_of(n)
            eng.wait_ge(t_filled.sem, t_filled.at(b, n + 1))
            out = pT[:, g % 2, j, 0:i + 1, i * P:(i + 1) * P]
            bank = c.bank[:, T_BANKS[n % len(T_BANKS)], 0:(i + 1) * P].rearrange("p (k q) -> p k q", q=P)
            if copier[n] == "scalar":
                nc.scalar.copy(out, bank).then_inc(copied["scalar"].sem, 1)
            else:
                nc.vector.tensor_copy(out, bank).then_inc(copied["vector"].sem, 1)

        @block.scalar
        def _(act):
            def drain(b, s):
                what, part = plan[s]
                act.wait_ge(rows_filled.sem, rows_filled.at(b, s + 1))
                bank = c.bank[:, bank_of(s), :]
                if what.endswith("stack"):
                    out = stack[what.split()[0]][:, part, :]
                    return nc.scalar.copy(out, bank)
                rows = {"q": q_rows, "k": k_rows, "v": v_rows}[what]
                out = rows[:, 2 * part:2 * part + 2, :, 0:DH1]
                source = bank.rearrange("p (t h d) -> p t h d", t=2, d=DH1)
                if kind == "splat" and what != "v":
                    return nc.scalar.mul(out, source, 0.5)
                return nc.scalar.copy(out, source)

            def exponentials(b, n):
                width = (n % NT + 1) * P
                for m in range(1 + two):
                    act.wait_ge(max_ready[m].sem, max_ready[m].at(b, n + 1))
                    nc.scalar.activation(probs[m][:, n % (LAG + 1), 0:width], c.bank[:, 2 * m + n % DEEP, 0:width], ACT.Exp,
                                         bias=neg_max[m][:, n:n + 1],
                                         accum_out=total[m][:, n:n + 1]).then_inc(exp_done[m].sem, 1)

            if kind == "differential":
                act.wait_ge(sums_ready.sem, sums_ready.at(0, 1))
                nc.scalar.activation(small[:, 2:4], small[:, 0:2], ACT.Exp).then_inc(setup_exp.sem, 1)
            if kind == "splat":
                act.wait_ge(loaded["logs"].sem, loaded["logs"].at(0, 16))
                act.wait_ge(loaded["scal"].sem, loaded["scal"].at(0, 16))
                logs = held["logs"]
                nc.scalar.activation(logs[:, 0, :], logs[:, 0, :], ACT.Exp, scale=-2.0)
                nc.scalar.activation(logs[:, 1, :], logs[:, 1, :], ACT.Exp)
                nc.scalar.activation(small[:, 0:1], held["scal"][:, 2:3], ACT.Exp, scale=-1.0)
                act.wait_ge(sums_ready.sem, sums_ready.at(0, 1))
                nc.scalar.activation(inv_norm[:, :], inv_norm[:, :], ACT.Sqrt).then_inc(setup_exp.sem, 1)
            with act.Fori(0, B) as b:
                norm.scalar(act, b, (0, 1))
                for s in range(len(plan)):
                    if kind == "splat" and plan[s] == ("q stack", 0):
                        act.wait_ge(args_ready.sem, args_ready.at(b, 1))
                        nc.scalar.activation(gauss[:, :, :, :, :], gauss[:, :, :, :, :], ACT.Exp)
                        nc.scalar.activation(tilt[:, :, :, :, :], tilt[:, :, :, :, :], ACT.Tanh).then_inc(features.sem, 1)
                    if owner[s] == "scalar":
                        drain(b, s).then_inc(drained["scalar"].sem, 1)
                for n in range(cells + AFTER):
                    if n < cells:
                        exponentials(b, n)
                    if COPY_LAG <= n < cells + COPY_LAG and copier[n - COPY_LAG] == "scalar":
                        copy_pT(act, b, n - COPY_LAG)
                    g = n // group_cells - 1
                    if g >= 0 and n % group_cells == STRIPS_AT:
                        act.wait_ge(ov_filled.sem, ov_filled.at(b, g + 1))
                        nc.scalar.copy(ovT[:, :], c.bank[:, OV, :]).then_inc(ov_ready.sem, 1)
                for k in range(KD):
                    act.wait_ge(ot_filled.sem, ot_filled.at(b, k + 1))
                    nc.scalar.copy(attnT[:, k, :], c.bank[:, 4 + k, :]).then_inc(ot_ready.sem, 1)

        @block.vector
        def _(dve):
            link = lambda ins: chain.link(dve, ins)

            def setup_differential():
                for n in ("bq", "bk", "bv", "lam", "gsub"):
                    dve.wait_ge(loaded[n].sem, loaded[n].at(0, 16))
                lam = held["lam"]
                nc.vector.tensor_tensor(lam[:, 0, :], lam[:, 0, :], lam[:, 1, :], ALU.mult)
                link(nc.vector.tensor_tensor(lam[:, 2, :], lam[:, 2, :], lam[:, 3, :], ALU.mult))
                nc.vector.reduce_sum(small[:, 0:1], lam[:, 0, :], axis=AX.X)
                nc.vector.reduce_sum(small[:, 1:2], lam[:, 2, :], axis=AX.X).then_inc(sums_ready.sem, 1)
                nc.vector.tensor_scalar_mul(held["bq"][:, :], held["bq"][:, :], SCALE_DIFF)
                nc.vector.tensor_scalar_mul(held["gsub"][:, :], held["gsub"][:, :], 1.0 - LAMBDA_INIT)
                dve.wait_ge(setup_exp.sem, setup_exp.at(0, 1))
                link(nc.vector.tensor_tensor(small[:, 4:5], small[:, 3:4], small[:, 2:3], ALU.subtract))
                link(nc.vector.tensor_scalar_add(small[:, 5:6], small[:, 4:5], -LAMBDA_INIT))

            def setup_splat():
                for n in ("pos", "dir"):
                    dve.wait_ge(loaded[n].sem, loaded[n].at(0, 16))
                by_splat = work.rearrange("p (s d) -> p s d", d=DH1)
                link(nc.vector.tensor_tensor(work, raw_pos, raw_pos, ALU.mult))
                link(nc.vector.reduce_sum(half_p2[:, :], by_splat, axis=AX.X))
                link(nc.vector.tensor_scalar_mul(half_p2[:, :], half_p2[:, :], 0.5))
                link(nc.vector.tensor_tensor(work, raw_pos, raw_dir, ALU.mult))
                link(nc.vector.reduce_sum(p_dir[:, :], by_splat, axis=AX.X))
                link(nc.vector.tensor_tensor(work, raw_dir, raw_dir, ALU.mult))
                nc.vector.reduce_sum(inv_norm[:, :], by_splat, axis=AX.X).then_inc(sums_ready.sem, 1)
                dve.wait_ge(setup_exp.sem, setup_exp.at(0, 1))
                link(nc.vector.tensor_scalar_add(inv_norm[:, :], inv_norm[:, :], 1e-8))
                dve.wait_ge(feature_w_filled.sem, feature_w_filled.at(0, 1))
                for side in range(2):
                    last = nc.vector.tensor_copy(feature_w[:, side, :, :].rearrange("p a b -> p (a b)"), c.bank[:, side, :])
                last.then_inc(feature_w_ready.sem, 1)
                nc.vector.reciprocal(inv_norm[:, :], inv_norm[:, :])
                nc.vector.tensor_scalar(held["logs"][:, 1, :], held["logs"][:, 1, :], held["scal"][:, 1:2], None, ALU.mult)
                link(nc.vector.tensor_scalar_add(small[:, 1:2], small[:, 0:1], 1.0))
                link(nc.vector.reciprocal(small[:, 2:3], small[:, 1:2]))
                link(nc.vector.tensor_scalar(small[:, 3:4], small[:, 2:3], 0.15, 0.03, ALU.mult, ALU.min))
                link(nc.vector.tensor_scalar(small[:, 4:5], small[:, 3:4], -1.0, 1.0, ALU.mult, ALU.add))
                link(nc.vector.reciprocal(small[:, 6:7], small[:, 4:5]))
                link(nc.vector.tensor_tensor(small[:, 5:6], small[:, 6:7], small[:, 3:4], ALU.mult))

            def drain_biased(what, part, bank):
                rows = {"q": q_rows, "k": k_rows, "v": v_rows}[what]
                width, d = {"q": (QH, DH1), "k": (KH, dk), "v": (VH, DH1)}[what]
                n = 512 // width
                out = rows[:, n * part:n * (part + 1), :, 0:d]
                src = bank.rearrange("p (t h d) -> p t h d", t=n, d=d)
                bias = held["b" + what][:, :].rearrange("p (a h d) -> p a h d", a=1, d=d).broadcast_to([P, n, width // d, d])
                if what == "q":
                    for t in range(n):
                        last = nc.vector.scalar_tensor_tensor(out[:, t], src[:, t], SCALE_DIFF, bias[:, t], ALU.mult, ALU.add)
                    return last
                return nc.vector.tensor_tensor(out, src, bias, ALU.add)

            def drain_rotated(b, what, part, bank):
                rows = {"q": q_rows, "k": k_rows}[what]
                cos = held["cos"][:, "qk".index(what), 2 * part:2 * part + 2, :]
                sin = held["sin"][:, "qk".index(what), 2 * part:2 * part + 2, :]
                before = {"q": 0, "k": 2}[what] + part
                if before:
                    dve.wait_ge(drained["vector"].sem, drained["vector"].at(b, before))
                pairs = bank.rearrange("p (t h d e) -> p t h d e", t=2, d=DH1 // 2, e=2)
                wide = lambda a: a.rearrange("p t (a d) -> p t a d", a=1).broadcast_to([P, 2, H1, DH1 // 2])
                even, odd = pairs[:, :, :, :, 0], pairs[:, :, :, :, 1]
                for t in range(2):
                    sub = lambda a: a[:, t]
                    nc.vector.tensor_tensor(turned[0][:, t, :, 0:8], sub(even), sub(wide(cos)), ALU.mult)
                    nc.vector.tensor_tensor(turned[0][:, t, :, 8:16], sub(even), sub(wide(sin)), ALU.mult)
                    nc.vector.tensor_tensor(turned[1][:, t, :, 0:8], sub(odd), sub(wide(sin)), ALU.mult)
                    last = nc.vector.tensor_tensor(turned[1][:, t, :, 8:16], sub(odd), sub(wide(cos)), ALU.mult)
                link(last)
                out = rows[:, 2 * part:2 * part + 2, :, 0:DH1].rearrange("p t h (d e) -> p t h d e", e=2)
                nc.vector.tensor_tensor(out[:, :, :, :, 0], turned[0][:, :, :, 0:8], turned[1][:, :, :, 0:8], ALU.subtract)
                return nc.vector.tensor_tensor(out[:, :, :, :, 1], turned[0][:, :, :, 8:16], turned[1][:, :, :, 8:16], ALU.add)

            all_rows = lambda a: a.rearrange("p s t h n -> p (s t h) n")
            per_splat = lambda a: a.rearrange("p (a n) -> p a n", a=1).broadcast_to([P, 2 * NT, H1 * 8])
            by_tile = lambda a: a.rearrange("p s t h n -> p (s t) (h n)")

            def squares(b):
                dve.wait_ge(drained["scalar"].sem, drained["scalar"].at(b, 4))
                link(nc.vector.tensor_tensor(square, arena[0], arena[0], ALU.mult))
                link(nc.vector.reduce_sum(half_q2[:, :], square.rearrange("p (u d) -> p u d", d=DH1), axis=AX.X))
                link(nc.vector.tensor_scalar_mul(half_q2[:, :], half_q2[:, :], 2.0))

            def take_products(b, s):
                dve.wait_ge(rows_filled.sem, rows_filled.at(b, s + 1))
                side, first = "qk".index(plan[s][0][0]), bank_of(s) - 1
                products = c.bank[:, first:first + 2, :].rearrange("p a (u n) -> p (a u) n", n=16)
                rows = slice(side * NT * H1, (side + 1) * NT * H1)
                half = half_q2[:, rows].rearrange("p (u a) -> p u a", a=1).broadcast_to([P, NT * H1, 8])
                nc.vector.tensor_tensor(all_rows(gauss)[:, rows, :], products[:, :, 0:8], half, ALU.subtract)
                nc.vector.tensor_copy(all_rows(tilt)[:, rows, :], products[:, :, 8:16]).then_inc(drained["vector"].sem, 2)

            def arguments(b):
                dve.wait_ge(drained["vector"].sem, drained["vector"].at(b, 4))
                link(nc.vector.tensor_tensor(by_tile(gauss), by_tile(gauss), per_splat(half_p2[:, :]), ALU.subtract))
                link(nc.vector.tensor_tensor(by_tile(tilt), by_tile(tilt), per_splat(p_dir[:, :]), ALU.subtract))
                nc.vector.tensor_tensor(by_tile(gauss), by_tile(gauss), per_splat(held["logs"][:, 0, :]), ALU.mult)
                nc.vector.tensor_tensor(by_tile(tilt), by_tile(tilt), per_splat(inv_norm[:, :]),
                                        ALU.mult).then_inc(args_ready.sem, 1)

            def make_features(b):
                near, toward = (feature_rows[:, :, :, :, i * 8:(i + 1) * 8] for i in range(2))
                dve.wait_ge(features.sem, features.at(b, 1))
                for t in range(NT):
                    last = nc.vector.tensor_tensor(near[:, 0, t], gauss[:, 0, t],
                                                   held["logs"][:, 1, :].rearrange("p (h n) -> p h n", n=8), ALU.mult)
                link(last)
                flat = lambda a: a.rearrange("p t h n -> p (t h) n")
                nc.vector.scalar_tensor_tensor(flat(toward[:, 0]), flat(near[:, 0]), held["scal"][:, 0:1],
                                               flat(tilt[:, 0]), ALU.mult, ALU.mult)
                nc.vector.tensor_copy(flat(near[:, 1]), flat(gauss[:, 1]))
                link(nc.vector.tensor_tensor(flat(toward[:, 1]), flat(gauss[:, 1]), flat(tilt[:, 1]), ALU.mult))

            def split(b, what, source):
                side = what[0]
                d = dk if side == "k" else DH1
                if splits.index(what):
                    dve.wait_ge(split_ready.sem, split_ready.at(b, splits.index(what)))
                source = source.rearrange("p t h d -> p (t h) d")
                compact = lambda a: a[:, 0:NT * H1 * d].rearrange("p (u d) -> p u d", d=d)
                left, (high, middle, low) = compact(rest), map(compact, part_of)
                link(nc.vector.tensor_copy(high, source))
                link(nc.vector.tensor_tensor(left, source, high, ALU.subtract))
                link(nc.vector.tensor_copy(middle, left))
                link(nc.vector.tensor_tensor(low, left, middle, ALU.subtract))
                at = PAD if side == "k" else 0
                places = parts[side][:, :, :, at:at + P].rearrange("p t h (c d) -> p (t h) c d", d=DH1)
                for i, part in enumerate((high, middle, low)):
                    for place in [n for n in range(8) if (n % 3 if side == "k" else n // 3) == i]:
                        last = nc.vector.tensor_copy(places[:, :, place, 0:d], part)
                last.then_inc(split_ready.sem, 1)

            def drain(b, s):
                what, part = plan[s]
                dve.wait_ge(rows_filled.sem, rows_filled.at(b, s + 1))
                bank = c.bank[:, bank_of(s), :]
                if what.endswith("stack"):
                    out = stack[what.split()[0]][:, part, :]
                    return nc.vector.tensor_copy(out, bank)
                return drain_rotated(b, what, part, bank) if kind == "rope" else drain_biased(what, part, bank)

            def maximum(b, n, m):
                dve.wait_ge(s_filled[m].sem, s_filled[m].at(b, n + 1))
                nc.vector.tensor_reduce(neg_max[m][:, n:n + 1], c.bank[:, 2 * m + n % DEEP, 0:(n % NT + 1) * P],
                                        axis=AX.X, op=ALU.max, negate=True).then_inc(max_ready[m].sem, 1)

            def mix(b, n):
                dve.wait_ge(weight_ready.sem, weight_ready.at(b, n + 1))
                p0, p1 = (probs[m][:, n % (LAG + 1), 0:(n % NT + 1) * P] for m in range(2))
                nc.vector.scalar_tensor_tensor(p0, p1, weight[:, n:n + 1], p0, ALU.mult, ALU.add).then_inc(p_ready.sem, 1)

            def attn_of(g):
                return attn[:, :, g * HG * DH1:(g + 1) * HG * DH1].rearrange("p t (h d) -> p t h d", d=DH1)

            def finish_group(b, g):
                cols = slice(g * group_cells, (g + 1) * group_cells)
                dve.wait_ge(or_filled.sem, or_filled.at(b, g + 1))
                link(nc.vector.reciprocal(row_inv[:, :], total[0][:, cols]))
                if kind == "splat":
                    link(nc.vector.tensor_scalar(row_inv[:, :], row_inv[:, :], small[:, 4:5], None, ALU.mult))
                out = attn_of(g)
                rows = c.bank[:, OR, :].rearrange("p (t h d) -> p t h d", t=NT, d=STRIP)[:, :, :, 0:DH1]
                scale = row_inv[:, :].rearrange("p (h t a) -> p t h a", t=NT, a=1).broadcast_to([P, NT, HG, DH1])
                nc.vector.tensor_tensor(out, rows, scale, ALU.mult).then_inc(or_read.sem, 1)
                if kind != "differential":
                    return
                dve.wait_ge(or_read.sem, or_read.at(b, g + 1))
                link(nc.vector.tensor_tensor(square[:, :, :, :], out, out, ALU.mult))
                link(nc.vector.tensor_reduce(mean_sq[:, :, :], square[:, :, :, :], axis=AX.X, op=ALU.add))
                nc.vector.tensor_scalar(mean_sq[:, :, :], mean_sq[:, :, :], 1.0 / DH1, RMS_EPS,
                                        ALU.mult, ALU.add).then_inc(square_ready.sem, 1)
                for_each = held["gsub"][:, :].rearrange("p (a d) -> p a d", a=1).broadcast_to([P, HG, DH1])
                for t in range(NT):
                    last = nc.vector.tensor_tensor(out[:, t], out[:, t], for_each, ALU.mult)
                link(last)

            def apply_rms(b, g):
                out = attn_of(g)
                dve.wait_ge(rms_ready.sem, rms_ready.at(b, NT * (g + 1)))
                nc.vector.tensor_tensor(out, out, rms[:, :, :].rearrange("p t (h a) -> p t h a", a=1)
                                        .broadcast_to([P, NT, HG, DH1]), ALU.mult).then_inc(group_done.sem, 1)

            nc.vector.memset((parts["k"] if PAD else c.wait_mark)[:], 0.0).then_inc(zeroed.sem, 1)
            nc.vector.memset(v_rows[:, :, :, :], 0.0).then_inc(zeroed.sem, 1)
            dve.wait_ge(zeroed.sem, zeroed.at(0, 2))
            if kind == "differential":
                setup_differential()
            elif kind == "splat":
                setup_splat()
            else:
                for n in ("cos", "sin"):
                    dve.wait_ge(loaded[n].sem, loaded[n].at(0, 16))
            if two:
                nc.vector.memset(c.wait_mark[:, :], 0.0).then_inc(kappa_ready.sem, 1)
            norm.moments(dve, 0)
            norm.rows(dve, 0)
            dve.sem_inc(y_added.sem, 1)
            chain.begin_loop(dve)
            with dve.Fori(0, B) as b:
                chain.turn(b)
                for s in range(len(plan)):
                    what, part = plan[s]
                    if what in ("qf", "kf"):
                        if part == 1:
                            take_products(b, s)
                    elif owner[s] == "vector":
                        drain(b, s).then_inc(drained["vector"].sem, 1)
                    if kind == "splat":
                        if (what, part) == ("q", 1):
                            dve.wait_ge(drained["scalar"].sem, drained["scalar"].at(b, 2))
                            split(b, "q", q_rows)
                        if (what, part) == ("k", 1):
                            squares(b)
                        if (what, part) == ("kf", 1):
                            arguments(b)
                            split(b, "k", k_rows)
                            make_features(b)
                        if what == "q stack" and part == H1 - 1:
                            split(b, "qf", feature_rows[:, 0])
                        if what == "k stack" and part == H1 - 1:
                            split(b, "kf", feature_rows[:, 1])
                    else:
                        ready = {"q": "q", "v": "k"}.get(what)
                        if ready and plan[s + 1][0] != what:
                            dve.wait_ge(drained["vector"].sem, drained["vector"].at(b, drains_up_to(s, "vector")))
                            split(b, ready, {"q": q_rows, "k": k_rows}[ready])
                for n in range(cells + AFTER):
                    if n == NEXT_AT:
                        norm.moments(dve, b + 1)
                    if n == NEXT_AT + 2:
                        norm.rows(dve, b + 1)
                    if n < cells:
                        maximum(b, n, 0)
                    if two and n < cells:
                        maximum(b, n, 1)
                    if two and MIX_LAG <= n < cells + MIX_LAG:
                        mix(b, n - MIX_LAG)
                    if COPY_LAG <= n < cells + COPY_LAG and copier[n - COPY_LAG] == "vector":
                        copy_pT(dve, b, n - COPY_LAG)
                    g, after = n // group_cells - 1, n % group_cells
                    if g >= 0 and after == FINISH_AT:
                        finish_group(b, g)
                    if g >= 0 and after == RMS_AT and kind == "differential":
                        apply_rms(b, g)
                for half in range(2):
                    dve.wait_ge(y_filled.sem, y_filled.at(b, half + 1))
                    xs = c.x_cols(b, half * 512, 512)
                    last = nc.vector.tensor_tensor(xs, xs, c.bank[:, 6 + half, :], ALU.add)
                last.then_inc(y_added.sem, 1)
                chain.top_up(dve)

        @block.gpsimd
        def _(pool):
            def weigh(b, n):
                pool.wait_ge(exp_done[1].sem, exp_done[1].at(b, n + 1))
                nc.gpsimd.tensor_tensor(inv[:, n:n + 1], total[1][:, n:n + 1], c.minus_one[:, :], ALU.pow)\
                  .then_inc(inv_ready.sem, 1)
                nc.gpsimd.tensor_tensor(scaled_total[:, n:n + 1], total[0][:, n:n + 1], small[:, 5:6], ALU.mult)\
                  .then_inc(inv_ready.sem, 1)
                pool.wait_ge(inv_ready.sem, inv_ready.at(b, 2 * n + 2))
                nc.gpsimd.tensor_tensor(weight[:, n:n + 1], inv[:, n:n + 1], scaled_total[:, n:n + 1], ALU.mult)\
                  .then_inc(weight_ready.sem, 1)

            if two:
                pool.wait_ge(kappa_ready.sem, kappa_ready.at(0, 1))
            norm.pool(pool, 0)
            with pool.Fori(0, B) as b:
                for n in range(cells + AFTER):
                    if n == NEXT_AT:
                        norm.pool(pool, b + 1)
                    if two and n < cells:
                        weigh(b, n)
                    g, t = n // group_cells - 1, n % group_cells - FINISH_AT
                    if kind == "differential" and g >= 0 and 0 <= t < NT:
                        pool.wait_ge(square_ready.sem, square_ready.at(b, g + 1))
                        nc.gpsimd.tensor_tensor(rms[:, t, :], mean_sq[:, t, :], c.minus_half[:, 0:HG],
                                                ALU.pow).then_inc(rms_ready.sem, 1)
    norm.end()
    chain.end(B)
    for s in (*loaded.values(), zeroed):
        s.end(1)
    split_ready.end(B)
    if kind == "splat":
        feature_w_filled.end(1)
        feature_w_ready.end(1)
    if two:
        kappa_ready.end(1)
        sums_ready.end(1)
        setup_exp.end(1)
    if kind == "splat":
        for s in (args_ready, features):
            s.end(B)
    if kind == "differential":
        for s in (square_ready, rms_ready):
            s.end(B)
    for s in (s_filled[1], max_ready[1], exp_done[1], inv_ready, weight_ready, p_ready):
        if two:
            s.end(B)
    for s in (rows_filled, *drained.values(), s_filled[0], max_ready[0], exp_done[0], t_filled, *copied.values(),
              ov_filled, ov_ready, or_filled, or_read, group_done, ot_filled, ot_ready, y_filled, y_added):
        s.end(B)


E_ALL, F, K, R, TOPK = 64, 8, 8, 8, 6
I = 176
KR = K * R
TAIL = I - P
UP = 2 * I
AT = {}
for _name, _width in (("w1", KD * (UP + 2 * KR)), ("qb", UP), ("qb_scale", UP), ("mu", D), ("down", D + KR),
                      ("qa_tail", KR), ("low", D), ("low_scale", D)):
    AT[_name] = sum(w for _, w in AT.values()), _width
PACK_E = sum(w for _, w in AT.values())


def build_moe(c, ins):
    nc = c.nc
    tiles = B * NT
    units = 2 * B
    turns = F // 2 + 1
    loaded = {n: c.counter(f"moe_loaded_{i}", 16) for i, n in enumerate(("gate", "map"))}
    w_loaded = [c.counter(f"moe_w_loaded{p}", 16) for p in range(2)]
    chain = Chain(c, "moe_chain")
    index_ready, pick_ready = c.counter("moe_index_ready", 1), c.counter("moe_pick_ready", 1)
    xT_filled, xT_ready = c.counter("moe_xT_filled", B * KD), c.counter("moe_xT_ready", B * KD)
    logits_filled = c.counter("moe_logits_filled", B)
    arg_ready, exp_done = c.counter("moe_arg_ready", 2), c.counter("moe_exp_done", 2)
    dense_ready, soft_ready = c.counter("moe_dense_ready", 1), c.counter("moe_soft_ready", 1)
    denseT_filled, denseT_ready = c.counter("moe_denseT_filled", B), c.counter("moe_denseT_ready", B)
    flat_filled = c.counter("moe_flat_filled", 1)
    softT_filled, softT_ready = c.counter("moe_softT_filled", B), c.counter("moe_softT_ready", B)
    scaled = c.counter("moe_scaled", 2)
    sig = {n: c.counter(f"moe_{n}", per * units, credit=int(n == "y_added")) for n, per in (
        ("xe_filled", 1), ("xe_ready", 1), ("a_filled", 1), ("aw_ready", 1), ("aT_filled", 1), ("aT_ready", 1),
        ("gu_filled", NT), ("silu_done", NT), ("h_ready", NT), ("hT_filled", 1), ("hT_ready", 1),
        ("a2_filled", 1), ("aw2_ready", 1), ("tailT_filled", 1), ("tailT_ready", 1), ("y_filled", 1), ("y_added", 1))}
    XB, AB, TB, GB, HB = 0, 2, 3, 4, 6
    with ExitStack() as ctx:
        sb = lambda name, shape, dt=F32: c.sb(f"moe_{name}", shape, dt, ctx=ctx)
        w = sb("w", [P, 2, PACK_E])
        gate = sb("gate", [P, KD, E_ALL])
        mapping = sb("mapping", [E_ALL, E_ALL], I32)
        entry = sb("entry", [E_ALL, E_ALL])
        negative = sb("negative", [E_ALL, E_ALL])
        index = sb("index", [E_ALL, 1], I32)
        index_f = sb("index_f", [E_ALL, 1])
        pick = sb("pick", [E_ALL, E_ALL])
        xT = sb("xT", [P, KD, B * T])
        norm = NormAll(c, ctx)
        soft = sb("soft", [P, tiles, E_ALL])
        share = sb("share", [P, tiles, F])
        softT = sb("softT", [E_ALL, B * T])
        score = sb("score", [P, tiles, E_ALL + 2])
        rest = sb("rest", [P, tiles, E_ALL + 2])
        dense = sb("dense", [P, tiles, E_ALL])
        denseT = sb("denseT", [E_ALL, B * T])
        row = sb("row", [P, tiles * F])
        row2 = sb("row2", [P, tiles * F])
        top8 = sb("top8", [P, tiles, 8])
        xeT = sb("xeT", [P, 2, KD, T])
        aw = sb("aw", [P, NT, 2 * KR])
        awT = sb("awT", [P, 2, T])
        silu = sb("silu", [P, NT, I])
        inner = sb("inner", [P, 2, NT, KR + I])
        hT = sb("hT", [P, 2, T])
        hT_tail = sb("hT_tail", [TAIL, 2, T])
        tailT = sb("tailT", [KR + TAIL, 2, T])
        block = ctx.enter_context(nc.Block())

        def cols(slot, name, rows=P, start=0, n=None):
            at, width = AT[name]
            return w[0:rows, slot, at + start:at + (width if n is None else start + n)]

        def unit_of(u):
            return u // B, u % B

        @block.sync
        def _(sp):
            sp.dma_start(gate[:, :, :], ins["moe_gate"]).then_inc(loaded["gate"].sem, 16)
            sp.dma_start(mapping[:, :], ins["moe_map"]).then_inc(loaded["map"].sem, 16)
            for slot in range(2):
                sp.dma_start(w[:, slot, :], ins["moe_w"][slot]).then_inc(w_loaded[slot].sem, 16)
            with sp.Fori(1, turns) as turn:
                for slot in range(2):
                    expert = sp.snap(turn * 2 + slot)
                    y = sig["y_filled"]
                    sp.wait_ge(y.sem, y.at(turn, -units + (slot + 1) * B))
                    sp.dma_start(w[:, slot, :], ins["moe_w"][bass.ds(expert, 1)].rearrange("a p n -> p (a n)"))\
                      .then_inc(w_loaded[slot].sem, 16)

        @block.gpsimd
        def _(pool):
            nc.gpsimd.iota(index[:, :], pattern=[[0, 1]], base=0, channel_multiplier=1).then_inc(index_ready.sem, 1)
            norm.pool(pool)

        @block.tensor
        def _(pe):
            def transpose_x(b):
                pe.wait_ge(norm.xn_ready.sem, norm.xn_ready.at(0, (b + 1) * NT))
                if b >= 2:
                    pe.wait_ge(xT_ready.sem, xT_ready.at(0, (b - 1) * KD))
                for k in range(KD):
                    for t in range(NT):
                        last = nc.tensor.transpose(c.bank[:, 4 * (b % 2) + k, t * P:(t + 1) * P],
                                                   norm.xn[:, b * NT + t, k * P:(k + 1) * P], c.ident[:, :])
                    last.then_inc(xT_filled.sem, 1)

            def logits(b):
                pe.wait_ge(xT_ready.sem, xT_ready.at(0, (b + 1) * KD))
                for t in range(b * NT, (b + 1) * NT):
                    for k in range(KD):
                        last = nc.tensor.matmul(by_tile(t), xT[:, k, t * P:(t + 1) * P], gate[:, k, :],
                                                start=(k == 0), stop=(k == KD - 1))
                last.then_inc(logits_filled.sem, 1)

            def by_tile(t):
                at = t % (2 * NT) * E_ALL
                return c.bank[:, 2 + t // (2 * NT), at:at + E_ALL]

            def transpose_entries(source, filled):
                for t in range(tiles):
                    mm = nc.tensor.matmul(c.bank[0:E_ALL, 4 + t // NT, t % NT * P:(t % NT + 1) * P], source[:, t, :],
                                          c.ident[:, :], start=True, stop=True)
                    if t % NT == NT - 1:
                        mm.then_inc(filled.sem, 1)

            def route():
                for b in range(B + 1):
                    if b < B:
                        transpose_x(b)
                    if b:
                        logits(b - 1)
                pe.wait_ge(dense_ready.sem, dense_ready.at(0, 1))
                transpose_entries(dense, denseT_filled)
                pe.wait_ge(pick_ready.sem, pick_ready.at(0, 1))
                for t in range(tiles):
                    if t % NT == 0:
                        pe.wait_ge(denseT_ready.sem, denseT_ready.at(0, t // NT + 1))
                    last = nc.tensor.matmul(by_tile(t), denseT[:, t * P:(t + 1) * P], pick[:, :], start=True, stop=True)
                last.then_inc(flat_filled.sem, 1)
                pe.wait_ge(soft_ready.sem, soft_ready.at(0, 1))
                transpose_entries(soft, softT_filled)

            def experts(turn, routed):
                def wait(name, u, n=1, per=1):
                    pe.wait_ge(sig[name].sem, sig[name].at(turn, u * per + n))

                def expert_input(u):
                    slot, b = unit_of(u)
                    if b == 0:
                        pe.wait_ge(w_loaded[slot].sem, w_loaded[slot].at(turn, 16))
                    if u == 0 or u >= 3:
                        wait("y_added", max(u - 3, 0), int(u > 0))
                    for k in range(KD):
                        last = nc.tensor.matmul(c.bank[:, XB + k, :], cols(slot, "mu", E_ALL, k * P, P),
                                                softT[:, b * T:(b + 1) * T], start=True, stop=True)
                    last.then_inc(sig["xe_filled"].sem, 1)

                def low_rank_in(u):
                    slot, b = unit_of(u)
                    wait("xe_ready", u)
                    if u >= 2:
                        wait("aw2_ready", u - 2)
                    for t in range(NT):
                        for k in range(KD):
                            last = nc.tensor.matmul(c.bank[:, AB, t * P:(t + 1) * P], xeT[:, u % 2, k, t * P:(t + 1) * P],
                                                    cols(slot, "w1", P, k * (UP + 2 * KR) + UP, 2 * KR),
                                                    start=(k == 0), stop=(k == KD - 1))
                    last.then_inc(sig["a_filled"].sem, 1)

                def transpose_in(u):
                    wait("aw_ready", u)
                    if u >= 2:
                        wait("tailT_ready", u - 2)
                    for t in range(NT):
                        last = nc.tensor.transpose(c.bank[:, TB, t * P:(t + 1) * P], aw[:, t, :], c.ident[:, :])
                    last.then_inc(sig["aT_filled"].sem, 1)

                def gate_up(u, t):
                    slot, b = unit_of(u)
                    if t == 0:
                        if routed:
                            if b == 0:
                                pe.wait_ge(scaled.sem, scaled.at(turn, slot + 1))
                            wait("aT_ready", u)
                        elif b == 0:
                            pe.wait_ge(w_loaded[slot].sem, w_loaded[slot].at(turn, 16))
                    if u * NT + t >= 2:
                        wait("h_ready", u * NT + t - 2)
                    out = c.bank[:, GB + t % 2, 0:UP]
                    for k in range(KD):
                        x = xeT[:, u % 2, k, t * P:(t + 1) * P] if routed else xT[:, k, b * T + t * P:b * T + (t + 1) * P]
                        last = nc.tensor.matmul(out, x, cols(slot, "w1", P, k * (UP + 2 * KR), UP),
                                                start=(k == 0), stop=(not routed and k == KD - 1))
                    if routed:
                        last = nc.tensor.matmul(out, awT[:, u % 2, t * P:(t + 1) * P], cols(slot, "qb"),
                                                start=False, stop=True)
                    last.then_inc(sig["gu_filled"].sem, 1)

                def transpose_h(u):
                    for t in range(NT):
                        wait("h_ready", u, t + 1, NT)
                        h = inner[:, u % 2, t, KR:KR + I]
                        nc.tensor.transpose(c.bank[:, HB, t * P:(t + 1) * P], h[:, TAIL:I], c.ident[:, :])
                        last = nc.tensor.transpose(c.bank[0:TAIL, HB + 1, t * P:(t + 1) * P], h[:, 0:TAIL], c.ident[:, :])
                    last.then_inc(sig["hT_filled"].sem, 1)

                def low_rank_down(u):
                    slot, b = unit_of(u)
                    wait("hT_ready", u)
                    for t in range(NT):
                        out = c.bank[:, AB, t * KR:(t + 1) * KR]
                        nc.tensor.matmul(out, hT[:, u % 2, t * P:(t + 1) * P], cols(slot, "down", P, D, KR),
                                         start=True, stop=False)
                        last = nc.tensor.matmul(out, hT_tail[:, u % 2, t * P:(t + 1) * P], cols(slot, "qa_tail", TAIL),
                                                start=False, stop=True)
                    last.then_inc(sig["a2_filled"].sem, 1)

                def transpose_tail(u):
                    wait("aw2_ready", u)
                    for t in range(NT):
                        last = nc.tensor.transpose(c.bank[0:KR + TAIL, TB, t * P:(t + 1) * P],
                                                   inner[:, u % 2, t, 0:KR + TAIL], c.ident[:, :])
                    last.then_inc(sig["tailT_filled"].sem, 1)

                def output(u):
                    slot, b = unit_of(u)
                    wait("tailT_ready" if routed else "hT_ready", u)
                    if not routed or u >= units - 2:
                        wait("y_added", u, 0)
                    for t in range(NT):
                        out = c.bank[:, XB + t // 2, (t % 2) * D:(t % 2 + 1) * D]
                        nc.tensor.matmul(out, hT[:, u % 2, t * P:(t + 1) * P], cols(slot, "down", P, 0, D),
                                         start=True, stop=False)
                        if routed:
                            last = nc.tensor.matmul(out, tailT[:, u % 2, t * P:(t + 1) * P],
                                                    cols(slot, "low", KR + TAIL), start=False, stop=True)
                        else:
                            last = nc.tensor.matmul(out, hT_tail[:, u % 2, t * P:(t + 1) * P],
                                                    cols(slot, "low", TAIL), start=False, stop=True)
                    last.then_inc(sig["y_filled"].sem, 1)

                if routed:
                    expert_input(0)
                    low_rank_in(0)
                    transpose_in(0)
                for u in range(units + 1):
                    if u < units:
                        gate_up(u, 0)
                        if routed and u + 1 < units:
                            expert_input(u + 1)
                    if routed and u:
                        low_rank_down(u - 1)
                    if u < units:
                        gate_up(u, 1)
                        if routed and u + 1 < units:
                            low_rank_in(u + 1)
                    if routed and u:
                        transpose_tail(u - 1)
                    if u < units:
                        gate_up(u, 2)
                        if routed and u + 1 < units:
                            transpose_in(u + 1)
                        gate_up(u, 3)
                    if u:
                        output(u - 1)
                    if u < units:
                        transpose_h(u)

            pe.wait_ge(loaded["gate"].sem, loaded["gate"].at(0, 16))
            route()
            pe.wait_ge(softT_ready.sem, softT_ready.at(0, B))
            with pe.Fori(0, turns - 1) as turn:
                experts(turn, True)
            experts(turns - 1, False)

        @block.scalar
        def _(act):
            for b in range(B):
                for k in range(KD):
                    act.wait_ge(xT_filled.sem, xT_filled.at(0, b * KD + k + 1))
                    nc.scalar.copy(xT[:, k, b * T:(b + 1) * T], c.bank[:, 4 * (b % 2) + k, :]).then_inc(xT_ready.sem, 1)
            act.wait_ge(arg_ready.sem, arg_ready.at(0, 1))
            nc.scalar.activation(score[:, :, 0:E_ALL], score[:, :, 0:E_ALL], ACT.Exp).then_inc(exp_done.sem, 1)
            for b in range(B):
                act.wait_ge(denseT_filled.sem, denseT_filled.at(0, b + 1))
                nc.scalar.copy(denseT[:, b * T:(b + 1) * T], c.bank[0:E_ALL, 4 + b, :]).then_inc(denseT_ready.sem, 1)
            act.wait_ge(arg_ready.sem, arg_ready.at(0, 2))
            nc.scalar.activation(dense[:, :, :], dense[:, :, :], ACT.Exp).then_inc(exp_done.sem, 1)
            for b in range(B):
                act.wait_ge(softT_filled.sem, softT_filled.at(0, b + 1))
                nc.scalar.copy(softT[:, b * T:(b + 1) * T], c.bank[0:E_ALL, 4 + b, :]).then_inc(softT_ready.sem, 1)

            def experts(turn, routed):
                def wait(name, u, n=1, per=1):
                    act.wait_ge(sig[name].sem, sig[name].at(turn, u * per + n))

                def apply_silu(u, t):
                    wait("gu_filled", u, t + 1, NT)
                    nc.scalar.activation(silu[:, t, :], c.bank[:, GB + t % 2, 0:I], ACT.Silu).then_inc(sig["silu_done"].sem, 1)

                for u in range(-1, units + 1):
                    if 0 <= u < units:
                        apply_silu(u, 0)
                        apply_silu(u, 1)
                    if routed and u >= 1:
                        wait("tailT_filled", u - 1)
                        nc.scalar.copy(tailT[:, (u - 1) % 2, :], c.bank[0:KR + TAIL, TB, :]).then_inc(sig["tailT_ready"].sem, 1)
                    if 0 <= u < units:
                        apply_silu(u, 2)
                    if routed and u + 1 < units:
                        wait("aT_filled", u + 1)
                        nc.scalar.copy(awT[:, (u + 1) % 2, :], c.bank[:, TB, :]).then_inc(sig["aT_ready"].sem, 1)
                    if 0 <= u < units:
                        apply_silu(u, 3)
                        wait("hT_filled", u)
                        nc.scalar.copy(hT[:, u % 2, :], c.bank[:, HB, :])
                        nc.scalar.copy(hT_tail[:, u % 2, :], c.bank[0:TAIL, HB + 1, :]).then_inc(sig["hT_ready"].sem, 1)

            with act.Fori(0, turns - 1) as turn:
                experts(turn, True)
            experts(turns - 1, False)

        @block.vector
        def _(dve):
            link = lambda ins: chain.link(dve, ins)
            wide = lambda a, n: a.rearrange("p (u a) -> p u a", a=1).broadcast_to([a.shape[0], a.shape[1], n])

            def route():
                logits = c.bank[:, 2:4, :].rearrange("p a (t e) -> p (a t) e", e=E_ALL)
                scores = score[:, :, 0:E_ALL]
                dve.wait_ge(logits_filled.sem, logits_filled.at(0, B))
                link(nc.vector.tensor_reduce(row[:, 0:tiles], logits, axis=AX.X, op=ALU.max))
                nc.vector.tensor_tensor(scores, logits, wide(row[:, 0:tiles], E_ALL), ALU.subtract).then_inc(arg_ready.sem, 1)
                dve.wait_ge(exp_done.sem, exp_done.at(0, 1))
                link(nc.vector.tensor_reduce(row[:, 0:tiles], scores, axis=AX.X, op=ALU.add))
                link(nc.vector.reciprocal(row2[:, 0:tiles], row[:, 0:tiles]))
                link(nc.vector.tensor_tensor(scores, scores, wide(row2[:, 0:tiles], E_ALL), ALU.mult))
                nc.vector.memset(c.wait_mark[:, :], 0.0)
                for t in range(tiles):
                    last = nc.vector.max(top8[:, t, :], score[:, t, 0:E_ALL])
                link(last)
                nc.vector.memset(top8[:, :, 6:7], -1.0)
                link(nc.vector.memset(top8[:, :, 7:8], -2.0))
                nc.vector.memset(c.wait_mark[:, :], 0.0)
                for t in range(tiles):
                    last = nc.vector.match_replace(rest[:, t, :], top8[:, t, :], score[:, t, :], 0.0)
                link(last)
                nc.vector.tensor_tensor(dense[:, :, :], scores, rest[:, :, 0:E_ALL], ALU.subtract).then_inc(dense_ready.sem, 1)
                dve.wait_ge(flat_filled.sem, flat_filled.at(0, 1))
                flat = c.bank[:, 2:4, :].rearrange("p a n -> p (a n)")
                by_expert = lambda a: a.rearrange("p (u k) -> p u k", k=K)
                all_dense = dense[:, :, :].rearrange("p t e -> p (t e)")
                link(nc.vector.tensor_scalar(all_dense, flat, 0.0, -1e9, ALU.is_equal, ALU.mult))
                link(nc.vector.tensor_tensor(all_dense, all_dense, flat, ALU.add))
                nc.vector.tensor_reduce(share[:, :, :].rearrange("p t f -> p (t f)"), by_expert(flat), axis=AX.X, op=ALU.add)
                link(nc.vector.tensor_reduce(row2[:, :], by_expert(all_dense), axis=AX.X, op=ALU.max))
                nc.vector.tensor_tensor(by_expert(all_dense), by_expert(all_dense), wide(row2[:, :], K),
                                        ALU.subtract).then_inc(arg_ready.sem, 1)
                dve.wait_ge(exp_done.sem, exp_done.at(0, 2))
                link(nc.vector.tensor_reduce(row[:, :], by_expert(all_dense), axis=AX.X, op=ALU.add))
                link(nc.vector.reciprocal(row2[:, :], row[:, :]))
                nc.vector.tensor_tensor(by_expert(soft[:, :, :].rearrange("p t e -> p (t e)")), by_expert(all_dense),
                                        wide(row2[:, :], K), ALU.mult).then_inc(soft_ready.sem, 1)
                dve.wait_ge(soft_ready.sem, soft_ready.at(0, 1))
                nc.vector.memset(c.wait_mark[:, :], 0.0)

            def experts(turn, routed):
                def wait(name, u, n=1, per=1):
                    dve.wait_ge(sig[name].sem, sig[name].at(turn, u * per + n))

                def scale_weights(slot):
                    dve.wait_ge(w_loaded[slot].sem, w_loaded[slot].at(turn, 16))
                    nc.vector.tensor_tensor(cols(slot, "qb"), cols(slot, "qb"), cols(slot, "qb_scale"), ALU.mult)
                    nc.vector.tensor_tensor(cols(slot, "low", KR), cols(slot, "low", KR), cols(slot, "low_scale", KR),
                                            ALU.mult).then_inc(scaled.sem, 1)

                def routing(u):
                    slot, b = unit_of(u)
                    at = turn * (2 * K) + slot * K
                    return soft[:, b * NT:(b + 1) * NT, bass.ds(at, K)].rearrange("p t (k a) -> p t k a", a=1)

                def add_input(u):
                    slot, b = unit_of(u)
                    wait("xe_filled", u)
                    for k in range(KD):
                        last = nc.vector.tensor_tensor(xeT[:, u % 2, k, :], c.bank[:, XB + k, :],
                                                       xT[:, k, b * T:(b + 1) * T], ALU.add)
                    last.then_inc(sig["xe_ready"].sem, 1)

                def weigh(u):
                    wait("a_filled", u)
                    nc.vector.tensor_tensor(aw[:, :, :].rearrange("p t (k r) -> p t k r", k=K),
                                            c.bank[:, AB, :].rearrange("p (t k r) -> p t k r", t=NT, k=K),
                                            routing(u).broadcast_to([P, NT, K, 2 * R]), ALU.mult).then_inc(sig["aw_ready"].sem, 1)

                def weigh_down(u):
                    wait("a2_filled", u)
                    nc.vector.tensor_tensor(inner[:, u % 2, :, 0:KR].rearrange("p t (k r) -> p t k r", k=K),
                                            c.bank[:, AB, 0:NT * KR].rearrange("p (t k r) -> p t k r", t=NT, k=K),
                                            routing(u).broadcast_to([P, NT, K, R]), ALU.mult).then_inc(sig["aw2_ready"].sem, 1)

                def multiply(u, t):
                    slot, b = unit_of(u)
                    wait("silu_done", u, t + 1, NT)
                    h, up = inner[:, u % 2, t, KR:KR + I], c.bank[:, GB + t % 2, I:UP]
                    if routed:
                        by = share[:, b * NT + t, bass.ds(turn * 2 + slot, 1)]
                        ins = nc.vector.scalar_tensor_tensor(h, up, by, silu[:, t, :], ALU.mult, ALU.mult)
                    else:
                        ins = nc.vector.tensor_tensor(h, up, silu[:, t, :], ALU.mult)
                    ins.then_inc(sig["h_ready"].sem, 1)

                def add_output(u):
                    slot, b = unit_of(u)
                    wait("y_filled", u)
                    for half in range(2):
                        xs = c.x[:, b * TURN + half * 512:b * TURN + (half + 1) * 512]
                        last = nc.vector.tensor_tensor(xs, xs, c.bank[:, XB + half, :], ALU.add)
                    last.then_inc(sig["y_added"].sem, 1)

                if routed:
                    scale_weights(0)
                    add_input(0)
                    weigh(0)
                for u in range(units + 1):
                    if u < units:
                        multiply(u, 0)
                        if routed and u + 1 < units:
                            add_input(u + 1)
                    if routed and u:
                        weigh_down(u - 1)
                    if u < units:
                        multiply(u, 1)
                        if routed and u + 1 < units:
                            weigh(u + 1)
                        multiply(u, 2)
                        multiply(u, 3)
                        if routed and u == 2:
                            scale_weights(1)
                    if u:
                        add_output(u - 1)

            dve.sem_inc(sig["y_added"].sem, 1)
            for b in range(B):
                norm.moments(dve, b)
            for b in range(B):
                norm.rows(dve, b)
            nc.vector.memset(score[:, :, E_ALL:E_ALL + 1], -1.0)
            link(nc.vector.memset(score[:, :, E_ALL + 1:E_ALL + 2], -2.0))
            dve.wait_ge(index_ready.sem, index_ready.at(0, 1))
            nc.vector.tensor_copy(index_f[:, :], index[:, :])
            dve.wait_ge(loaded["map"].sem, loaded["map"].at(0, 16))
            link(nc.vector.tensor_copy(entry[:, :], mapping[:, :]))
            link(nc.vector.tensor_scalar(negative[:, :], entry[:, :], 0.0, float(E_ALL), ALU.is_lt, ALU.mult))
            link(nc.vector.tensor_tensor(entry[:, :], entry[:, :], negative[:, :], ALU.add))
            link(nc.vector.tensor_scalar(entry[:, :], entry[:, :], 0.0, float(E_ALL - 1), ALU.max, ALU.min))
            nc.vector.tensor_scalar(pick[:, :], entry[:, :], index_f[:, :], None, ALU.is_equal).then_inc(pick_ready.sem, 1)
            route()
            with dve.Fori(0, turns - 1) as turn:
                experts(turn, True)
            experts(turns - 1, False)
    norm.end()
    chain.finish()
    for s in (*loaded.values(), index_ready, pick_ready, xT_filled, xT_ready, logits_filled, arg_ready, exp_done, dense_ready, soft_ready, denseT_filled,
              denseT_ready, flat_filled, softT_filled, softT_ready):
        s.end(1)
    for s in w_loaded:
        s.end(turns)
    routed_only = ("xe_filled", "xe_ready", "a_filled", "aw_ready", "aT_filled", "aT_ready", "a2_filled",
                   "aw2_ready", "tailT_filled", "tailT_ready")
    scaled.end(turns - 1)
    for n, s in sig.items():
        s.end(turns - (n in routed_only))


def build_store(c, out_dram):
    stored = c.counter("stored", 16)
    with c.nc.Block() as block:
        @block.sync
        def _(sp):
            sp.dma_start(out_dram.rearrange("b (t p) d -> p b t d", p=P),
                         c.x[:, 0:B * TURN].rearrange("p (b t d) -> p b t d", b=B, t=NT)).then_inc(stored.sem, 16)
            sp.wait_ge(stored.sem, stored.at(0, 16))


def build_program(nc, ins, out, stages):
    with ExitStack() as ctx:
        c = Chip(ctx, nc)
        build_constants(c, ins["x"])
        for stage in stages:
            if stage == "big":
                build_big_attention(c, ins["big_w"], ins["big_wo"], ins["big_bo"])
            elif stage == "ffn":
                build_ffn(c, ins["ffn_w"], ins["ffn_bias"], ins["ffn_affine"])
            elif stage == "moe":
                build_moe(c, ins)
            else:
                build_small_attention(c, stage, ins)
        build_store(c, out)


STAGES = ("big", "ffn", "differential", "ffn", "splat", "moe", "rope", "moe")



def rows(w):
    return w.reshape(-1, P, w.shape[-1]).transpose(1, 0, 2)


def put(pack, name, v, row=0, col=0):
    at = AT[name][0] + col
    pack[row:row + v.shape[0], at:at + v.shape[1]] = v


def lay_out(a):
    g = {}
    g["x"] = a["L0_attn_a_query"]
    big = [a[f"L0_attn_a_w_{n}"].reshape(D, H0, DH0).transpose(1, 0, 2) for n in "qkv"]
    big = np.concatenate(big, axis=2).reshape(H0, KD, P, QKV0).transpose(0, 2, 1, 3).reshape(H0, P, KD * QKV0)
    bq, bk, bv = (a[f"L0_attn_a_b_{n}"].reshape(H0, DH0) for n in "qkv")
    g["big_w"] = np.concatenate([big, bq[:, :, None], bk[:, :, None],
                                 np.broadcast_to(bv[:, None, :], (H0, P, DH0))], axis=2)
    g["big_wo"] = a["L0_attn_a_w_o"].reshape(H0, DH0, D)
    g["big_bo"] = np.tile(a["L0_attn_a_b_o"][None, :], (1, 2))
    g["ffn_w"] = rows(a["L0_ffn_weight"].T)
    g["ffn_bias"] = np.tile(a["L0_ffn_bias"][None, :], (1, 2))
    g["ffn_affine"] = np.broadcast_to(np.stack([a["L0_ffn_ln_gamma"], a["L0_ffn_ln_beta"]])[None], (P, 2, D))
    spread = lambda v: np.broadcast_to(v, (P, *v.shape))
    d = {n: a[f"L0_attn_b_{n}"] for n in ("Wq", "Wk", "Wv", "Wo", "bq", "bk", "bv", "bo", "lq1", "lk1", "lq2", "lk2", "g_subln")}
    for n in "qkvo":
        g[f"differential_w{n}"] = rows(d[f"W{n}"])
        g[f"splat_w{n}"] = rows(a[f"L1_attn_a_W{n}"].T)
        g[f"rope_w{n}"] = rows(a[f"L1_attn_b_W{n}"].T)
    for n in "qkv":
        g[f"differential_b{n}"] = spread(d[f"b{n}"])
    g["differential_bo"] = np.tile(d["bo"][None, :], (1, 2))
    g["differential_lam"] = spread(np.stack([d["lq1"], d["lk1"], d["lq2"], d["lk2"]]))
    g["differential_gsub"] = spread(d["g_subln"])
    pos, direction = a["L1_attn_a_splat_positions"], a["L1_attn_a_splat_directions"]
    g["splat_pos"] = spread(pos.reshape(-1))
    g["splat_dir"] = spread(direction.reshape(-1))
    g["splat_logs"] = spread(np.stack([a["L1_attn_a_splat_log_scales"].reshape(-1),
                                       a["L1_attn_a_splat_log_amplitudes"].reshape(-1)]))
    g["splat_scal"] = spread(np.stack([a["L1_attn_a_directional_strength"], a["L1_attn_a_position_sensitivity"],
                                       a["L1_attn_a_gsa_strength"]]))
    for n in "qk":
        g[f"splat_w{n}_out"] = rows(a[f"L1_attn_a_W{n}"])
    blocks = np.zeros((KD, H1 // KD, DH1, H1 // KD, 16), np.float32)
    for h in range(H1):
        half, at = h // (H1 // KD), h % (H1 // KD)
        blocks[half, at, :, at, 0:8] = pos[h].T
        blocks[half, at, :, at, 8:16] = direction[h].T
    g["splat_blocks"] = blocks.reshape(KD, P, P).transpose(1, 0, 2)
    inv_freq = np.float32(10000.0) ** (-np.arange(0, DH1, 2, dtype=np.float32) / np.float32(DH1))
    angles = (np.arange(T, dtype=np.float32)[:, None] * inv_freq[None, :]).astype(np.float32)
    for n, f in (("cos", np.cos), ("sin", np.sin)):
        table = f(angles).astype(np.float32).reshape(NT, P, DH1 // 2).transpose(1, 0, 2)
        g[f"rope_{n}"] = np.stack([table * np.float32(0.25), table], axis=1)
    m = {n[len("L1_ffn_"):]: v for n, v in a.items() if n.startswith("L1_ffn_")}
    g["moe_gate"] = rows(m["gate_weight"].T)
    g["moe_map"] = np.broadcast_to(m["inv_mapping"].reshape(1, -1), (E_ALL, E_ALL))
    packs = np.zeros((F + 2, P, PACK_E), np.float32)
    for f in range(F):
        qa = np.concatenate([m["gate_qa"][f], m["up_qa"][f]], axis=1).reshape(2 * KR, D)
        w1 = np.concatenate([m["gate_W"][f].T, m["up_W"][f].T, qa.T], axis=1)
        put(packs[f], "w1", rows(w1).reshape(P, -1))
        qb = np.zeros((K, 2, R, 2, I), np.float32)
        qb[:, 0, :, 0, :] = m["gate_qb"][f].transpose(0, 2, 1)
        qb[:, 1, :, 1, :] = m["up_qb"][f].transpose(0, 2, 1)
        put(packs[f], "qb", qb.reshape(P, UP))
        put(packs[f], "qb_scale", np.broadcast_to(np.concatenate([m["gate_scale"][f], m["up_scale"][f]]), (P, UP)))
        put(packs[f], "mu", m["mask_up_W"][f].T, row=f * K)
        down, down_qa = m["down_W"][f].T, m["down_qa"][f].reshape(KR, I).T
        put(packs[f], "down", down[TAIL:])
        put(packs[f], "down", down_qa[TAIL:], col=D)
        put(packs[f], "qa_tail", down_qa[:TAIL])
        put(packs[f], "low", m["down_qb"][f].transpose(0, 2, 1).reshape(KR, D))
        put(packs[f], "low", down[:TAIL], row=KR)
        put(packs[f], "low_scale", np.broadcast_to(m["down_scale"][f], (KR, D)))
    for i in range(2):
        f, part = F + i, slice(i * I, (i + 1) * I)
        w1 = np.concatenate([m["sh_gate_W"][part].T, m["sh_up_W"][part].T, np.zeros((D, 2 * KR), np.float32)], axis=1)
        put(packs[f], "w1", rows(w1).reshape(P, -1))
        put(packs[f], "down", m["sh_down_W"].T[part][TAIL:])
        put(packs[f], "low", m["sh_down_W"].T[part][:TAIL])
    g["moe_w"] = packs
    return {k: np.ascontiguousarray(v) for k, v in g.items()}


def kernel(**inputs):
    import concourse.bacc as bacc
    from concourse.bass_utils import run_bass_kernel_spmd

    arrays = lay_out({k: np.asarray(v) for k, v in inputs.items()})
    nc = bacc.Bacc("TRN2", target_bir_lowering=False, num_devices=1)
    ins = {k: nc.dram_tensor(f"in_{k}", v.shape, mybir.dt.from_np(v.dtype), kind="ExternalInput").ap()
           for k, v in arrays.items()}
    out = nc.dram_tensor("out", (B, T, D), F32, kind="ExternalOutput").ap()
    build_program(nc, ins, out, STAGES)
    result = run_bass_kernel_spmd(nc, [{f"in_{k}": v for k, v in arrays.items()}], core_ids=[0])
    return result.results[0]["out"]
```
